# Optimizing a Trainium2 kernel written in Bass

```python
import numpy as np
import jax
import jax.numpy as jnp

def _softmax(x, axis=-1):
    return jax.nn.softmax(x, axis=axis)

def _gelu(x):
    return jax.nn.gelu(x, approximate=True)

def _silu(x):
    return jax.nn.silu(x)

def _sigmoid(x):
    return jax.nn.sigmoid(x)

def _layernorm(x, axis=-1, eps=1e-05):
    m = jnp.mean(x, axis=axis, keepdims=True)
    v = jnp.var(x, axis=axis, keepdims=True)
    return (x - m) / jnp.sqrt(v + eps)

def _scatter_add(tgt, idx, src, axis=0):
    return tgt.at[idx].add(src)

def _segment_sum(src, seg, n):
    return jax.ops.segment_sum(src, seg, n)
kernel_name = 'mk_flamingo_gated_d2_seqx_r8_7759f5'

def setup_inputs(seed: int=0):
    np.random.seed(seed)
    _w = jnp.asarray

    def _rec_inputs():
        import jax
        import jax.numpy as jnp
        _rk = jax.random.key(seed)
        x = -0.0002928 + 1 * jax.random.normal(jax.random.fold_in(_rk, 1), (16, 128, 128), jnp.float32)
        _lenS = 128 - jax.random.randint(jax.random.fold_in(_rk, 7), (16,), 0, max(1, 128 // 4) + 1, jnp.int32)
        _lenS2 = 128 - jax.random.randint(jax.random.fold_in(_rk, 8), (16,), 0, max(1, 128 // 4) + 1, jnp.int32)
        _ctx_1024P = jax.random.normal(jax.random.fold_in(_rk, 11), (16, 16, 128), jnp.float32)
        _ctx_1024c = jax.random.dirichlet(jax.random.fold_in(_rk, 511), 0.3 * jnp.ones((16,), jnp.float32), (16, 128))
        _ctx_1024t = jnp.einsum('bsk,bkd->bsd', _ctx_1024c, _ctx_1024P)
        _ctx_1024t = _ctx_1024t * jax.lax.rsqrt(jnp.mean(jnp.square(_ctx_1024t)) + 1e-12) * 0.953939
        ctx_1024 = -1.39393e-06 + 0.999914 * (_ctx_1024t + 0.3 * jax.random.normal(jax.random.fold_in(_rk, 611), (16, 128, 128), jnp.float32))
        fside_SxS2_0 = 0.000675642 + 1.00031 * jax.random.normal(jax.random.fold_in(_rk, 12), (128, 128), jnp.float32)
        _validS = jnp.arange(128)[None, :] < _lenS[:, None]
        _validS2 = jnp.arange(128)[None, :] < _lenS2[:, None]
        _causal = jnp.tril(jnp.ones((128, 128), dtype=bool))
        mask_BxS2_if0 = jnp.where(jnp.ones((16, 128), dtype=bool), 0, 1).astype(jnp.int32)
        _g = jax.random.normal(jax.random.fold_in(_rk, 9001), (2, 2), jnp.float32)
        _g = jnp.sign(_g) * jnp.maximum(jnp.abs(_g), 1.0) + (_g == 0) * 1.0
        g_xattn = _g[0]
        g_ffn = _g[1]
        return (x, ctx_1024, fside_SxS2_0, mask_BxS2_if0, g_xattn, g_ffn)
    x, ctx_1024, fside_SxS2_0, mask_BxS2_if0, g_xattn, g_ffn = _rec_inputs()

    def _L0_xattn_setup():
        import jax, jax.numpy as jnp
        import numpy as np
        D_MODEL = 128
        N_HEADS = 16
        HEAD_DIM = D_MODEL // N_HEADS
        key = jax.random.key(seed)
        ks = jax.random.split(key, 11)
        B, S, D = (2, 256, D_MODEL)
        scale = 1.0 / np.sqrt(D)
        return {'q': jax.random.normal(ks[0], (B, S, D), jnp.float32), 'k': jax.random.normal(ks[1], (B, S, D), jnp.float32), 'v': jax.random.normal(ks[2], (B, S, D), jnp.float32), 'Wq': jax.random.normal(ks[3], (D, D), jnp.float32) * scale, 'bq': jnp.zeros((D,), jnp.float32), 'Wk': jax.random.normal(ks[4], (D, D), jnp.float32) * scale, 'bk': jnp.zeros((D,), jnp.float32), 'Wv': jax.random.normal(ks[5], (D, D), jnp.float32) * scale, 'bv': jnp.zeros((D,), jnp.float32), 'Wo': jax.random.normal(ks[6], (D, D), jnp.float32) * scale, 'bo': jnp.zeros((D,), jnp.float32)}
    _L0_xattn_all = _L0_xattn_setup()
    _L0_xattn_in = {k: v for k, v in _L0_xattn_all.items() if k in ('Wq', 'bq', 'Wk', 'bk', 'Wv', 'bv', 'Wo', 'bo')}
    del _L0_xattn_all

    def _L0_ffn_setup():
        import jax, jax.numpy as jnp
        import numpy as np
        TOP_K = 2
        key = jax.random.key(seed)
        k1, k2, k3, k4 = jax.random.split(key, 4)
        B, T, D, H, E = (2, 256, 128, 256, 8)
        x = jax.random.normal(k1, (B, T, D), dtype=jnp.float32)
        w12 = jax.random.normal(k2, (E, 2 * H, D), dtype=jnp.float32) * D ** (-0.5)
        w3 = jax.random.normal(k3, (E, D, H), dtype=jnp.float32) * H ** (-0.5)
        gate_w = jax.random.normal(k4, (E, D), dtype=jnp.float32) * D ** (-0.5)
        return {'x': x, 'w12': w12, 'w3': w3, 'gate_w': gate_w}
    _L0_ffn_all = _L0_ffn_setup()
    _L0_ffn_in = {k: v for k, v in _L0_ffn_all.items() if k in ('w12', 'w3', 'gate_w')}
    del _L0_ffn_all

    def _L1_xattn_setup():
        import jax, jax.numpy as jnp
        import numpy as np
        D_MODEL = 128
        NHEAD = 16
        DK = D_MODEL // NHEAD
        B, S = (2, 256)
        key = jax.random.key(seed)
        ks = jax.random.split(key, 8)
        Q = jax.random.normal(ks[0], (B, S, D_MODEL), dtype=jnp.float32)
        K = jax.random.normal(ks[1], (B, S, D_MODEL), dtype=jnp.float32)
        V = jax.random.normal(ks[2], (B, S, D_MODEL), dtype=jnp.float32)
        additive_mask = jax.random.normal(ks[3], (S, S), dtype=jnp.float32)
        key_padding_mask = jnp.zeros((B, S), dtype=jnp.int32)
        scale = 1.0 / np.sqrt(D_MODEL)
        WQ = jax.random.normal(ks[4], (NHEAD, D_MODEL, DK), dtype=jnp.float32) * scale
        WK = jax.random.normal(ks[5], (NHEAD, D_MODEL, DK), dtype=jnp.float32) * scale
        WV = jax.random.normal(ks[6], (NHEAD, D_MODEL, DK), dtype=jnp.float32) * scale
        WO = jax.random.normal(ks[7], (D_MODEL, D_MODEL), dtype=jnp.float32) * scale
        return {'Q': Q, 'K': K, 'V': V, 'additive_mask': additive_mask, 'key_padding_mask': key_padding_mask, 'WQ': WQ, 'WK': WK, 'WV': WV, 'WO': WO}
    _L1_xattn_all = _L1_xattn_setup()
    _L1_xattn_in = {k: v for k, v in _L1_xattn_all.items() if k in ('WQ', 'WK', 'WV', 'WO')}
    del _L1_xattn_all

    def _L1_ffn_setup():
        import jax, jax.numpy as jnp
        import numpy as np
        HIDDEN = 128
        INNER = 512

        def _weight_quant(w):
            scale = 1.0 / jnp.clip(jnp.mean(jnp.abs(w)), 1e-05)
            wq = jnp.clip(jnp.round(w * scale), -1.0, 1.0) / scale
            return w + jax.lax.stop_gradient(wq - w)

        def _act_quant(x):
            scale = 127.0 / jnp.clip(jnp.max(jnp.abs(x), axis=-1, keepdims=True), 1e-05)
            xq = jnp.clip(jnp.round(x * scale), -128.0, 127.0) / scale
            return x + jax.lax.stop_gradient(xq - x)

        def _bitlinear(x, w):
            return jnp.einsum('bsi,oi->bso', _act_quant(x), _weight_quant(w))
        key = jax.random.key(seed)
        k0, k1, k2, k3 = jax.random.split(key, 4)
        x = jax.random.normal(k0, (4, 256, HIDDEN), dtype=jnp.float32)
        w_gate = jax.random.normal(k1, (INNER, HIDDEN), dtype=jnp.float32) / np.sqrt(HIDDEN)
        w_up = jax.random.normal(k2, (INNER, HIDDEN), dtype=jnp.float32) / np.sqrt(HIDDEN)
        w_down = jax.random.normal(k3, (HIDDEN, INNER), dtype=jnp.float32) / np.sqrt(INNER)
        return {'x': x, 'w_gate': w_gate, 'w_up': w_up, 'w_down': w_down}
    _L1_ffn_all = _L1_ffn_setup()
    _L1_ffn_in = {k: v for k, v in _L1_ffn_all.items() if k in ('w_gate', 'w_up', 'w_down')}
    del _L1_ffn_all
    return {'x': x, 'ctx_1024': ctx_1024, 'fside_SxS2_0': fside_SxS2_0, 'mask_BxS2_if0': mask_BxS2_if0, 'g_xattn': g_xattn, 'g_ffn': g_ffn, 'L0_xattn_Wq': _L0_xattn_in['Wq'], 'L0_xattn_bq': _L0_xattn_in['bq'], 'L0_xattn_Wk': _L0_xattn_in['Wk'], 'L0_xattn_bk': _L0_xattn_in['bk'], 'L0_xattn_Wv': _L0_xattn_in['Wv'], 'L0_xattn_bv': _L0_xattn_in['bv'], 'L0_xattn_Wo': _L0_xattn_in['Wo'], 'L0_xattn_bo': _L0_xattn_in['bo'], 'L0_ffn_w12': _L0_ffn_in['w12'], 'L0_ffn_w3': _L0_ffn_in['w3'], 'L0_ffn_gate_w': _L0_ffn_in['gate_w'], 'L1_xattn_WQ': _L1_xattn_in['WQ'], 'L1_xattn_WK': _L1_xattn_in['WK'], 'L1_xattn_WV': _L1_xattn_in['WV'], 'L1_xattn_WO': _L1_xattn_in['WO'], 'L1_ffn_w_gate': _L1_ffn_in['w_gate'], 'L1_ffn_w_up': _L1_ffn_in['w_up'], 'L1_ffn_w_down': _L1_ffn_in['w_down']}

def reference(x, ctx_1024, fside_SxS2_0, mask_BxS2_if0, g_xattn, g_ffn, L0_xattn_Wq, L0_xattn_bq, L0_xattn_Wk, L0_xattn_bk, L0_xattn_Wv, L0_xattn_bv, L0_xattn_Wo, L0_xattn_bo, L0_ffn_w12, L0_ffn_w3, L0_ffn_gate_w, L1_xattn_WQ, L1_xattn_WK, L1_xattn_WV, L1_xattn_WO, L1_ffn_w_gate, L1_ffn_w_up, L1_ffn_w_down):
    import jax
    import jax.numpy as jnp

    def _L0_xattn_ref(q, k, v, Wq, bq, Wk, bk, Wv, bv, Wo, bo):
        import jax, jax.numpy as jnp
        import numpy as np
        D_MODEL = 128
        N_HEADS = 16
        HEAD_DIM = D_MODEL // N_HEADS
        B, S, D = q.shape
        H, Hd = (N_HEADS, HEAD_DIM)

        def split_heads(x):
            return x.reshape(B, S, H, Hd).transpose(0, 2, 1, 3)
        qh = split_heads(q @ Wq + bq)
        kh = split_heads(k @ Wk + bk)
        vh = split_heads(v @ Wv + bv)
        scores = jnp.einsum('bhqd,bhkd->bhqk', qh, kh) / jnp.sqrt(jnp.float32(Hd))
        probs = jax.nn.softmax(scores, axis=-1)
        ctx = jnp.einsum('bhqk,bhkd->bhqd', probs, vh)
        out = ctx.transpose(0, 2, 1, 3).reshape(B, S, D)
        return out @ Wo + bo

    def _L0_ffn_ref(x, w12, w3, gate_w):
        import jax, jax.numpy as jnp
        import numpy as np
        TOP_K = 2
        E = gate_w.shape[0]
        H = w3.shape[-1]
        scores = jnp.einsum('btd,ed->bte', x, gate_w)
        topk_scores, topk_idx = jax.lax.top_k(scores, TOP_K)
        topk_probs = jax.nn.softmax(topk_scores, axis=-1)
        total_probs = jnp.sum(jax.nn.one_hot(topk_idx, E, dtype=topk_probs.dtype) * topk_probs[..., None], axis=-2)
        h12 = jnp.einsum('btd,ehd->bteh', x, w12)
        h1, h2 = (h12[..., :H], h12[..., H:])
        hidden = jax.nn.silu(h1) * h2
        expert_out = jnp.einsum('bteh,edh->bted', hidden, w3)
        y = jnp.sum(total_probs[..., None] * expert_out, axis=-2)
        return y

    def _L1_xattn_ref(Q, K, V, additive_mask, key_padding_mask, WQ, WK, WV, WO):
        import jax, jax.numpy as jnp
        import numpy as np
        D_MODEL = 128
        NHEAD = 16
        DK = D_MODEL // NHEAD
        B, S = (2, 256)
        q = jnp.einsum('bsd,hdk->bhsk', Q, WQ)
        k = jnp.einsum('bsd,hdk->bhsk', K, WK)
        v = jnp.einsum('bsd,hdk->bhsk', V, WV)
        scores = jnp.einsum('bhqk,bhsk->bhqs', q, k) / np.sqrt(DK)
        scores = scores + additive_mask[None, None, :, :]
        attn = jax.nn.softmax(scores, axis=-1)
        o = jnp.einsum('bhqs,bhsk->bhqk', attn, v)
        o = o.transpose(0, 2, 1, 3).reshape(Q.shape[0], Q.shape[1], D_MODEL)
        return o @ WO

    def _L1_ffn_ref(x, w_gate, w_up, w_down):
        import jax, jax.numpy as jnp
        import numpy as np
        HIDDEN = 128
        INNER = 512

        def _weight_quant(w):
            scale = 1.0 / jnp.clip(jnp.mean(jnp.abs(w)), 1e-05)
            wq = jnp.clip(jnp.round(w * scale), -1.0, 1.0) / scale
            return w + jax.lax.stop_gradient(wq - w)

        def _act_quant(x):
            scale = 127.0 / jnp.clip(jnp.max(jnp.abs(x), axis=-1, keepdims=True), 1e-05)
            xq = jnp.clip(jnp.round(x * scale), -128.0, 127.0) / scale
            return x + jax.lax.stop_gradient(xq - x)

        def _bitlinear(x, w):
            return jnp.einsum('bsi,oi->bso', _act_quant(x), _weight_quant(w))
        gate = jax.nn.silu(_bitlinear(x, w_gate))
        up = _bitlinear(x, w_up)
        return _bitlinear(gate * up, w_down)
    x = x + jnp.tanh(g_xattn[0]) * _L0_xattn_ref(_layernorm(x, axis=-1), ctx_1024, ctx_1024, L0_xattn_Wq, L0_xattn_bq, L0_xattn_Wk, L0_xattn_bk, L0_xattn_Wv, L0_xattn_bv, L0_xattn_Wo, L0_xattn_bo)
    x = x + jnp.tanh(g_ffn[0]) * _L0_ffn_ref(_layernorm(x, axis=-1), L0_ffn_w12, L0_ffn_w3, L0_ffn_gate_w)
    x = x + jnp.tanh(g_xattn[1]) * _L1_xattn_ref(_layernorm(x, axis=-1), ctx_1024, ctx_1024, fside_SxS2_0, mask_BxS2_if0, L1_xattn_WQ, L1_xattn_WK, L1_xattn_WV, L1_xattn_WO)
    x = x + jnp.tanh(g_ffn[1]) * _L1_ffn_ref(_layernorm(x, axis=-1), L1_ffn_w_gate, L1_ffn_w_up, L1_ffn_w_down)
    return x

_drawn_inputs = setup_inputs


def setup_inputs(seed=0):
    import zlib

    import numpy as np

    out = dict(_drawn_inputs(seed))
    spreads = {'g_ffn': (-1.0, 0.2),
     'L0_xattn_bq': (0.0, 0.1),
     'L0_xattn_bk': (0.0, 0.1),
     'L0_xattn_bv': (0.0, 0.1),
     'L0_xattn_bo': (0.0, 0.1)}
    factors = {}
    for name, (base, spread) in spreads.items():
        noise = np.random.default_rng([zlib.crc32(name.encode()), seed]).standard_normal(out[name].shape)
        drawn = base * np.exp(spread * noise) if base else spread * noise
        out[name] = jnp.asarray(drawn.astype(out[name].dtype))
    for name, factor in factors.items():
        out[name] = (out[name] * factor).astype(out[name].dtype)
    return out
```

```python
import concourse.bass as bass
from concourse import mybir
from contextlib import ExitStack


def gated_cross_attention_stack(nc, t, stop_after=99):
    F32, BF16 = mybir.dt.float32, mybir.dt.bfloat16
    ALU = mybir.AluOpType
    ACT = mybir.ActivationFunctionType
    AX = mybir.AxisListType

    BATCHES, TOKENS, D = t["x"].shape
    HEADS, HD = 16, D // 16
    UNITS, UH = 2, HEADS // 2
    EXPERTS, TWO_H = t["w12T"].shape[1:]
    H_TILES = TWO_H // 2 // 128
    INNER = t["w_gateT"].shape[1]
    I_TILES = INNER // 128
    GROUP = 4
    GROUPS = BATCHES // GROUP
    SLOTS, SLOT_ROWS = 8, 64
    V_COLS = 32
    EPS = 1e-5
    MAGIC = 1.5 * 2.0 ** 23

    ctx = ExitStack()
    with ctx:
        def sb(name, shape, dt=F32):
            return ctx.enter_context(nc.sbuf_tensor(f"{name}_sb", shape, dt))

        def sem(name):
            return ctx.enter_context(nc.semaphore(name))

        def need(eng, semaphore, count):
            if not isinstance(count, int) or count > 0:
                eng.wait_ge(semaphore, count)

        x_all = sb("x_all", [128, BATCHES, D])
        eye = sb("eye_f32", [128, 128])
        eye_b = sb("eye_bf16", [128, 128], BF16)
        ones = sb("ones_f32", [128, 128])
        half = sb("minus_half", [128, 1])
        eps = sb("eps", [128, 1])
        zero = sb("zero", [128, 1])
        gains = sb("gains", [128, 4])
        tanh_g = sb("tanh_g", [128, 4])
        wq = [sb(f"wq{l}", [128, 128]) for l in range(2)]
        wkv = [sb(f"wkv{l}", [128, 256]) for l in range(2)]
        wo = [sb(f"wo{l}", [128, 128]) for l in range(2)]
        bqk = sb("bqk", [128, 256])
        bv_col = sb("bv_col", [128, 1])
        bv_rep = sb("bv_rep", [128, 128])
        bo_row = sb("bo_row", [128, 128])
        bias_out = sb("bias_out", [128, 128])
        mask = sb("mask", [128, 128])
        mask_rest = sb("mask_rest", [128, 128])
        mask_parts = sb("mask_parts", [128, 3, 128], BF16)
        sel_ind = sb("sel_ind", [128, HEADS])
        sel = sb("sel", [128, HEADS, 128], BF16)
        ctx_in = sb("ctx_in", [128, 2, D])
        stats = sb("stats", [128, 2, 6])
        mean_var = sb("mean_var", [128, 2, 2])
        var_eps = sb("var_eps", [128, 2, 1])
        rstd = sb("rstd", [128, 2, 1])
        xn = sb("xn", [128, 2, D])
        xcT = sb("xcT", [128, 2, 256])
        qk = sb("qk", [128, 2, 256])
        qk_rest = sb("qk_rest", [128, 2, 256])
        stack = sb("stack", [128, 2, 2, HEADS, SLOTS * HD], BF16)
        qT = sb("qT", [128, 2, HEADS // 2, 128], BF16)
        kT = sb("kT", [128, 2, HEADS // 2, 128], BF16)
        v_one = sb("v_one", [128, 2, HEADS, V_COLS])
        neg_max = sb("neg_max", [128, 2, HEADS])
        neg_rest = sb("neg_rest", [128, 2, HEADS])
        neg_parts = sb("neg_parts", [128, 2, 2, 4, HEADS], BF16)
        mT = sb("mT", [128, 2, 128], BF16)
        probs = sb("probs", [128, UNITS, 2, UH // 2, 128])
        o_raw = sb("o_raw", [128, 512])
        o_rden = sb("o_rden", [128, HEADS])
        o_norm = sb("o_norm", [128, 128])
        o_normT = sb("o_normT", [128, 128])

        w12 = sb("w12", [128, EXPERTS, TWO_H])
        w3 = sb("w3", [128, EXPERTS, H_TILES, D])
        gate_w = sb("gate_w", [128, EXPERTS])
        before = sb("before", [128, EXPERTS, EXPERTS])
        xnT_ring = sb("xnT_ring", [128, 2, 128])
        xnT_all = sb("xnT_all", [128, BATCHES, 128])
        scores = sb("scores", [128, BATCHES, EXPERTS])
        top = sb("top", [128, BATCHES])
        greater = sb("greater", [128, BATCHES, EXPERTS, EXPERTS])
        at_least = sb("at_least", [128, BATCHES, EXPERTS, EXPERTS])
        rank = sb("rank", [128, BATCHES, EXPERTS])
        chosen = sb("chosen", [128, BATCHES, EXPERTS])
        shifted = sb("shifted", [128, BATCHES, EXPERTS])
        weight = sb("weight", [128, BATCHES, EXPERTS])
        weight_sum = sb("weight_sum", [128, BATCHES])
        silu = sb("silu", [128, 2, GROUP * 128])
        hidden = sb("hidden", [128, 2, H_TILES, GROUP * 128])
        w_gu = sb("w_gu", [128, 2, INNER])
        w_dn = sb("w_dn", [128, I_TILES, D])
        w_abs = sb("w_abs", [128, 2 * INNER])
        w_sums = sb("w_sums", [128, 3])
        w_mean = sb("w_mean", [128, 3])
        w_scale = sb("w_scale", [128, 3])
        w_inv = sb("w_inv", [128, 3])
        w_back = sb("w_back", [128, 3])
        wq_gu = sb("wq_gu", [128, 2, INNER], BF16)
        wq_dn = sb("wq_dn", [128, I_TILES, D], BF16)
        top_x = sb("top_x", [128, 2, 1])
        clip_x = sb("clip_x", [128, 2, 1])
        scale_x = sb("scale_x", [128, 2, 1])
        back_x = sb("back_x", [128, 2, 2])
        top_h = sb("top_h", [128, 2, 1])
        clip_h = sb("clip_h", [128, 2, 1])
        scale_h = sb("scale_h", [128, 2, 1])
        back_h = sb("back_h", [128, 2, 1])
        x_round = sb("x_round", [128, D])
        xq = sb("xq", [128, 2, D], BF16)
        xqT = sb("xqT", [128, 2, 128], BF16)
        gate = sb("gate", [128, 2, INNER])
        h = sb("h", [128, 2, INNER])
        h_round = sb("h_round", [128, INNER])
        hq = sb("hq", [128, INNER], BF16)
        down_scale = sb("down_scale", [128, 2, 1])
        hqT = sb("hqT", [128, I_TILES, 128], BF16)

        ps_max = ctx.enter_context(nc.psum_tensor("ps_max", [128, 2, UH // 2, 128], F32))
        ps_exp = ctx.enter_context(nc.psum_tensor("ps_exp", [128, 2, UH // 2, 128], F32))
        ps_q = ctx.enter_context(nc.psum_tensor("ps_q", [128, 512], F32))
        ps_k = ctx.enter_context(nc.psum_tensor("ps_k", [128, 512], F32))
        ps_in = ctx.enter_context(nc.psum_tensor("ps_in", [128, 512], F32))
        ps_out = ctx.enter_context(nc.psum_tensor("ps_out", [128, 512], F32))
        ps_h1 = [ps_max[:, u, :, :].rearrange("p g k -> p (g k)") for u in range(2)]
        ps_h2 = [ps_exp[:, u, :, :].rearrange("p g k -> p (g k)") for u in range(2)]
        ps_expert = [ps_q, ps_k]
        ps_gu = [a[:, :, :, :].rearrange("p w g k -> p w (g k)") for a in (ps_max, ps_exp)]
        ps_q_b = ps_q[:, :].bitcast(BF16).rearrange("p (h t) -> p h t", h=HEADS // 2)
        ps_k_b = ps_k[:, :].bitcast(BF16).rearrange("p (h t) -> p h t", h=HEADS // 2)

        x_loaded, consts_loaded, ffn_loaded, out_stored = (
            sem("x_loaded"), sem("consts_loaded"), sem("ffn_loaded"), sem("out_stored"))
        ctx_loaded = [sem(f"ctx_loaded{r}") for r in range(2)]
        dve_setup, act_setup, pool_setup, pe_setup = sem("dve_setup"), sem("act_setup"), sem("pool_setup"), sem("pe_setup")
        stats_done, aggr_done, eps_done, rstd_done, xn_done = (
            sem("stats_done"), sem("aggr_done"), sem("eps_done"), sem("rstd_done"), sem("xn_done"))
        xc_turned, xcT_done, qk_made, v_made, v_done = (
            sem("xc_turned"), sem("xcT_done"), sem("qk_made"), sem("v_made"), sem("v_done"))
        f_done, hi_done, rest_done, mid_done, lo_done, stack_done = (
            sem("f_done"), sem("hi_done"), sem("rest_done"), sem("mid_done"), sem("lo_done"), sem("stack_done"))
        k_turned, q_turned, kT_done, qT_done = sem("k_turned"), sem("q_turned"), sem("kT_done"), sem("qT_done")
        max_scores, max_done = sem("max_scores"), sem("max_done")
        n0_done, n0_rest, n1_done, neg_done, m_turned, mT_done = (
            sem("n0_done"), sem("n0_rest"), sem("n1_done"), sem("neg_done"), sem("m_turned"), sem("mT_done"))
        exp_scores, exp_done = sem("exp_scores"), sem("exp_done")
        pv_made, o_done, o_turned, rden_done, norm_done, norm_turned, normT_done = (
            sem("pv_made"), sem("o_done"), sem("o_turned"), sem("rden_done"), sem("norm_done"),
            sem("norm_turned"), sem("normT_done"))
        attn_made, bias_added, attn_done = sem("attn_made"), sem("bias_added"), sem("attn_done")

        ring_done, all_done, xn_turned, gate_made = sem("ring_done"), sem("all_done"), sem("xn_turned"), sem("gate_made")
        route_dve, route_exp = sem("route_dve"), sem("route_exp")
        h1_made, h2_made, silu_done, hidden_done, expert_made, expert_added = (
            sem("h1_made"), sem("h2_made"), sem("silu_done"), sem("hidden_done"), sem("expert_made"), sem("expert_added"))
        w_summed, w_totalled, w_scaled, w_quantised = (
            sem("w_summed"), sem("w_totalled"), sem("w_scaled"), sem("w_quantised"))
        clip_x_done, clip_h_done, scale_x_done, scale_h_done, back_x_done, back_h_done = (
            sem("clip_x_done"), sem("clip_h_done"), sem("scale_x_done"), sem("scale_h_done"), sem("back_x_done"),
            sem("back_h_done"))
        recip_x_done, recip_h_done = sem("recip_x_done"), sem("recip_h_done")
        top_x_done, x_rounded, xq_done, xq_turned, xqT_done, gu_made, gate_done = (
            sem("top_x_done"), sem("x_rounded"), sem("xq_done"), sem("xq_turned"), sem("xqT_done"),
            sem("gu_made"), sem("gate_done"))
        h_done, top_h_done, h_rounded, hq_done, hq_turned, hqT_done, down_made, ffn_done = (
            sem("h_done"), sem("top_h_done"), sem("h_rounded"), sem("hq_done"), sem("hq_turned"),
            sem("hqT_done"), sem("down_made"), sem("ffn_done"))

        LAST = BATCHES - 1

        def batches(eng, step):
            for i in range(-3, 2):
                step(i, i % 2, lambda d: 0 <= i + d <= LAST)
            with eng.Fori(2, LAST - 3, 2) as j:
                for u in range(2):
                    step(j + u, u, lambda d: True)
            for i in range(LAST - 3, LAST + 3):
                step(i, i % 2, lambda d: 0 <= i + d <= LAST)

        block = ctx.enter_context(nc.Block())

        const_loads = [
            (eye[:, :], t["eye"]), (mask[:, :], t["mask"]),
            (gains[:, 0:2], t["g_xattn"].partition_broadcast(128)),
            (gains[:, 2:4], t["g_ffn"].partition_broadcast(128)),
            (wq[0][:, :], t["Wq0"]), (wkv[0][:, 0:128], t["Wk0"]), (wkv[0][:, 128:256], t["Wv0"]),
            (wo[0][:, :], t["Wo0"]),
            (bqk[:, 0:128], t["bq"].partition_broadcast(128)), (bqk[:, 128:256], t["bk"].partition_broadcast(128)),
            (bv_col[:, :], t["bv"].rearrange("(p o) -> p o", o=1)), (bo_row[:, :], t["bo"].partition_broadcast(128)),
            (wq[1][:, :], t["Wq1"]), (wkv[1][:, 0:128], t["Wk1"]), (wkv[1][:, 128:256], t["Wv1"]),
            (wo[1][:, :], t["Wo1"]),
        ]
        ffn_loads = [
            (gate_w[:, :], t["gateT"]),
            (before[:, :, :].rearrange("p a b -> p (a b)"), t["before"].rearrange("a b -> (a b)").partition_broadcast(128)),
            (w12[:, :, :], t["w12T"]), (w3[:, :, :, :], t["w3T"].rearrange("(k p) e d -> p e k d", k=H_TILES)),
            (w_gu[:, 0, :], t["w_gateT"]), (w_gu[:, 1, :], t["w_upT"]),
            (w_dn[:, :, :], t["w_downT"].rearrange("(k p) d -> p k d", k=I_TILES)),
        ]
        CONSTS = 16 * len(const_loads)
        FFN_CONSTS = 16 * len(ffn_loads)
        SETUP_BIAS, SETUP_ALL = 9, 15

        @block.sync
        def _(sp):
            sp.dma_start(x_all[:, :, :], t["x"].rearrange("b s d -> s b d")).then_inc(x_loaded, 16)
            for dst, src in const_loads:
                sp.dma_start(dst, src).then_inc(consts_loaded, 16)

            for dst, src in ffn_loads:
                sp.dma_start(dst, src).then_inc(ffn_loaded, 16)

            def load_contexts(layer):
                def step(i, r, live):
                    n = i + BATCHES * layer
                    if live(0):
                        need(sp, xc_turned, n - 1)
                        sp.dma_start(ctx_in[:, r, :], t["ctx"][i, :, :]).then_inc(ctx_loaded[r], 16)

                for i in range(2):
                    step(i, i % 2, lambda d: True)
                with sp.Fori(2, LAST, 2) as j:
                    for u in range(2):
                        step(j + u, u, lambda d: True)

            load_contexts(0)
            load_contexts(1)
            with sp.Fori(0, BATCHES, 1) as b:
                sp.wait_ge(ffn_done, b + 1)
                sp.dma_start(t["out"][b, :, :], x_all[:, b, :]).then_inc(out_stored, 16)
            sp.wait_ge(out_stored, 16 * BATCHES)

        @block.gpsimd
        def _(pool):
            nc.gpsimd.memset(half[:, :], -0.5).then_inc(pool_setup, 1)
            nc.gpsimd.memset(eps[:, :], EPS).then_inc(pool_setup, 1)
            nc.gpsimd.memset(zero[:, :], 0.0).then_inc(pool_setup, 1)
            nc.gpsimd.memset(ones[:, :], 1.0).then_inc(pool_setup, 1)
            nc.gpsimd.memset(stack[:, :, :, :, :], 0.0).then_inc(pool_setup, 1)
            nc.gpsimd.memset(neg_parts[:, :, :, :, :], 0.0).then_inc(pool_setup, 1)
            nc.gpsimd.memset(v_one[:, :, :, :], 0.0).then_inc(pool_setup, 1)
            pool.wait_ge(pool_setup, 7)
            for r in range(2):
                nc.gpsimd.memset(v_one[:, r, :, HD:HD + 1], 1.0).then_inc(pool_setup, 1)

            def norm_scale(n, s):
                pool.wait_ge(aggr_done, n + 1)
                nc.gpsimd.tensor_tensor(var_eps[:, s, :], mean_var[:, s, 1:2], eps[:, :], ALU.add).then_inc(eps_done, 1)
                pool.wait_ge(eps_done, n + 1)
                nc.gpsimd.tensor_tensor(rstd[:, s, :], var_eps[:, s, :], half[:, :], ALU.pow).then_inc(rstd_done, 1)

            def attention(layer):
                def step(i, r, live):
                    n = i + BATCHES * layer
                    if live(3):
                        norm_scale(n + 3 + BATCHES * layer, (r + 3) % 2)
                    if live(2):
                        if layer == 0:
                            pool.wait_ge(xn_done, n + 3)
                            if isinstance(i, int) and i == -2:
                                pool.wait_ge(dve_setup, SETUP_BIAS)
                            nc.gpsimd.tensor_tensor(x_all[:, i + 2, :], x_all[:, i + 2, :], bias_out[:, :],
                                                    ALU.add).then_inc(bias_added, 1)
                        pool.wait_ge(lo_done, n + 3)
                        q, k = stack[:, r, 0, :, :], stack[:, r, 1, :, :]
                        pair = lambda a, s: a[:, :, s * HD:(s + 2) * HD]
                        nc.gpsimd.tensor_tensor(pair(q, 5), pair(q, 1),
                                                zero[:, :].unsqueeze(2).broadcast_to([128, HEADS, 2 * HD]),
                                                ALU.add).then_inc(stack_done, 1)
                        nc.gpsimd.tensor_scalar(pair(k, 3), pair(k, 1), 1.0, 0.0, ALU.mult, ALU.add).then_inc(stack_done, 1)
                        for a, s in ((q, 3), (k, 5)):
                            dst = pair(a, s).rearrange("p h (c d) -> p h c d", c=2)
                            src = a[:, :, 0:HD].unsqueeze(2).broadcast_to([128, HEADS, 2, HD])
                            nc.gpsimd.tensor_scalar(dst, src, 1.0, 0.0, ALU.mult, ALU.add).then_inc(stack_done, 1)

                batches(pool, step)

            def route():
                def step(i, r, live):
                    if live(3):
                        norm_scale(i + 3 + BATCHES, (r + 3) % 2)
                    if live(2):
                        pool.wait_ge(ring_done, i + 3)
                        nc.gpsimd.tensor_copy(xnT_all[:, i + 2, :], xnT_ring[:, r, :]).then_inc(all_done, 1)

                batches(pool, step)

            def quantise_weights():
                pool.wait_ge(w_scaled, 4)
                for m, (w, out) in enumerate(((w_gu[:, 0, :], wq_gu[:, 0, :]), (w_gu[:, 1, :], wq_gu[:, 1, :]),
                                              (w_dn[:, :, :], wq_dn[:, :, :]))):
                    nc.gpsimd.tensor_scalar(w, w, w_scale[:, m:m + 1], MAGIC, ALU.mult, ALU.add).then_inc(w_quantised, 1)
                    pool.wait_ge(w_quantised, 3 * m + 1)
                    nc.gpsimd.tensor_scalar(w, w, -MAGIC, 1.0, ALU.add, ALU.min).then_inc(w_quantised, 1)
                    pool.wait_ge(w_quantised, 3 * m + 2)
                    nc.gpsimd.tensor_scalar(out, w, -1.0, 1.0, ALU.max, ALU.mult).then_inc(w_quantised, 1)

            def feed_forward():
                def step(i, r, live):
                    s = (r + 1) % 2
                    if live(3):
                        norm_scale(i + 3 + 3 * BATCHES, s)
                    if live(1):
                        pool.wait_ge(clip_h_done, i + 2)
                        nc.gpsimd.tensor_tensor(back_h[:, s, :], clip_h[:, s, :], w_back[:, 2:3], ALU.mult).then_inc(back_h_done, 1)
                    if live(3):
                        pool.wait_ge(clip_x_done, i + 4)
                        nc.gpsimd.tensor_tensor(back_x[:, s, :], clip_x[:, s, :].broadcast_to([128, 2]), w_back[:, 0:2],
                                                ALU.mult).then_inc(back_x_done, 1)

                batches(pool, step)

            attention(0)
            route()
            quantise_weights()
            attention(1)
            feed_forward()

        @block.vector
        def _(dve):
            scale = float(HD) ** -0.5
            dve.wait_ge(consts_loaded, CONSTS)
            nc.vector.tensor_copy(eye_b[:, :], eye[:, :]).then_inc(dve_setup, 1)
            nc.vector.tensor_scalar(wq[0][:, :], wq[0][:, :], scale, None, ALU.mult).then_inc(dve_setup, 1)
            nc.vector.tensor_scalar(wq[1][:, :], wq[1][:, :], scale, None, ALU.mult).then_inc(dve_setup, 1)
            nc.vector.tensor_scalar(bqk[:, 0:128], bqk[:, 0:128], scale, None, ALU.mult).then_inc(dve_setup, 1)
            nc.vector.tensor_reduce(sel_ind[:, :], eye[:, :].rearrange("p (a c h) -> p h a c", a=2, c=4)[:, :, :, 0:3],
                                    AX.XY, ALU.add).then_inc(dve_setup, 1)
            dve.wait_ge(pool_setup, 9)
            nc.vector.tensor_scalar(bv_rep[:, :], ones[:, :], bv_col[:, 0:1], None, ALU.mult).then_inc(dve_setup, 1)
            dve.wait_ge(dve_setup, 5)
            nc.vector.tensor_copy(sel[:, :, :], sel_ind[:, :].unsqueeze(2).broadcast_to([128, HEADS, 128])).then_inc(dve_setup, 1)
            dve.wait_ge(pe_setup, 1)
            nc.vector.tensor_tensor(bias_out[:, :], ps_in[:, 0:128], bo_row[:, :], ALU.add).then_inc(dve_setup, 1)
            dve.wait_ge(dve_setup, 8)
            dve.wait_ge(act_setup, 1)
            nc.vector.tensor_scalar(bias_out[:, :], bias_out[:, :], tanh_g[:, 0:1], None, ALU.mult).then_inc(dve_setup, 1)
            nc.vector.tensor_scalar(wo[0][:, :], wo[0][:, :], tanh_g[:, 0:1], None, ALU.mult).then_inc(dve_setup, 1)
            nc.vector.tensor_scalar(wo[1][:, :], wo[1][:, :], tanh_g[:, 1:2], None, ALU.mult).then_inc(dve_setup, 1)
            nc.vector.tensor_copy(mask_parts[:, 0, :], mask[:, :]).then_inc(dve_setup, 1)
            dve.wait_ge(dve_setup, 12)
            nc.vector.tensor_tensor(mask_rest[:, :], mask[:, :], mask_parts[:, 0, :], ALU.subtract).then_inc(dve_setup, 1)
            dve.wait_ge(dve_setup, 13)
            nc.vector.tensor_copy(mask_parts[:, 1, :], mask_rest[:, :]).then_inc(dve_setup, 1)
            dve.wait_ge(dve_setup, 14)
            nc.vector.tensor_tensor(mask_parts[:, 2, :], mask_rest[:, :], mask_parts[:, 1, :], ALU.subtract).then_inc(dve_setup, 1)
            dve.wait_ge(x_loaded, 16)

            def norm_stats(b, s):
                nc.vector.bn_stats(stats[:, s, :], x_all[:, b, :]).then_inc(stats_done, 1)

            def norm_aggregate(s):
                nc.vector.bn_aggr(mean_var[:, s, :], stats[:, s, :]).then_inc(aggr_done, 1)

            def norm_apply(n, b, s):
                dve.wait_ge(rstd_done, n + 1)
                nc.vector.tensor_scalar(xn[:, s, :], x_all[:, b, :], mean_var[:, s, 0:1], rstd[:, s, :],
                                        ALU.subtract, ALU.mult).then_inc(xn_done, 1)

            def attention(layer):
                def row_max(n, r, u):
                    dve.wait_ge(max_scores, 2 * n + u + 1)
                    out = neg_max[:, r, UH * u:UH * u + UH].rearrange("p (g j) -> p j g", j=2)
                    nc.vector.tensor_reduce(out, ps_max[:, :, :, :], AX.X, ALU.max, negate=True).then_inc(max_done, 1)

                def step(i, r, live):
                    n = i + BATCHES * layer
                    if live(0):
                        row_max(n, r, 0)
                    if live(-2):
                        dve.wait_ge(o_turned, n - 1)
                        o = ps_out[:, :].rearrange("p (h c) -> p h c", h=HEADS)
                        nc.vector.reciprocal(o_rden[:, :], o[:, :, HD]).then_inc(rden_done, 1)
                        dve.wait_ge(rden_done, n - 1)
                        nc.vector.tensor_tensor(o_norm[:, :].rearrange("p (h d) -> p h d", h=HEADS), o[:, :, 0:HD],
                                                o_rden[:, :].unsqueeze(2).broadcast_to([128, HEADS, HD]),
                                                ALU.mult).then_inc(norm_done, 1)
                    if live(3):
                        norm_stats(i + 3, (r + 3) % 2)
                        dve.wait_ge(stats_done, n + 4 + BATCHES * layer)
                    if live(0):
                        row_max(n, r, 1)
                    if live(3):
                        norm_aggregate((r + 3) % 2)
                    if live(-2):
                        dve.wait_ge(attn_made, n - 1)
                        if layer == 0:
                            dve.wait_ge(bias_added, n - 1)
                        nc.vector.tensor_tensor(x_all[:, i - 2, :], ps_out[:, 128:256], x_all[:, i - 2, :],
                                                ALU.add).then_inc(attn_done, 1)
                    if live(0):
                        part = lambda c: neg_parts[:, r, :, c, :]
                        twice = lambda a: a.unsqueeze(1).broadcast_to([128, 2, HEADS])
                        dve.wait_ge(max_done, 2 * n + 2)
                        nc.vector.tensor_copy(part(0), twice(neg_max[:, r, :])).then_inc(n0_done, 1)
                        dve.wait_ge(n0_done, n + 1)
                        nc.vector.tensor_tensor(neg_rest[:, r, :], neg_max[:, r, :], neg_parts[:, r, 0, 0, :],
                                                ALU.subtract).then_inc(n0_rest, 1)
                        dve.wait_ge(n0_rest, n + 1)
                        nc.vector.tensor_copy(part(1), twice(neg_rest[:, r, :])).then_inc(n1_done, 1)
                        dve.wait_ge(n1_done, n + 1)
                        nc.vector.tensor_tensor(part(2), twice(neg_rest[:, r, :]), part(1),
                                                ALU.subtract).then_inc(neg_done, 1)
                    if live(2):
                        heads = lambda a: a[:, r, :].rearrange("p (w h d) -> p w h d", w=2, h=HEADS)
                        slot = lambda c: stack[:, r, :, :, c * HD:(c + 1) * HD]
                        dve.wait_ge(qk_made, n + 3)
                        if layer == 0:
                            nc.vector.tensor_tensor(qk[:, r, :], ps_in[:, 0:256], bqk[:, :], ALU.add).then_inc(f_done, 1)
                        else:
                            nc.vector.tensor_copy(qk[:, r, :], ps_in[:, 0:256]).then_inc(f_done, 1)
                        dve.wait_ge(f_done, n + 3)
                        nc.vector.tensor_copy(slot(0), heads(qk)).then_inc(hi_done, 1)
                        dve.wait_ge(hi_done, n + 3)
                        nc.vector.tensor_tensor(heads(qk_rest), heads(qk), slot(0), ALU.subtract).then_inc(rest_done, 1)
                        dve.wait_ge(rest_done, n + 3)
                        nc.vector.tensor_copy(slot(1), heads(qk_rest)).then_inc(mid_done, 1)
                        dve.wait_ge(mid_done, n + 3)
                        nc.vector.tensor_tensor(slot(2), heads(qk_rest), slot(1), ALU.subtract).then_inc(lo_done, 1)
                    if live(3):
                        norm_apply(n + 3 + BATCHES * layer, i + 3, (r + 3) % 2)

                batches(dve, step)

            def route():
                def step(i, r, live):
                    if live(3):
                        norm_stats(i + 3, (r + 3) % 2)
                        dve.wait_ge(stats_done, i + 4 + BATCHES)
                    if live(2):
                        norm_apply(i + 2 + BATCHES, i + 2, r)
                    if live(3):
                        norm_aggregate((r + 3) % 2)

                batches(dve, step)
                pairs = [128, BATCHES, EXPERTS, EXPERTS]
                other = scores[:, :, :].unsqueeze(2).broadcast_to(pairs)
                this = scores[:, :, :].unsqueeze(3).broadcast_to(pairs)
                lower = before[:, :, :].unsqueeze(1).broadcast_to(pairs)
                over = lambda a: a.unsqueeze(2).broadcast_to([128, BATCHES, EXPERTS])
                dve.wait_ge(gate_made, BATCHES)
                nc.vector.tensor_copy(scores[:, :, :], ps_out[:, 0:BATCHES * EXPERTS].rearrange("p (b e) -> p b e", e=EXPERTS)).then_inc(route_dve, 1)
                dve.wait_ge(route_dve, 1)
                nc.vector.tensor_reduce(top[:, :], scores[:, :, :], AX.X, ALU.max).then_inc(route_dve, 1)
                dve.wait_ge(route_dve, 2)
                nc.vector.tensor_tensor(shifted[:, :, :], scores[:, :, :], over(top[:, :]), ALU.subtract).then_inc(route_dve, 1)
                dve.wait_ge(ffn_loaded, FFN_CONSTS)
                nc.vector.tensor_tensor(greater[:, :, :, :], other, this, ALU.is_gt).then_inc(route_dve, 1)
                nc.vector.tensor_tensor(at_least[:, :, :, :], other, this, ALU.is_ge).then_inc(route_dve, 1)
                dve.wait_ge(route_dve, 5)
                nc.vector.tensor_tensor(at_least[:, :, :, :], at_least[:, :, :, :], greater[:, :, :, :], ALU.subtract).then_inc(route_dve, 1)
                dve.wait_ge(route_dve, 6)
                nc.vector.tensor_tensor(at_least[:, :, :, :], at_least[:, :, :, :], lower, ALU.mult).then_inc(route_dve, 1)
                dve.wait_ge(route_dve, 7)
                nc.vector.tensor_tensor(greater[:, :, :, :], at_least[:, :, :, :], greater[:, :, :, :], ALU.add).then_inc(route_dve, 1)
                dve.wait_ge(route_dve, 8)
                nc.vector.tensor_reduce(rank[:, :, :], greater[:, :, :, :], AX.X, ALU.add).then_inc(route_dve, 1)
                dve.wait_ge(route_dve, 9)
                nc.vector.tensor_scalar(chosen[:, :, :], rank[:, :, :], 2.0, None, ALU.is_lt).then_inc(route_dve, 1)
                dve.wait_ge(route_dve, 10)
                dve.wait_ge(route_exp, 1)
                nc.vector.tensor_tensor(weight[:, :, :], chosen[:, :, :], shifted[:, :, :], ALU.mult).then_inc(route_dve, 1)
                dve.wait_ge(route_dve, 11)
                nc.vector.tensor_reduce(weight_sum[:, :], weight[:, :, :], AX.X, ALU.add).then_inc(route_dve, 1)
                dve.wait_ge(route_dve, 12)
                nc.vector.reciprocal(top[:, :], weight_sum[:, :]).then_inc(route_dve, 1)
                dve.wait_ge(route_dve, 13)
                nc.vector.tensor_scalar(top[:, :], top[:, :], tanh_g[:, 2:3], None, ALU.mult).then_inc(route_dve, 1)
                dve.wait_ge(route_dve, 14)
                nc.vector.tensor_tensor(weight[:, :, :], weight[:, :, :], over(top[:, :]), ALU.mult).then_inc(route_dve, 1)

            def add_expert(g, e):
                dve.wait_ge(expert_made, EXPERTS * g + e + 1)
                need(dve, expert_added, EXPERTS * g + e)
                for b in range(GROUP):
                    nc_b = GROUP * g + b
                    last = nc.vector.scalar_tensor_tensor(x_all[:, nc_b, :], ps_expert[e % 2][:, 128 * b:128 * (b + 1)],
                                                          weight[:, nc_b, e:e + 1], x_all[:, nc_b, :],
                                                          ALU.mult, ALU.add)
                last.then_inc(expert_added, 1)

            def experts():
                def group(g, first):
                    for e in range(EXPERTS):
                        for k in range(H_TILES):
                            m = (EXPERTS * g + e) * H_TILES + k
                            u = k % 2
                            dve.wait_ge(silu_done, m + 1)
                            dve.wait_ge(h2_made, m + 1)
                            nc.vector.tensor_tensor(hidden[:, e % 2, k, :], silu[:, u, :], ps_h2[u], ALU.mult).then_inc(hidden_done, 1)
                        if e:
                            add_expert(g, e - 1)
                        elif not first:
                            add_expert(g - 1, EXPERTS - 1)

                dve.wait_ge(route_dve, 15)
                group(0, True)
                with dve.Fori(1, GROUPS, 1) as g:
                    group(g, False)
                add_expert(GROUPS - 1, EXPERTS - 1)
                dve.wait_ge(expert_added, EXPERTS * GROUPS)

            def weight_scales():
                count = INNER * D
                dve.wait_ge(w_totalled, 1)
                nc.vector.tensor_scalar(w_mean[:, :], ps_in[:, 0:3], 1.0 / count, 1e-5, ALU.mult, ALU.max).then_inc(w_scaled, 1)
                dve.wait_ge(w_scaled, 1)
                nc.vector.reciprocal(w_scale[:, :], w_mean[:, :]).then_inc(w_scaled, 1)
                dve.wait_ge(w_scaled, 2)
                nc.vector.reciprocal(w_inv[:, :], w_scale[:, :]).then_inc(w_scaled, 1)
                dve.wait_ge(w_scaled, 3)
                nc.vector.tensor_scalar(w_back[:, :], w_inv[:, :], 1.0 / 127.0, None, ALU.mult).then_inc(w_scaled, 1)

            def quant_scale(n, top, top_done, clip, clip_done, scale, recip_done, scale_done):
                dve.wait_ge(top_done, n + 1)
                nc.vector.tensor_scalar(clip, top, 1e-5, None, ALU.max).then_inc(clip_done, 1)
                dve.wait_ge(clip_done, n + 1)
                nc.vector.reciprocal(scale, clip).then_inc(recip_done, 1)
                dve.wait_ge(recip_done, n + 1)
                nc.vector.tensor_scalar(scale, scale, 127.0, None, ALU.mult).then_inc(scale_done, 1)

            def feed_forward():
                def step(i, r, live):
                    s = (r + 1) % 2
                    if live(-1):
                        dve.wait_ge(down_made, i)
                        nc.vector.scalar_tensor_tensor(x_all[:, i - 1, :], ps_out[:, 0:128], down_scale[:, s, :],
                                                       x_all[:, i - 1, :], ALU.mult, ALU.add).then_inc(ffn_done, 1)
                    if live(0):
                        dve.wait_ge(scale_h_done, i + 1)
                        dve.wait_ge(back_h_done, i + 1)
                        nc.vector.tensor_scalar(h_round[:, :], h[:, r, :], scale_h[:, r, :], MAGIC, ALU.mult, ALU.add).then_inc(h_rounded, 1)
                        nc.vector.tensor_scalar(down_scale[:, r, :], back_h[:, r, :], tanh_g[:, 3:4], None, ALU.mult)
                        dve.wait_ge(h_rounded, i + 1)
                        nc.vector.tensor_scalar(hq[:, :], h_round[:, :], MAGIC, 127.0, ALU.subtract, ALU.min).then_inc(hq_done, 1)
                    if live(3):
                        norm_stats(i + 3, s)
                        dve.wait_ge(stats_done, i + 4 + 3 * BATCHES)
                    if live(2):
                        dve.wait_ge(scale_x_done, i + 3)
                        nc.vector.tensor_scalar(x_round[:, :], xn[:, r, :], scale_x[:, r, :], MAGIC, ALU.mult, ALU.add).then_inc(x_rounded, 1)
                        dve.wait_ge(x_rounded, i + 3)
                        nc.vector.tensor_scalar(xq[:, r, :], x_round[:, :], MAGIC, 127.0, ALU.subtract, ALU.min).then_inc(xq_done, 1)
                    if live(3):
                        norm_aggregate(s)
                    if live(1):
                        dve.wait_ge(gate_done, i + 2)
                        nc.vector.scalar_tensor_tensor(h[:, s, :], ps_gu[s][:, 1, :], back_x[:, s, 1:2], gate[:, s, :],
                                                       ALU.mult, ALU.mult).then_inc(h_done, 1)
                        dve.wait_ge(h_done, i + 2)
                        nc.vector.tensor_reduce(top_h[:, s, :], h[:, s, :], AX.X, ALU.max, apply_absolute_value=True).then_inc(top_h_done, 1)
                        quant_scale(i + 1, top_h[:, s, :], top_h_done, clip_h[:, s, :], clip_h_done,
                                    scale_h[:, s, :], recip_h_done, scale_h_done)
                    if live(3):
                        norm_apply(i + 3 + 3 * BATCHES, i + 3, s)
                        dve.wait_ge(xn_done, i + 4 + 3 * BATCHES)
                        nc.vector.tensor_reduce(top_x[:, s, :], xn[:, s, :], AX.X, ALU.max, apply_absolute_value=True).then_inc(top_x_done, 1)
                        quant_scale(i + 3, top_x[:, s, :], top_x_done, clip_x[:, s, :], clip_x_done,
                                    scale_x[:, s, :], recip_x_done, scale_x_done)

                batches(dve, step)

            attention(0)
            dve.wait_ge(attn_done, BATCHES)
            route()
            weight_scales()
            experts()
            attention(1)
            dve.wait_ge(attn_done, 2 * BATCHES)
            feed_forward()

        @block.scalar
        def _(act):
            act.wait_ge(consts_loaded, CONSTS)
            nc.scalar.activation(tanh_g[:, :], gains[:, :], ACT.Tanh).then_inc(act_setup, 1)
            act.wait_ge(dve_setup, SETUP_ALL)

            def attention(layer):
                def exponentials(n, u):
                    act.wait_ge(exp_scores, 2 * n + u + 1)
                    need(act, pv_made, 2 * n + u - 1)
                    nc.scalar.activation(probs[:, u, :, :, :], ps_exp[:, :, :, :], ACT.Exp).then_inc(exp_done, 1)

                def step(i, r, live):
                    n = i + BATCHES * layer
                    if live(-1):
                        exponentials(n - 1, 0)
                    if live(2):
                        act.wait_ge(xc_turned, n + 3)
                        nc.scalar.activation(xcT[:, r, :], ps_in[:, 0:256], ACT.Copy).then_inc(xcT_done, 1)
                    if live(-2):
                        act.wait_ge(norm_turned, n - 1)
                        nc.scalar.activation(o_normT[:, :], ps_out[:, 0:128], ACT.Copy).then_inc(normT_done, 1)
                    if live(-1):
                        exponentials(n - 1, 1)
                    if live(1):
                        s = (r + 1) % 2
                        act.wait_ge(k_turned, n + 2)
                        nc.scalar.activation(kT[:, s, :, :], ps_k_b, ACT.Copy).then_inc(kT_done, 1)
                        act.wait_ge(q_turned, n + 2)
                        nc.scalar.activation(qT[:, s, :, :], ps_q_b, ACT.Copy).then_inc(qT_done, 1)
                    if live(-1):
                        act.wait_ge(pv_made, 2 * n)
                        nc.scalar.activation(o_raw[:, :], ps_out[:, :], ACT.Copy).then_inc(o_done, 1)
                    if live(1):
                        s = (r + 1) % 2
                        act.wait_ge(v_made, n + 2)
                        nc.scalar.activation(v_one[:, s, :, 0:HD],
                                             ps_in[:, 256:384].rearrange("p (h d) -> p h d", h=HEADS),
                                             ACT.Copy).then_inc(v_done, 1)
                    if live(0):
                        act.wait_ge(m_turned, n + 1)
                        nc.scalar.activation(mT[:, r, :], ps_k_b[:, 0, :], ACT.Copy).then_inc(mT_done, 1)

                batches(act, step)

            def route():
                def step(i, r, live):
                    if live(2):
                        act.wait_ge(xn_turned, i + 3)
                        need(act, all_done, i + 1)
                        nc.scalar.activation(xnT_ring[:, r, :], ps_in[:, 128 * r:128 * r + 128], ACT.Copy).then_inc(ring_done, 1)

                batches(act, step)
                act.wait_ge(ffn_loaded, FFN_CONSTS)
                nc.scalar.activation(w_abs[:, 0:INNER], w_gu[:, 0, :], ACT.Abs, accum_out=w_sums[:, 0:1]).then_inc(w_summed, 1)
                nc.scalar.activation(w_abs[:, INNER:2 * INNER], w_gu[:, 1, :], ACT.Abs, accum_out=w_sums[:, 1:2]).then_inc(w_summed, 1)
                act.wait_ge(w_summed, 2)
                nc.scalar.activation(w_abs[:, 0:INNER].rearrange("p (k d) -> p k d", k=I_TILES), w_dn[:, :, :], ACT.Abs,
                                     accum_out=w_sums[:, 2:3]).then_inc(w_summed, 1)
                act.wait_ge(route_dve, 3)
                nc.scalar.activation(shifted[:, :, :], shifted[:, :, :], ACT.Exp).then_inc(route_exp, 1)

            def experts():
                def group(g):
                    for m in range(EXPERTS * H_TILES):
                        n = EXPERTS * H_TILES * g + m
                        act.wait_ge(h1_made, n + 1)
                        need(act, hidden_done, n - 1 if isinstance(g, int) else n - 1)
                        nc.scalar.activation(silu[:, m % 2, :], ps_h1[m % 2], ACT.Silu).then_inc(silu_done, 1)

                group(0)
                with act.Fori(1, GROUPS, 1) as g:
                    group(g)

            def feed_forward():
                def step(i, r, live):
                    s = (r + 1) % 2
                    if live(1):
                        act.wait_ge(gu_made, i + 2)
                        act.wait_ge(back_x_done, i + 2)
                        nc.scalar.activation(gate[:, s, :], ps_gu[s][:, 0, :], ACT.Silu, scale=back_x[:, s, 0:1]).then_inc(gate_done, 1)
                    if live(0):
                        act.wait_ge(hq_turned, i + 1)
                        nc.scalar.activation(hqT[:, :, :], ps_q_b[:, 0:I_TILES, :], ACT.Copy).then_inc(hqT_done, 1)
                    if live(2):
                        act.wait_ge(xq_turned, i + 3)
                        nc.scalar.activation(xqT[:, r, :], ps_k_b[:, 0, :], ACT.Copy).then_inc(xqT_done, 1)

                batches(act, step)

            attention(0)
            route()
            experts()
            attention(1)
            feed_forward()

        @block.tensor
        def _(pe):
            pe.wait_ge(dve_setup, 6)
            nc.tensor.matmul(ps_in[:, 0:128], bv_rep[:, :], wo[0][:, :], start=True, stop=True).then_inc(pe_setup, 1)
            pe.wait_ge(dve_setup, SETUP_ALL)

            def attention(layer):
                q4 = lambda a: a.unsqueeze(1).broadcast_to([128, UH // 2, 128])

                def scores_for_max(n, r, u):
                    if u == 0:
                        pe.wait_ge(kT_done, n + 1)
                        pe.wait_ge(qT_done, n + 1)
                    need(pe, max_done, 2 * n + u)
                    if layer == 1:
                        for j in range(2):
                            for c in range(2):
                                nc.tensor.matmul(ps_max[:, j, :, :], eye_b[:, :], q4(mask_parts[:, c, :]),
                                                 start=(c == 0), stop=False, skip_group_check=True)
                    for g in range(UH // 2):
                        for j in range(2):
                            rows = slice(SLOT_ROWS * j, SLOT_ROWS * (j + 1))
                            p = UH // 2 * u + g
                            last = nc.tensor.matmul(ps_max[:, j, g, :], qT[rows, r, p, :], kT[rows, r, p, :],
                                                    start=(layer == 0), stop=True, skip_group_check=True)
                    last.then_inc(max_scores, 1)

                def scores_for_exp(n, r, u):
                    if u == 0:
                        pe.wait_ge(mT_done, n + 1)
                    need(pe, exp_done, 2 * n + u)
                    if layer == 1:
                        for j in range(2):
                            for c in range(3):
                                nc.tensor.matmul(ps_exp[:, j, :, :], mask_parts[:, c, :], q4(eye_b[:, :]),
                                                 start=(c == 0), stop=False, skip_group_check=True)
                    for g in range(UH // 2):
                        for j in range(2):
                            rows = slice(SLOT_ROWS * j, SLOT_ROWS * (j + 1))
                            p = UH // 2 * u + g
                            nc.tensor.matmul(ps_exp[:, j, g, :], kT[rows, r, p, :], qT[rows, r, p, :],
                                             start=(layer == 0), stop=False, skip_group_check=True)
                            last = nc.tensor.matmul(ps_exp[:, j, g, :], sel[rows, 2 * p + j, :], mT[rows, r, :],
                                                    start=False, stop=True, skip_group_check=True)
                    last.then_inc(exp_scores, 1)

                def probs_times_v(n, r, u):
                    pe.wait_ge(exp_done, 2 * n + u + 1)
                    if u == 0:
                        pe.wait_ge(v_done, n + 1)
                        need(pe, attn_done, n)
                    for g in range(UH // 2):
                        for j in range(2):
                            h = UH * u + 2 * g + j
                            strip = V_COLS * (h % 4)
                            last = nc.tensor.matmul(ps_out[strip:strip + V_COLS, 128 * (h // 4):128 * (h // 4 + 1)],
                                                    v_one[:, r, h, :], probs[:, u, j, g, :], start=True, stop=True,
                                                    skip_group_check=True)
                    last.then_inc(pv_made, 1)

                def step(i, r, live):
                    n = i + BATCHES * layer
                    if live(0):
                        scores_for_max(n, r, 0)
                    if live(-2):
                        pe.wait_ge(o_done, n - 1)
                        for c in range(4):
                            last = nc.tensor.transpose(ps_out[:, 128 * c:128 * c + 128], o_raw[:, 128 * c:128 * c + 128],
                                                       eye[:, :])
                        last.then_inc(o_turned, 1)
                    if live(-1):
                        scores_for_exp(n - 1, (r + 1) % 2, 0)
                    if live(2):
                        pe.wait_ge(xn_done, n + 3 + BATCHES * layer)
                        pe.wait_ge(ctx_loaded[r], 8 * (n + 2 - r) + 16)
                        if isinstance(i, int) and i == -2:
                            need(pe, v_done, n + 2)
                        else:
                            need(pe, v_done, n + 1)
                        nc.tensor.transpose(ps_in[:, 0:128], xn[:, r, :], eye[:, :])
                        nc.tensor.transpose(ps_in[:, 128:256], ctx_in[:, r, :], eye[:, :]).then_inc(xc_turned, 1)
                    if live(-2):
                        pe.wait_ge(norm_done, n - 1)
                        nc.tensor.transpose(ps_out[:, 0:128], o_norm[:, :], eye[:, :]).then_inc(norm_turned, 1)
                    if live(0):
                        scores_for_max(n, r, 1)
                    if live(-2):
                        pe.wait_ge(normT_done, n - 1)
                        nc.tensor.matmul(ps_out[:, 128:256], o_normT[:, :], wo[layer][:, :],
                                         start=True, stop=True).then_inc(attn_made, 1)
                    if live(2):
                        pe.wait_ge(xcT_done, n + 3)
                        nc.tensor.matmul(ps_in[:, 0:128], xcT[:, r, 0:128], wq[layer][:, :], start=True, stop=True)
                        nc.tensor.matmul(ps_in[:, 128:256], xcT[:, r, 128:256], wkv[layer][:, 0:128],
                                         start=True, stop=True).then_inc(qk_made, 1)
                    if live(-1):
                        scores_for_exp(n - 1, (r + 1) % 2, 1)
                        probs_times_v(n - 1, (r + 1) % 2, 0)
                    if live(1):
                        s = (r + 1) % 2
                        pe.wait_ge(stack_done, 4 * (n + 2))
                        need(pe, mT_done, n)
                        for p in range(HEADS // 2):
                            last = nc.tensor.transpose(ps_k_b[:, p, :], stack[:, s, 1, 2 * p:2 * p + 2, :], eye_b[:, :])
                        last.then_inc(k_turned, 1)
                        need(pe, qT_done, n + 1)
                        for p in range(HEADS // 2):
                            last = nc.tensor.transpose(ps_q_b[:, p, :], stack[:, s, 0, 2 * p:2 * p + 2, :], eye_b[:, :])
                        last.then_inc(q_turned, 1)
                    if live(-1):
                        probs_times_v(n - 1, (r + 1) % 2, 1)
                    if live(1):
                        s = (r + 1) % 2
                        pe.wait_ge(f_done, n + 3 if live(2) else n + 2)
                        nc.tensor.matmul(ps_in[:, 256:384], xcT[:, s, 128:256], wkv[layer][:, 128:256],
                                         start=True, stop=True).then_inc(v_made, 1)
                    if live(0):
                        pe.wait_ge(neg_done, n + 1)
                        pe.wait_ge(kT_done, n + 2 if live(1) else n + 1)
                        nc.tensor.transpose(ps_k_b[:, 0, :], neg_parts[:, r, :, :, :], eye_b[:, :]).then_inc(m_turned, 1)

                batches(pe, step)

            def route():
                def step(i, r, live):
                    if live(2):
                        pe.wait_ge(xn_done, i + 3 + BATCHES)
                        need(pe, ring_done, i + 2)
                        nc.tensor.transpose(ps_in[:, 128 * r:128 * r + 128], xn[:, r, :], eye[:, :]).then_inc(xn_turned, 1)
                    if live(1):
                        s = (r + 1) % 2
                        pe.wait_ge(ring_done, i + 2)
                        nc.tensor.matmul(ps_out[:, bass.ds((i + 1) * EXPERTS, EXPERTS)], xnT_ring[:, s, :], gate_w[:, :],
                                         start=True, stop=True, skip_group_check=True).then_inc(gate_made, 1)

                pe.wait_ge(ffn_loaded, FFN_CONSTS)
                batches(pe, step)
                pe.wait_ge(w_summed, 3)
                nc.tensor.matmul(ps_in[:, 0:3], ones[:, :], w_sums[:, :], start=True, stop=True).then_inc(w_totalled, 1)

            def experts():
                def up(g, e):
                    x_group = xnT_all[:, bass.ds(GROUP * g, GROUP), :]
                    for k in range(H_TILES):
                        m = (EXPERTS * g + e) * H_TILES + k
                        need(pe, hidden_done, m - 1)
                        nc.tensor.matmul(ps_h1[k % 2], w12[:, e, 128 * k:128 * k + 128], x_group,
                                         start=True, stop=True).then_inc(h1_made, 1)
                        k2 = TWO_H // 2 + 128 * k
                        nc.tensor.matmul(ps_h2[k % 2], w12[:, e, k2:k2 + 128], x_group,
                                         start=True, stop=True).then_inc(h2_made, 1)

                def down(g, e):
                    pe.wait_ge(hidden_done, (EXPERTS * g + e + 1) * H_TILES)
                    need(pe, expert_added, EXPERTS * g + e - 1)
                    for b in range(GROUP):
                        for k in range(H_TILES):
                            last = nc.tensor.matmul(ps_expert[e % 2][:, 128 * b:128 * b + 128],
                                                    hidden[:, e % 2, k, 128 * b:128 * b + 128], w3[:, e, k, :],
                                                    start=(k == 0), stop=(k == H_TILES - 1))
                    last.then_inc(expert_made, 1)

                def group(g, first):
                    for e in range(EXPERTS):
                        up(g, e)
                        if e:
                            down(g, e - 1)
                        elif not first:
                            down(g - 1, EXPERTS - 1)

                pe.wait_ge(all_done, BATCHES)
                group(0, True)
                with pe.Fori(1, GROUPS, 1) as g:
                    group(g, False)
                down(GROUPS - 1, EXPERTS - 1)

            def feed_forward():
                def step(i, r, live):
                    s = (r + 1) % 2
                    if live(1):
                        pe.wait_ge(xqT_done, i + 2)
                        need(pe, h_done, i)
                        for w in range(2):
                            last = nc.tensor.matmul(ps_gu[s][:, w, :], xqT[:, s, :], wq_gu[:, w, :], start=True, stop=True)
                        last.then_inc(gu_made, 1)
                    if live(0):
                        pe.wait_ge(hq_done, i + 1)
                        need(pe, hqT_done, i)
                        for k in range(I_TILES):
                            last = nc.tensor.transpose(ps_q_b[:, k, :], hq[:, 128 * k:128 * k + 128], eye_b[:, :])
                        last.then_inc(hq_turned, 1)
                    if live(2):
                        pe.wait_ge(xq_done, i + 3)
                        need(pe, xqT_done, i + 2)
                        nc.tensor.transpose(ps_k_b[:, 0, :], xq[:, r, :], eye_b[:, :]).then_inc(xq_turned, 1)
                    if live(0):
                        pe.wait_ge(hqT_done, i + 1)
                        need(pe, ffn_done, i)
                        for k in range(I_TILES):
                            last = nc.tensor.matmul(ps_out[:, 0:128], hqT[:, k, :], wq_dn[:, k, :],
                                                    start=(k == 0), stop=(k == I_TILES - 1))
                        last.then_inc(down_made, 1)

                pe.wait_ge(w_quantised, 9)
                batches(pe, step)

            attention(0)
            route()
            experts()
            attention(1)
            feed_forward()


def layouts(inputs):
    import numpy as np

    a = {k: np.asarray(v) for k, v in inputs.items()}
    turn = lambda w, *axes: np.ascontiguousarray(np.transpose(w, axes))
    d = a["x"].shape[-1]
    out = {
        "x": a["x"], "ctx": a["ctx_1024"], "mask": a["fside_SxS2_0"], "g_xattn": a["g_xattn"], "g_ffn": a["g_ffn"],
        "Wq0": a["L0_xattn_Wq"], "Wk0": a["L0_xattn_Wk"], "Wv0": a["L0_xattn_Wv"], "Wo0": a["L0_xattn_Wo"],
        "bq": a["L0_xattn_bq"], "bk": a["L0_xattn_bk"], "bv": a["L0_xattn_bv"], "bo": a["L0_xattn_bo"],
        "Wq1": turn(a["L1_xattn_WQ"], 1, 0, 2).reshape(d, d), "Wk1": turn(a["L1_xattn_WK"], 1, 0, 2).reshape(d, d),
        "Wv1": turn(a["L1_xattn_WV"], 1, 0, 2).reshape(d, d), "Wo1": a["L1_xattn_WO"],
        "w12T": turn(a["L0_ffn_w12"], 2, 0, 1), "w3T": turn(a["L0_ffn_w3"], 2, 0, 1),
        "gateT": turn(a["L0_ffn_gate_w"], 1, 0),
        "w_gateT": turn(a["L1_ffn_w_gate"], 1, 0), "w_upT": turn(a["L1_ffn_w_up"], 1, 0),
        "w_downT": turn(a["L1_ffn_w_down"], 1, 0),
        "eye": np.eye(128, dtype=np.float32), "before": np.tril(np.ones((8, 8), np.float32), -1),
    }
    return {k: np.ascontiguousarray(v) for k, v in out.items()}


def kernel(**inputs):
    import concourse.bacc as bacc
    from concourse.bass_utils import run_bass_kernel_spmd

    arrays = layouts(inputs)
    nc = bacc.Bacc("TRN2", target_bir_lowering=False, num_devices=1)
    t = {k: nc.dram_tensor(f"in_{k}", a.shape, mybir.dt.from_np(a.dtype), kind="ExternalInput").ap()
         for k, a in arrays.items()}
    t["out"] = nc.dram_tensor("out_x", arrays["x"].shape, mybir.dt.float32, kind="ExternalOutput").ap()
    gated_cross_attention_stack(nc, t)
    r = run_bass_kernel_spmd(nc, [{f"in_{k}": a for k, a in arrays.items()}], core_ids=[0])
    return r.results[0]["out_x"]
```

```python
import concourse.bass as bass
from concourse import mybir
from contextlib import ExitStack


def gated_cross_attention_stack(nc, t):
    F32, BF16 = mybir.dt.float32, mybir.dt.bfloat16
    ALU = mybir.AluOpType
    ACT = mybir.ActivationFunctionType
    AX = mybir.AxisListType

    BATCHES, _, D = t["x"].shape
    HEADS, HD = 16, D // 16
    UNITS, UH = 2, HEADS // 2
    EXPERTS, TWO_H = t["w12T"].shape[1:]
    H_TILES = TWO_H // 2 // 128
    INNER = t["w_gateT"].shape[1]
    I_TILES = INNER // 128
    GROUP = 4
    GROUPS = BATCHES // GROUP
    SLOTS, SLOT_ROWS = 8, 64
    V_COLS = 32
    EPS = 1e-5
    MAGIC = 1.5 * 2.0 ** 23

    ctx = ExitStack()
    with ctx:
        def sb(name, shape, dt=F32):
            return ctx.enter_context(nc.sbuf_tensor(f"{name}_sb", shape, dt))

        def sem(name):
            return ctx.enter_context(nc.semaphore(name))

        def need(eng, semaphore, count):
            if not isinstance(count, int) or count > 0:
                eng.wait_ge(semaphore, count)

        x_all = sb("x_all", [128, BATCHES, D])
        eye = sb("eye_f32", [128, 128])
        eye_b = sb("eye_bf16", [128, 128], BF16)
        ones = sb("ones_f32", [128, 128])
        half = sb("minus_half", [128, 1])
        eps = sb("eps", [128, 1])
        zero = sb("zero", [128, 1])
        gains = sb("gains", [128, 4])
        tanh_g = sb("tanh_g", [128, 4])
        wq = [sb(f"wq{l}", [128, 128]) for l in range(2)]
        wkv = [sb(f"wkv{l}", [128, 256]) for l in range(2)]
        wo = [sb(f"wo{l}", [128, 128]) for l in range(2)]
        bqk = sb("bqk", [128, 256])
        bv_col = sb("bv_col", [128, 1])
        bv_rep = sb("bv_rep", [128, 128])
        bo_row = sb("bo_row", [128, 128])
        bias_out = sb("bias_out", [128, 128])
        mask = sb("mask", [128, 128])
        maskT = sb("maskT", [128, 128])
        mask_rest = sb("mask_rest", [128, 128])
        mask_parts = sb("mask_parts", [128, 3, 128], BF16)
        sel_ind = sb("sel_ind", [128, HEADS])
        sel = sb("sel", [128, HEADS, 128], BF16)
        ctx_in = sb("ctx_in", [128, 2, D])
        stats = sb("stats", [128, 2, 6])
        mean_var = sb("mean_var", [128, 2, 2])
        var_eps = sb("var_eps", [128, 2, 1])
        rstd = sb("rstd", [128, 2, 1])
        neg_mean = sb("neg_mean", [128, 2, 1])
        shift = sb("shift", [128, 2, 1])
        xn = sb("xn", [128, 2, D])
        xcT = sb("xcT", [128, 2, 256])
        qk = sb("qk", [128, 2, 256])
        qk_rest = sb("qk_rest", [128, 2, 256])
        stack = sb("stack", [128, 2, 2, HEADS, SLOTS * HD], BF16)
        qT = sb("qT", [128, 2, HEADS // 2, 128], BF16)
        kT = sb("kT", [128, 2, HEADS // 2, 128], BF16)
        v_one = sb("v_one", [128, 2, HEADS, V_COLS])
        neg_max = sb("neg_max", [128, 2, HEADS])
        neg_rest = sb("neg_rest", [128, 2, HEADS])
        neg_parts = sb("neg_parts", [128, 2, 2, 4, HEADS], BF16)
        mT = sb("mT", [128, 2, 128], BF16)
        masked = sb("masked", [128, UNITS, 2, UH // 2, 128])
        probs = sb("probs", [128, UNITS, 2, UH // 2, 128])
        o_raw = sb("o_raw", [128, 512])
        o_rden = sb("o_rden", [128, HEADS])
        o_norm = sb("o_norm", [128, 128])
        o_normT = sb("o_normT", [128, 128])

        w12 = sb("w12", [128, EXPERTS, TWO_H])
        w3 = sb("w3", [128, EXPERTS, H_TILES, D])
        gate_w = sb("gate_w", [128, EXPERTS])
        before = sb("before", [128, EXPERTS, EXPERTS])
        stats2 = sb("stats2", [128, 2, 6])
        mean_var2 = sb("mean_var2", [128, 2, 2])
        var_eps2 = sb("var_eps2", [128, 2, 1])
        rstd2 = sb("rstd2", [128, 2, 1])
        neg_mean2 = sb("neg_mean2", [128, 2, 1])
        shift2 = sb("shift2", [128, 2, 1])
        xn2 = sb("xn2", [128, 2, D])
        xnT_ring = sb("xnT_ring", [128, 2, 128])
        xnT_all = sb("xnT_all", [128, BATCHES, 128])
        scores = sb("scores", [128, BATCHES, EXPERTS])
        top = sb("top", [128, BATCHES])
        greater = sb("greater", [128, BATCHES, EXPERTS, EXPERTS])
        at_least = sb("at_least", [128, BATCHES, EXPERTS, EXPERTS])
        rank = sb("rank", [128, BATCHES, EXPERTS])
        chosen = sb("chosen", [128, BATCHES, EXPERTS])
        midway = sb("midway", [128, BATCHES])
        weight = sb("weight", [128, BATCHES, EXPERTS])
        silu = sb("silu", [128, 2, GROUP * 128])
        hidden = sb("hidden", [128, 2, H_TILES, GROUP * 128])
        w_gu = sb("w_gu", [128, 2, INNER])
        w_dn = sb("w_dn", [128, I_TILES, D])
        w_abs = sb("w_abs", [128, 2 * INNER])
        w_sums = sb("w_sums", [128, 3])
        w_mean = sb("w_mean", [128, 3])
        w_scale = sb("w_scale", [128, 3])
        w_inv = sb("w_inv", [128, 3])
        w_factor = sb("w_factor", [128, 3])
        half_gain = sb("half_gain", [128, 1])
        w_back = sb("w_back", [128, 3])
        wq_gu = sb("wq_gu", [128, 2, INNER], BF16)
        wq_dn = sb("wq_dn", [128, I_TILES, D], BF16)
        top_x = sb("top_x", [128, 2, 1])
        clip_x = sb("clip_x", [128, 2, 1])
        scale_x = sb("scale_x", [128, 2, 1])
        back_x = sb("back_x", [128, 2, 2])
        back_gu = sb("back_gu", [128, 2, 1])
        top_h = sb("top_h", [128, 2, 1])
        clip_h = sb("clip_h", [128, 2, 1])
        scale_h = sb("scale_h", [128, 2, 1])
        back_h = sb("back_h", [128, 2, 1])
        x_round = sb("x_round", [128, D])
        xq = sb("xq", [128, 2, D], BF16)
        xqT = sb("xqT", [128, 2, 128], BF16)
        gate = sb("gate", [128, 2, INNER])
        gated = sb("gated", [128, INNER])
        h = sb("h", [128, 2, INNER])
        h_round = sb("h_round", [128, INNER])
        hq = sb("hq", [128, INNER], BF16)
        hqT = sb("hqT", [128, I_TILES, 128], BF16)

        ps_max = ctx.enter_context(nc.psum_tensor("ps_max", [128, 2, UH // 2, 128], F32))
        ps_exp = ctx.enter_context(nc.psum_tensor("ps_exp", [128, 2, UH // 2, 128], F32))
        ps_q = ctx.enter_context(nc.psum_tensor("ps_q", [128, 512], F32))
        ps_k = ctx.enter_context(nc.psum_tensor("ps_k", [128, 512], F32))
        ps_in = ctx.enter_context(nc.psum_tensor("ps_in", [128, 512], F32))
        ps_out = ctx.enter_context(nc.psum_tensor("ps_out", [128, 512], F32))
        ps_h1 = [ps_max[:, u, :, :].rearrange("p g k -> p (g k)") for u in range(2)]
        ps_h2 = [ps_exp[:, u, :, :].rearrange("p g k -> p (g k)") for u in range(2)]
        ps_expert = [ps_q, ps_k]
        ps_gate, ps_up = ps_q, ps_k
        ps_in_b = ps_in[:, :].bitcast(BF16).rearrange("p (h t) -> p h t", h=HEADS // 2)
        ps_q_b = ps_q[:, :].bitcast(BF16).rearrange("p (h t) -> p h t", h=HEADS // 2)
        ps_k_b = ps_k[:, :].bitcast(BF16).rearrange("p (h t) -> p h t", h=HEADS // 2)

        x_loaded, consts_loaded, ffn_loaded, out_stored = (
            sem("x_loaded"), sem("consts_loaded"), sem("ffn_loaded"), sem("out_stored"))
        ctx_loaded = [sem(f"ctx_loaded{r}") for r in range(2)]
        dve_setup, act_setup, pool_setup, pe_setup = sem("dve_setup"), sem("act_setup"), sem("pool_setup"), sem("pe_setup")
        mask_split = sem("mask_split")
        stats_done, aggr_done, eps_done, rstd_done, shift_done, xn_done = (
            sem("stats_done"), sem("aggr_done"), sem("eps_done"), sem("rstd_done"), sem("shift_done"), sem("xn_done"))
        xc_turned, xcT_done, qk_made, qk_done, v_made, v_done = (
            sem("xc_turned"), sem("xcT_done"), sem("qk_made"), sem("qk_done"), sem("v_made"), sem("v_done"))
        hi_done, rest_done, mid_done, lo_done, stack_done = (
            sem("hi_done"), sem("rest_done"), sem("mid_done"), sem("lo_done"), sem("stack_done"))
        k_turned, q_turned, kT_done, qT_done = sem("k_turned"), sem("q_turned"), sem("kT_done"), sem("qT_done")
        unit = lambda name: [sem(f"{name}{u}") for u in range(UNITS)]
        max_scores, max_done, exp_scores, masked_done, exp_done, pv_made = (
            unit("max_scores"), unit("max_done"), unit("exp_scores"), unit("masked_done"), unit("exp_done"),
            unit("pv_made"))
        n0_done, n0_rest, n1_done, neg_done, m_turned, mT_done = (
            sem("n0_done"), sem("n0_rest"), sem("n1_done"), sem("neg_done"), sem("m_turned"), sem("mT_done"))
        o_done, o_turned, rden_done, norm_done, norm_turned, normT_done = (
            sem("o_done"), sem("o_turned"), sem("rden_done"), sem("norm_done"), sem("norm_turned"), sem("normT_done"))
        attn_made, bias_added, attn_done = sem("attn_made"), sem("bias_added"), sem("attn_done")
        stats2_done, aggr2_done, eps2_done, rstd2_done, shift2_done, xn2_done = (
            sem("stats2_done"), sem("aggr2_done"), sem("eps2_done"), sem("rstd2_done"), sem("shift2_done"), sem("xn2_done"))
        xn_turned, ring_done, all_done, gate_made, score_done = (
            sem("xn_turned"), sem("ring_done"), sem("all_done"), sem("gate_made"), sem("score_done"))
        route_dve, route_tanh_done, gains_done = sem("route_dve"), sem("route_tanh_done"), sem("gains_done")
        h1_made, h2_made, silu_done, hidden_done, expert_made, expert_added = (
            sem("h1_made"), sem("h2_made"), sem("silu_done"), sem("hidden_done"), sem("expert_made"), sem("expert_added"))
        w_summed, w_totalled, w_scaled, w_quantised = (
            sem("w_summed"), sem("w_totalled"), sem("w_scaled"), sem("w_quantised"))
        top_x_done, clip_x_done, recip_x_done, scale_x_done, back_x_done, back_gu_done = (
            sem("top_x_done"), sem("clip_x_done"), sem("recip_x_done"), sem("scale_x_done"), sem("back_x_done"),
            sem("back_gu_done"))
        x_rounded, xq_done, xq_turned, xqT_done, gu_made, gate_done, gated_done, h_done = (
            sem("x_rounded"), sem("xq_done"), sem("xq_turned"), sem("xqT_done"), sem("gu_made"), sem("gate_done"),
            sem("gated_done"), sem("h_done"))
        top_h_done, clip_h_done, recip_h_done, scale_h_done, back_h_done = (
            sem("top_h_done"), sem("clip_h_done"), sem("recip_h_done"), sem("scale_h_done"), sem("back_h_done"))
        h_rounded, hq_done, hq_turned, hqT_done, down_made, ffn_done = (
            sem("h_rounded"), sem("hq_done"), sem("hq_turned"), sem("hqT_done"), sem("down_made"), sem("ffn_done"))

        LAST = BATCHES - 1

        def pipeline(eng, layer, depth, step):
            def one(i, odd, live):
                step(i, live, lambda l: (i - l, i - l + BATCHES * layer, (odd + l) % 2))

            first = (depth + 3) // 2 * 2
            after = first + (BATCHES - first) // 2 * 2
            for i in range(first):
                one(i, i % 2, lambda l: 0 <= i - l <= LAST)
            with eng.Fori(first, after - 1, 2) as j:
                for u in range(2):
                    one(j + u, u, lambda l: True)
            for i in range(after, LAST + depth + 1):
                one(i, i % 2, lambda l: 0 <= i - l <= LAST)

        def latest(eng, *reads):
            for exists, semaphore, count in reads:
                if exists:
                    need(eng, semaphore, count)
                    return

        block = ctx.enter_context(nc.Block())

        const_loads = [
            (eye[:, :], t["eye"]), (mask[:, :], t["mask"]), (maskT[:, :], t["maskT"]),
            (gains[:, 0:2], t["g_xattn"].partition_broadcast(128)),
            (gains[:, 2:4], t["g_ffn"].partition_broadcast(128)),
            (wq[0][:, :], t["Wq0"]), (wkv[0][:, 0:128], t["Wk0"]), (wkv[0][:, 128:256], t["Wv0"]),
            (wo[0][:, :], t["Wo0"]),
            (bqk[:, 0:128], t["bq"].partition_broadcast(128)), (bqk[:, 128:256], t["bk"].partition_broadcast(128)),
            (bv_col[:, :], t["bv"].rearrange("(p o) -> p o", o=1)), (bo_row[:, :], t["bo"].partition_broadcast(128)),
            (wq[1][:, :], t["Wq1"]), (wkv[1][:, 0:128], t["Wk1"]), (wkv[1][:, 128:256], t["Wv1"]),
            (wo[1][:, :], t["Wo1"]),
        ]
        ffn_loads = [
            (gate_w[:, :], t["gateT"]),
            (before[:, :, :].rearrange("p a b -> p (a b)"), t["before"].rearrange("a b -> (a b)").partition_broadcast(128)),
            (w12[:, :, :], t["w12T"]), (w3[:, :, :, :], t["w3T"].rearrange("(k p) e d -> p e k d", k=H_TILES)),
            (w_gu[:, 0, :], t["w_gateT"]), (w_gu[:, 1, :], t["w_upT"]),
            (w_dn[:, :, :], t["w_downT"].rearrange("(k p) d -> p k d", k=I_TILES)),
        ]
        CONSTS = 16 * len(const_loads)
        FFN_CONSTS = 16 * len(ffn_loads)
        ROUTE_PARTS, ROUTE_STEPS = 7, 11
        DEPTHS = (5, 6)
        SETUP_BIAS, SETUP_ALL = 9, 12
        MASK_STEPS = 4

        @block.sync
        def _(sp):
            sp.dma_start(x_all[:, :, :], t["x"].rearrange("b s d -> s b d")).then_inc(x_loaded, 16)
            for dst, src in const_loads:
                sp.dma_start(dst, src).then_inc(consts_loaded, 16)

            for dst, src in ffn_loads:
                sp.dma_start(dst, src).then_inc(ffn_loaded, 16)

            def load_contexts(layer):
                def step(i, r, live):
                    n = i + BATCHES * layer
                    if live(0):
                        need(sp, xc_turned, n - 1)
                        sp.dma_start(ctx_in[:, r, :], t["ctx"][i, :, :]).then_inc(ctx_loaded[r], 16)

                for i in range(2):
                    step(i, i % 2, lambda d: True)
                with sp.Fori(2, LAST, 2) as j:
                    for u in range(2):
                        step(j + u, u, lambda d: True)

            load_contexts(0)
            load_contexts(1)
            with sp.Fori(0, BATCHES, 1) as b:
                sp.wait_ge(ffn_done, b + 1)
                sp.dma_start(t["out"][b, :, :], x_all[:, b, :]).then_inc(out_stored, 16)
            sp.wait_ge(out_stored, 16 * BATCHES)

        @block.gpsimd
        def _(pool):
            nc.gpsimd.memset(half[:, :], -0.5).then_inc(pool_setup, 1)
            nc.gpsimd.memset(eps[:, :], EPS).then_inc(pool_setup, 1)
            nc.gpsimd.memset(zero[:, :], 0.0).then_inc(pool_setup, 1)
            nc.gpsimd.memset(ones[:, :], 1.0).then_inc(pool_setup, 1)
            nc.gpsimd.memset(stack[:, :, :, :, :], 0.0).then_inc(pool_setup, 1)
            nc.gpsimd.memset(neg_parts[:, :, :, :, :], 0.0).then_inc(pool_setup, 1)
            nc.gpsimd.memset(v_one[:, :, :, :], 0.0).then_inc(pool_setup, 1)
            pool.wait_ge(pool_setup, 7)
            for r in range(2):
                nc.gpsimd.memset(v_one[:, r, :, HD:HD + 1], 1.0).then_inc(pool_setup, 1)

            def layer_steps(layer):
                def add_eps(b, m, r):
                    pool.wait_ge(aggr_done, m + 1)
                    need(pool, rstd_done, m - 1)
                    nc.gpsimd.tensor_tensor(var_eps[:, r, :], mean_var[:, r, 1:2], eps[:, :], ALU.add).then_inc(eps_done, 1)
                    if layer == 1:
                        nc.gpsimd.tensor_tensor(neg_mean[:, r, :], zero[:, :], mean_var[:, r, 0:1],
                                                ALU.subtract).then_inc(shift_done, 1)

                def inverse_deviation(b, m, r):
                    pool.wait_ge(eps_done, m + 1)
                    need(pool, xn_done, m - 1)
                    nc.gpsimd.tensor_tensor(rstd[:, r, :], var_eps[:, r, :], half[:, :], ALU.pow).then_inc(rstd_done, 1)
                    if layer == 1:
                        pool.wait_ge(rstd_done, m + 1)
                        pool.wait_ge(shift_done, 2 * b + 1)
                        nc.gpsimd.tensor_tensor(shift[:, r, :], neg_mean[:, r, :], rstd[:, r, :],
                                                ALU.mult).then_inc(shift_done, 1)

                def add_eps2(b, m, r):
                    pool.wait_ge(aggr2_done, m + 1)
                    need(pool, rstd2_done, m - 1)
                    nc.gpsimd.tensor_tensor(var_eps2[:, r, :], mean_var2[:, r, 1:2], eps[:, :], ALU.add).then_inc(eps2_done, 1)
                    if layer == 1:
                        nc.gpsimd.tensor_tensor(neg_mean2[:, r, :], zero[:, :], mean_var2[:, r, 0:1],
                                                ALU.subtract).then_inc(shift2_done, 1)

                def inverse_deviation2(b, m, r):
                    pool.wait_ge(eps2_done, m + 1)
                    need(pool, xn2_done, m - 1)
                    nc.gpsimd.tensor_tensor(rstd2[:, r, :], var_eps2[:, r, :], half[:, :], ALU.pow).then_inc(rstd2_done, 1)
                    if layer == 1:
                        pool.wait_ge(rstd2_done, m + 1)
                        pool.wait_ge(shift2_done, 2 * b + 1)
                        nc.gpsimd.tensor_tensor(shift2[:, r, :], neg_mean2[:, r, :], rstd2[:, r, :],
                                                ALU.mult).then_inc(shift2_done, 1)

                def add_bias(b, m, r):
                    pool.wait_ge(xn_done, m + 1)
                    if isinstance(b, int) and b == 0:
                        pool.wait_ge(dve_setup, SETUP_BIAS)
                    nc.gpsimd.tensor_tensor(x_all[:, b, :], x_all[:, b, :], bias_out[:, :], ALU.add).then_inc(bias_added, 1)

                def repeat_parts(b, m, r):
                    pool.wait_ge(lo_done, m + 1)
                    q, k = stack[:, r, 0, :, :], stack[:, r, 1, :, :]
                    pair = lambda a, c: a[:, :, c * HD:(c + 2) * HD]
                    nc.gpsimd.tensor_tensor(pair(q, 5), pair(q, 1),
                                            zero[:, :].unsqueeze(2).broadcast_to([128, HEADS, 2 * HD]),
                                            ALU.add).then_inc(stack_done, 1)
                    nc.gpsimd.tensor_scalar(pair(k, 3), pair(k, 1), 1.0, 0.0, ALU.mult, ALU.add).then_inc(stack_done, 1)
                    for a, c in ((q, 3), (k, 5)):
                        dst = pair(a, c).rearrange("p h (c d) -> p h c d", c=2)
                        src = a[:, :, 0:HD].unsqueeze(2).broadcast_to([128, HEADS, 2, HD])
                        nc.gpsimd.tensor_scalar(dst, src, 1.0, 0.0, ALU.mult, ALU.add).then_inc(stack_done, 1)

                def gather_xn(b, m, r):
                    pool.wait_ge(ring_done, b + 1)
                    nc.gpsimd.tensor_copy(xnT_all[:, b, :], xnT_ring[:, r, :]).then_inc(all_done, 1)

                def round_x(b, m, r):
                    pool.wait_ge(scale_x_done, b + 1)
                    need(pool, gate_done, b - 1)
                    need(pool, back_gu_done, b - 1)
                    need(pool, xq_done, b)
                    nc.gpsimd.tensor_tensor(back_x[:, r, :], clip_x[:, r, :].broadcast_to([128, 2]), w_back[:, 0:2],
                                            ALU.mult).then_inc(back_x_done, 1)
                    nc.gpsimd.tensor_scalar(x_round[:, :], xn2[:, r, :], scale_x[:, r, :], MAGIC, ALU.mult, ALU.add).then_inc(x_rounded, 1)
                    pool.wait_ge(back_x_done, b + 1)
                    need(pool, h_done, b - 1)
                    nc.gpsimd.tensor_tensor(back_gu[:, r, :], back_x[:, r, 0:1], back_x[:, r, 1:2],
                                            ALU.mult).then_inc(back_gu_done, 1)

                def round_h(b, m, r):
                    pool.wait_ge(scale_h_done, b + 1)
                    need(pool, ffn_done, b - 1)
                    need(pool, hq_done, b)
                    nc.gpsimd.tensor_tensor(back_h[:, r, :], clip_h[:, r, :], w_back[:, 2:3], ALU.mult).then_inc(back_h_done, 1)
                    nc.gpsimd.tensor_scalar(h_round[:, :], h[:, r, :], scale_h[:, r, :], MAGIC, ALU.mult, ALU.add).then_inc(h_rounded, 1)

                def first_layer(i, live, at):
                    if live(5):
                        add_eps2(*at(5))
                        inverse_deviation2(*at(5))
                    if live(0):
                        add_eps(*at(0))
                        inverse_deviation(*at(0))
                    if live(1):
                        repeat_parts(*at(1))
                    if live(0):
                        add_bias(*at(0))
                    if live(5):
                        gather_xn(*at(5))

                def second_layer(i, live, at):
                    if live(6):
                        round_h(*at(6))
                    if live(0):
                        add_eps(*at(0))
                        inverse_deviation(*at(0))
                    if live(1):
                        repeat_parts(*at(1))
                    if live(4):
                        add_eps2(*at(4))
                        inverse_deviation2(*at(4))
                        round_x(*at(4))
                pipeline(pool, layer, DEPTHS[layer], second_layer if layer else first_layer)

            def quantise_weights():
                pool.wait_ge(w_scaled, 5)
                for m, (w, out) in enumerate(((w_gu[:, 0, :], wq_gu[:, 0, :]), (w_gu[:, 1, :], wq_gu[:, 1, :]),
                                              (w_dn[:, :, :], wq_dn[:, :, :]))):
                    nc.gpsimd.tensor_scalar(w, w, w_scale[:, m:m + 1], MAGIC, ALU.mult, ALU.add).then_inc(w_quantised, 1)
                    pool.wait_ge(w_quantised, 3 * m + 1)
                    nc.gpsimd.tensor_scalar(w, w, -MAGIC, 1.0, ALU.add, ALU.min).then_inc(w_quantised, 1)
                    pool.wait_ge(w_quantised, 3 * m + 2)
                    nc.gpsimd.tensor_scalar(out, w, -1.0, 1.0, ALU.max, ALU.mult).then_inc(w_quantised, 1)

            layer_steps(0)
            quantise_weights()
            layer_steps(1)

        @block.vector
        def _(dve):
            scale = float(HD) ** -0.5
            dve.wait_ge(consts_loaded, CONSTS)
            nc.vector.tensor_copy(eye_b[:, :], eye[:, :]).then_inc(dve_setup, 1)
            nc.vector.tensor_scalar(wq[0][:, :], wq[0][:, :], scale, None, ALU.mult).then_inc(dve_setup, 1)
            nc.vector.tensor_scalar(wq[1][:, :], wq[1][:, :], scale, None, ALU.mult).then_inc(dve_setup, 1)
            nc.vector.tensor_scalar(bqk[:, 0:128], bqk[:, 0:128], scale, None, ALU.mult).then_inc(dve_setup, 1)
            nc.vector.tensor_reduce(sel_ind[:, :], eye[:, :].rearrange("p (a c h) -> p h a c", a=2, c=4)[:, :, :, 0:3],
                                    AX.XY, ALU.add).then_inc(dve_setup, 1)
            dve.wait_ge(pool_setup, 9)
            nc.vector.tensor_scalar(bv_rep[:, :], ones[:, :], bv_col[:, 0:1], None, ALU.mult).then_inc(dve_setup, 1)
            dve.wait_ge(dve_setup, 5)
            nc.vector.tensor_copy(sel[:, :, :], sel_ind[:, :].unsqueeze(2).broadcast_to([128, HEADS, 128])).then_inc(dve_setup, 1)
            dve.wait_ge(pe_setup, 1)
            nc.vector.tensor_tensor(bias_out[:, :], ps_in[:, 0:128], bo_row[:, :], ALU.add).then_inc(dve_setup, 1)
            dve.wait_ge(dve_setup, 8)
            dve.wait_ge(act_setup, 1)
            nc.vector.tensor_scalar(bias_out[:, :], bias_out[:, :], tanh_g[:, 0:1], None, ALU.mult).then_inc(dve_setup, 1)
            nc.vector.tensor_scalar(wo[0][:, :], wo[0][:, :], tanh_g[:, 0:1], None, ALU.mult).then_inc(dve_setup, 1)
            nc.vector.tensor_scalar(wo[1][:, :], wo[1][:, :], tanh_g[:, 1:2], None, ALU.mult).then_inc(dve_setup, 1)
            nc.vector.tensor_scalar(half_gain[:, :], tanh_g[:, 2:3], 0.5, None, ALU.mult).then_inc(dve_setup, 1)
            dve.wait_ge(x_loaded, 16)

            def layer_steps(layer):
                def statistics(b, m, r):
                    nc.vector.bn_stats(stats[:, r, :], x_all[:, b, :]).then_inc(stats_done, 1)

                def statistics_ready(b, m, r):
                    dve.wait_ge(stats_done, m + 1)
                    need(dve, xn_done, m - 1)

                def mean_and_variance(b, m, r):
                    nc.vector.bn_aggr(mean_var[:, r, :], stats[:, r, :]).then_inc(aggr_done, 1)

                def normalise(b, m, r):
                    dve.wait_ge(rstd_done, m + 1)
                    need(dve, xc_turned, m - 1)
                    nc.vector.tensor_scalar(xn[:, r, :], x_all[:, b, :], mean_var[:, r, 0:1], rstd[:, r, :],
                                            ALU.subtract, ALU.mult).then_inc(xn_done, 1)

                heads = lambda a, r: a[:, r, :].rearrange("p (w h d) -> p w h d", w=2, h=HEADS)
                slot = lambda r, c: stack[:, r, :, :, c * HD:(c + 1) * HD]

                def keep_qk(b, m, r):
                    dve.wait_ge(qk_made, m + 1)
                    need(dve, rest_done, m - 1)
                    nc.vector.tensor_tensor(qk[:, r, :], ps_in[:, 0:256], bqk[:, :], ALU.add).then_inc(qk_done, 1)

                def split_hi(b, m, r):
                    dve.wait_ge(qk_done, m + 1)
                    need(dve, q_turned, m - 1)
                    need(dve, k_turned, m - 1)
                    nc.vector.tensor_copy(slot(r, 0), heads(qk, r)).then_inc(hi_done, 1)

                def split_rest(b, m, r):
                    dve.wait_ge(hi_done, m + 1)
                    need(dve, lo_done, m - 1)
                    nc.vector.tensor_tensor(heads(qk_rest, r), heads(qk, r), slot(r, 0), ALU.subtract).then_inc(rest_done, 1)

                def split_mid(b, m, r):
                    dve.wait_ge(rest_done, m + 1)
                    nc.vector.tensor_copy(slot(r, 1), heads(qk_rest, r)).then_inc(mid_done, 1)

                def split_lo(b, m, r):
                    dve.wait_ge(mid_done, m + 1)
                    nc.vector.tensor_tensor(slot(r, 2), heads(qk_rest, r), slot(r, 1), ALU.subtract).then_inc(lo_done, 1)

                def row_max(b, m, r, u):
                    dve.wait_ge(max_scores[u], m + 1)
                    need(dve, n0_rest, m - 1)
                    out = neg_max[:, r, UH * u:UH * u + UH].rearrange("p (g j) -> p j g", j=2)
                    nc.vector.tensor_reduce(out, ps_max[:, :, :, :], AX.X, ALU.max, negate=True).then_inc(max_done[u], 1)

                part = lambda r, c: neg_parts[:, r, :, c, :]
                twice = lambda a: a.unsqueeze(1).broadcast_to([128, 2, HEADS])

                def max_hi(b, m, r):
                    dve.wait_ge(max_done[0], m + 1)
                    dve.wait_ge(max_done[1], m + 1)
                    need(dve, m_turned, m - 1)
                    nc.vector.tensor_copy(part(r, 0), twice(neg_max[:, r, :])).then_inc(n0_done, 1)

                def max_rest(b, m, r):
                    dve.wait_ge(n0_done, m + 1)
                    need(dve, neg_done, m - 1)
                    nc.vector.tensor_tensor(neg_rest[:, r, :], neg_max[:, r, :], neg_parts[:, r, 0, 0, :],
                                            ALU.subtract).then_inc(n0_rest, 1)

                def max_mid(b, m, r):
                    dve.wait_ge(n0_rest, m + 1)
                    nc.vector.tensor_copy(part(r, 1), twice(neg_rest[:, r, :])).then_inc(n1_done, 1)

                def max_lo(b, m, r):
                    dve.wait_ge(n1_done, m + 1)
                    nc.vector.tensor_tensor(part(r, 2), twice(neg_rest[:, r, :]), part(r, 1), ALU.subtract).then_inc(neg_done, 1)

                def add_mask(b, m, r, u):
                    dve.wait_ge(exp_scores[u], m + 1)
                    need(dve, exp_done[u], m)
                    for j in range(2):
                        last = nc.vector.tensor_tensor(masked[:, u, j, :, :], ps_exp[:, j, :, :],
                                                       maskT[:, :].unsqueeze(1).broadcast_to([128, UH // 2, 128]), ALU.add)
                    last.then_inc(masked_done[u], 1)

                o_heads = ps_out[:, :].rearrange("p (h c) -> p h c", h=HEADS)

                def invert_sums(b, m, r):
                    dve.wait_ge(o_turned, m + 1)
                    need(dve, norm_done, m)
                    nc.vector.reciprocal(o_rden[:, :], o_heads[:, :, HD]).then_inc(rden_done, 1)

                def divide(b, m, r):
                    dve.wait_ge(rden_done, m + 1)
                    need(dve, norm_turned, m)
                    nc.vector.tensor_tensor(o_norm[:, :].rearrange("p (h d) -> p h d", h=HEADS), o_heads[:, :, 0:HD],
                                            o_rden[:, :].unsqueeze(2).broadcast_to([128, HEADS, HD]),
                                            ALU.mult).then_inc(norm_done, 1)

                def add_attention(b, m, r):
                    dve.wait_ge(attn_made, m + 1)
                    if layer == 0:
                        dve.wait_ge(bias_added, m + 1)
                    nc.vector.tensor_tensor(x_all[:, b, :], ps_out[:, 128:256], x_all[:, b, :], ALU.add).then_inc(attn_done, 1)

                def attention_added(b, m, r):
                    dve.wait_ge(attn_done, m + 1)

                def statistics2(b, m, r):
                    nc.vector.bn_stats(stats2[:, r, :], x_all[:, b, :]).then_inc(stats2_done, 1)

                def statistics2_ready(b, m, r):
                    dve.wait_ge(stats2_done, m + 1)
                    need(dve, xn2_done, m - 1)

                def mean_and_variance2(b, m, r):
                    nc.vector.bn_aggr(mean_var2[:, r, :], stats2[:, r, :]).then_inc(aggr2_done, 1)

                def normalise2(b, m, r):
                    dve.wait_ge(rstd2_done, m + 1)
                    need(dve, xn_turned, b - 1)
                    nc.vector.tensor_scalar(xn2[:, r, :], x_all[:, b, :], mean_var2[:, r, 0:1], rstd2[:, r, :],
                                            ALU.subtract, ALU.mult).then_inc(xn2_done, 1)

                def top_of_x(b, m, r):
                    dve.wait_ge(xn2_done, m + 1)
                    need(dve, clip_x_done, b - 1)
                    nc.vector.tensor_reduce(top_x[:, r, :], xn2[:, r, :], AX.X, ALU.max, apply_absolute_value=True).then_inc(top_x_done, 1)

                def clip_x_top(b, m, r):
                    dve.wait_ge(top_x_done, b + 1)
                    need(dve, back_x_done, b - 1)
                    need(dve, recip_x_done, b - 1)
                    nc.vector.tensor_scalar(clip_x[:, r, :], top_x[:, r, :], 1e-5, None, ALU.max).then_inc(clip_x_done, 1)

                def invert_x_top(b, m, r):
                    dve.wait_ge(clip_x_done, b + 1)
                    need(dve, x_rounded, b - 1)
                    nc.vector.reciprocal(scale_x[:, r, :], clip_x[:, r, :]).then_inc(recip_x_done, 1)

                def x_scale(b, m, r):
                    dve.wait_ge(recip_x_done, b + 1)
                    nc.vector.tensor_scalar(scale_x[:, r, :], scale_x[:, r, :], 127.0, None, ALU.mult).then_inc(scale_x_done, 1)

                def clip_x_quantised(b, m, r):
                    dve.wait_ge(x_rounded, b + 1)
                    need(dve, xq_turned, b - 1)
                    nc.vector.tensor_scalar(xq[:, r, :], x_round[:, :], MAGIC, 127.0, ALU.subtract, ALU.min).then_inc(xq_done, 1)

                def times_gate(b, m, r):
                    dve.wait_ge(gate_done, b + 1)
                    need(dve, h_done, b)
                    nc.vector.scalar_tensor_tensor(gated[:, :], gate[:, r, :], 1.0, ps_gate[:, :], ALU.add, ALU.mult).then_inc(gated_done, 1)

                def times_up(b, m, r):
                    dve.wait_ge(back_gu_done, b + 1)
                    dve.wait_ge(gated_done, b + 1)
                    need(dve, h_rounded, b - 1)
                    need(dve, top_h_done, b - 1)
                    nc.vector.scalar_tensor_tensor(h[:, r, :], ps_up[:, :], back_gu[:, r, :], gated[:, :],
                                                   ALU.mult, ALU.mult).then_inc(h_done, 1)

                def top_of_h(b, m, r):
                    dve.wait_ge(h_done, b + 1)
                    need(dve, clip_h_done, b - 1)
                    nc.vector.tensor_reduce(top_h[:, r, :], h[:, r, :], AX.X, ALU.max, apply_absolute_value=True).then_inc(top_h_done, 1)

                def clip_h_top(b, m, r):
                    dve.wait_ge(top_h_done, b + 1)
                    need(dve, back_h_done, b - 1)
                    need(dve, recip_h_done, b - 1)
                    nc.vector.tensor_scalar(clip_h[:, r, :], top_h[:, r, :], 1e-5, None, ALU.max).then_inc(clip_h_done, 1)

                def invert_h_top(b, m, r):
                    dve.wait_ge(clip_h_done, b + 1)
                    need(dve, h_rounded, b - 1)
                    nc.vector.reciprocal(scale_h[:, r, :], clip_h[:, r, :]).then_inc(recip_h_done, 1)

                def h_scale(b, m, r):
                    dve.wait_ge(recip_h_done, b + 1)
                    nc.vector.tensor_scalar(scale_h[:, r, :], scale_h[:, r, :], 127.0, None, ALU.mult).then_inc(scale_h_done, 1)

                def clip_h_quantised(b, m, r):
                    dve.wait_ge(h_rounded, b + 1)
                    need(dve, hq_turned, b)
                    nc.vector.tensor_scalar(hq[:, :], h_round[:, :], MAGIC, 127.0, ALU.subtract, ALU.min).then_inc(hq_done, 1)

                def add_feed_forward(b, m, r):
                    dve.wait_ge(down_made, b + 1)
                    dve.wait_ge(back_h_done, b + 1)
                    nc.vector.scalar_tensor_tensor(x_all[:, b, :], ps_in[:, 0:128], back_h[:, r, :], x_all[:, b, :],
                                                   ALU.mult, ALU.add).then_inc(ffn_done, 1)

                def first_layer(i, live, at):
                    if live(0):
                        statistics(*at(0))
                    if live(0):
                        statistics_ready(*at(0))
                    if live(1):
                        split_rest(*at(1))
                    if live(0):
                        mean_and_variance(*at(0))
                    if live(1):
                        split_mid(*at(1))
                    if live(5):
                        normalise2(*at(5))
                    if live(1):
                        split_lo(*at(1))
                    if live(4):
                        invert_sums(*at(4))
                        divide(*at(4))
                    if live(2):
                        row_max(*at(2), 0)
                    if live(0):
                        normalise(*at(0))
                    if live(4):
                        add_attention(*at(4))
                    if live(2):
                        row_max(*at(2), 1)
                        max_hi(*at(2))
                        max_rest(*at(2))
                        max_mid(*at(2))
                    if live(4):
                        attention_added(*at(4))
                    if live(2):
                        max_lo(*at(2))
                    if live(4):
                        statistics2(*at(4))
                    if live(4):
                        statistics2_ready(*at(4))
                    if live(0):
                        keep_qk(*at(0))
                    if live(4):
                        mean_and_variance2(*at(4))
                    if live(0):
                        split_hi(*at(0))

                def second_layer(i, live, at):
                    if live(0):
                        statistics(*at(0))
                    if live(0):
                        statistics_ready(*at(0))
                    if live(5):
                        clip_x_quantised(*at(5))
                    if live(0):
                        mean_and_variance(*at(0))
                    if live(4):
                        invert_sums(*at(4))
                    if live(1):
                        split_lo(*at(1))
                    if live(4):
                        divide(*at(4))
                    if live(6):
                        clip_h_quantised(*at(6))
                    if live(3):
                        add_mask(*at(3), 0)
                    if live(2):
                        row_max(*at(2), 0)
                    if live(4):
                        add_attention(*at(4))
                    if live(4):
                        attention_added(*at(4))
                    if live(5):
                        times_gate(*at(5))
                    if live(4):
                        statistics2(*at(4))
                    if live(4):
                        statistics2_ready(*at(4))
                    if live(3):
                        add_mask(*at(3), 1)
                    if live(4):
                        mean_and_variance2(*at(4))
                    if live(5):
                        times_up(*at(5))
                    if live(2):
                        row_max(*at(2), 1)
                    if live(5):
                        top_of_h(*at(5))
                    if live(4):
                        top_of_x(*at(4))
                    if live(2):
                        max_hi(*at(2))
                    if live(5):
                        clip_h_top(*at(5))
                    if live(4):
                        clip_x_top(*at(4))
                    if live(2):
                        max_rest(*at(2))
                    if live(5):
                        invert_h_top(*at(5))
                    if live(4):
                        invert_x_top(*at(4))
                    if live(2):
                        max_mid(*at(2))
                    if live(5):
                        h_scale(*at(5))
                    if live(4):
                        x_scale(*at(4))
                    if live(2):
                        max_lo(*at(2))
                    if live(0):
                        split_rest(*at(0))
                    if live(6):
                        add_feed_forward(*at(6))
                pipeline(dve, layer, DEPTHS[layer], second_layer if layer else first_layer)

            def route(part, lo, hi, done):
                size = hi - lo
                pairs = [128, size, EXPERTS, EXPERTS]
                sc, ch, w = scores[:, lo:hi, :], chosen[:, lo:hi, :], weight[:, lo:hi, :]
                gr, al = greater[:, lo:hi, :, :], at_least[:, lo:hi, :, :]
                other, this = sc.unsqueeze(2).broadcast_to(pairs), sc.unsqueeze(3).broadcast_to(pairs)
                lower = before[:, :, :].unsqueeze(1).broadcast_to(pairs)
                mid = midway[:, lo:hi].unsqueeze(2).broadcast_to([128, size, EXPERTS])
                if part == 0:
                    dve.wait_ge(ffn_loaded, FFN_CONSTS)
                    dve.wait_ge(score_done, hi)
                    nc.vector.tensor_tensor(gr, other, this, ALU.is_gt).then_inc(route_dve, 1)
                    nc.vector.tensor_tensor(al, other, this, ALU.is_ge).then_inc(route_dve, 1)
                if part == 1:
                    dve.wait_ge(route_dve, done + 2)
                    nc.vector.tensor_tensor(al, al, gr, ALU.subtract).then_inc(route_dve, 1)
                if part == 2:
                    dve.wait_ge(route_dve, done + 3)
                    nc.vector.tensor_tensor(al, al, lower, ALU.mult).then_inc(route_dve, 1)
                if part == 3:
                    dve.wait_ge(route_dve, done + 4)
                    nc.vector.tensor_tensor(gr, al, gr, ALU.add).then_inc(route_dve, 1)
                if part == 4:
                    dve.wait_ge(route_dve, done + 5)
                    nc.vector.tensor_reduce(rank[:, lo:hi, :], gr, AX.X, ALU.add).then_inc(route_dve, 1)
                if part == 5:
                    dve.wait_ge(route_dve, done + 6)
                    nc.vector.tensor_scalar(ch, rank[:, lo:hi, :], 2.0, None, ALU.is_lt).then_inc(route_dve, 1)
                    dve.wait_ge(route_dve, done + 7)
                    nc.vector.tensor_tensor(w, ch, sc, ALU.mult).then_inc(route_dve, 1)
                    dve.wait_ge(route_dve, done + 8)
                    nc.vector.tensor_reduce(midway[:, lo:hi], w, AX.X, ALU.add).then_inc(route_dve, 1)
                    dve.wait_ge(route_dve, done + 9)
                    nc.vector.scalar_tensor_tensor(w, mid, -0.5, sc, ALU.mult, ALU.add).then_inc(route_dve, 1)
                    nc.vector.tensor_scalar(ch, ch, half_gain[:, :], None, ALU.mult).then_inc(gains_done, 1)
                if part == 6:
                    dve.wait_ge(route_tanh_done, 1 if lo == 0 else 2)
                    dve.wait_ge(gains_done, 1 if lo == 0 else 2)
                    nc.vector.scalar_tensor_tensor(w, w, 1.0, ch, ALU.add, ALU.mult).then_inc(route_dve, 1)

            def add_expert(g, e):
                dve.wait_ge(expert_made, EXPERTS * g + e + 1)
                need(dve, expert_added, EXPERTS * g + e)
                for b in range(GROUP):
                    nc_b = GROUP * g + b
                    last = nc.vector.scalar_tensor_tensor(x_all[:, nc_b, :], ps_expert[e % 2][:, 128 * b:128 * (b + 1)],
                                                          weight[:, nc_b, e:e + 1], x_all[:, nc_b, :],
                                                          ALU.mult, ALU.add)
                last.then_inc(expert_added, 1)

            def experts():
                def group(g, first):
                    for e in range(EXPERTS):
                        if first and e < ROUTE_PARTS:
                            route(e, GROUP, BATCHES, ROUTE_STEPS)
                        for k in range(H_TILES):
                            m = (EXPERTS * g + e) * H_TILES + k
                            u = k % 2
                            dve.wait_ge(silu_done, m + 1)
                            dve.wait_ge(h2_made, m + 1)
                            nc.vector.tensor_tensor(hidden[:, e % 2, k, :], silu[:, u, :], ps_h2[u], ALU.mult).then_inc(hidden_done, 1)
                        if e:
                            add_expert(g, e - 1)
                        elif not first:
                            add_expert(g - 1, EXPERTS - 1)

                dve.wait_ge(route_dve, ROUTE_STEPS)
                group(0, True)
                dve.wait_ge(route_dve, 2 * ROUTE_STEPS)
                with dve.Fori(1, GROUPS, 1) as g:
                    group(g, False)
                add_expert(GROUPS - 1, EXPERTS - 1)
                dve.wait_ge(expert_added, EXPERTS * GROUPS)

            def add_expert(g, e):
                dve.wait_ge(expert_made, EXPERTS * g + e + 1)
                need(dve, expert_added, EXPERTS * g + e)
                for b in range(GROUP):
                    nc_b = GROUP * g + b
                    last = nc.vector.scalar_tensor_tensor(x_all[:, nc_b, :], ps_expert[e % 2][:, 128 * b:128 * (b + 1)],
                                                          weight[:, nc_b, e:e + 1], x_all[:, nc_b, :],
                                                          ALU.mult, ALU.add)
                last.then_inc(expert_added, 1)

            def split_mask():
                nc.vector.tensor_copy(mask_parts[:, 0, :], mask[:, :]).then_inc(mask_split, 1)
                dve.wait_ge(mask_split, 1)
                nc.vector.tensor_tensor(mask_rest[:, :], mask[:, :], mask_parts[:, 0, :], ALU.subtract).then_inc(mask_split, 1)
                dve.wait_ge(mask_split, 2)
                nc.vector.tensor_copy(mask_parts[:, 1, :], mask_rest[:, :]).then_inc(mask_split, 1)
                dve.wait_ge(mask_split, 3)
                nc.vector.tensor_tensor(mask_parts[:, 2, :], mask_rest[:, :], mask_parts[:, 1, :],
                                        ALU.subtract).then_inc(mask_split, 1)

            def experts():
                def group(g, first):
                    for e in range(EXPERTS):
                        if first and e < ROUTE_PARTS:
                            route(e, GROUP, BATCHES, ROUTE_STEPS)
                        if first and e == ROUTE_PARTS:
                            split_mask()
                        for k in range(H_TILES):
                            m = (EXPERTS * g + e) * H_TILES + k
                            u = k % 2
                            dve.wait_ge(silu_done, m + 1)
                            dve.wait_ge(h2_made, m + 1)
                            nc.vector.tensor_tensor(hidden[:, e % 2, k, :], silu[:, u, :], ps_h2[u], ALU.mult).then_inc(hidden_done, 1)
                        if e:
                            add_expert(g, e - 1)
                        elif not first:
                            add_expert(g - 1, EXPERTS - 1)

                dve.wait_ge(route_dve, ROUTE_STEPS)
                group(0, True)
                dve.wait_ge(route_dve, 2 * ROUTE_STEPS)
                with dve.Fori(1, GROUPS, 1) as g:
                    group(g, False)
                add_expert(GROUPS - 1, EXPERTS - 1)

            def weight_scales():
                dve.wait_ge(w_totalled, 1)
                nc.vector.tensor_scalar(w_mean[:, :], ps_in[:, 0:3], 1.0 / (INNER * D), 1e-5, ALU.mult, ALU.max).then_inc(w_scaled, 1)
                dve.wait_ge(w_scaled, 1)
                nc.vector.reciprocal(w_scale[:, :], w_mean[:, :]).then_inc(w_scaled, 1)
                dve.wait_ge(w_scaled, 2)
                nc.vector.reciprocal(w_inv[:, :], w_scale[:, :]).then_inc(w_scaled, 1)
                dve.wait_ge(w_scaled, 3)
                nc.vector.tensor_tensor(w_back[:, :], w_inv[:, :], w_factor[:, :], ALU.mult).then_inc(w_scaled, 1)
                dve.wait_ge(w_scaled, 4)
                nc.vector.tensor_scalar(w_back[:, :], w_back[:, :], 1.0 / 127.0, None, ALU.mult).then_inc(w_scaled, 1)

            nc.vector.memset(w_factor[:, 0:1], 0.5)
            nc.vector.memset(w_factor[:, 1:2], 1.0)
            nc.vector.tensor_copy(w_factor[:, 2:3], tanh_g[:, 3:4])
            layer_steps(0)
            for part in range(ROUTE_PARTS):
                route(part, 0, GROUP, 0)
            weight_scales()
            experts()
            dve.wait_ge(expert_added, EXPERTS * GROUPS)
            layer_steps(1)

        @block.scalar
        def _(act):
            act.wait_ge(consts_loaded, CONSTS)
            nc.scalar.activation(tanh_g[:, :], gains[:, :], ACT.Tanh).then_inc(act_setup, 1)
            act.wait_ge(pool_setup, 9)

            def layer_steps(layer):
                def normalise(b, m, r):
                    act.wait_ge(shift_done, 2 * b + 2)
                    need(act, xc_turned, m - 1)
                    nc.scalar.activation(xn[:, r, :], x_all[:, b, :], ACT.Identity, bias=shift[:, r, :],
                                         scale=rstd[:, r, :]).then_inc(xn_done, 1)

                def normalise2(b, m, r):
                    act.wait_ge(shift2_done, 2 * b + 2)
                    need(act, xq_turned, b - 1)
                    need(act, x_rounded, b - 1)
                    nc.scalar.activation(xn2[:, r, :], x_all[:, b, :], ACT.Identity, bias=shift2[:, r, :],
                                         scale=rstd2[:, r, :]).then_inc(xn2_done, 1)

                def keep_inputs(b, m, r):
                    act.wait_ge(xc_turned, m + 1)
                    need(act, v_made, m - 1)
                    need(act, qk_made, m - 1)
                    nc.scalar.activation(xcT[:, r, :], ps_in[:, 0:256], ACT.Copy).then_inc(xcT_done, 1)

                def keep_qk(b, m, r):
                    act.wait_ge(qk_made, m + 1)
                    need(act, rest_done, m - 1)
                    nc.scalar.activation(qk[:, r, :], ps_in[:, 0:256], ACT.Copy).then_inc(qk_done, 1)

                heads = lambda a, r: a[:, r, :].rearrange("p (w h d) -> p w h d", w=2, h=HEADS)
                slot = lambda r, c: stack[:, r, :, :, c * HD:(c + 1) * HD]

                def split_hi(b, m, r):
                    act.wait_ge(qk_done, m + 1)
                    need(act, q_turned, m - 1)
                    need(act, k_turned, m - 1)
                    nc.scalar.activation(slot(r, 0), heads(qk, r), ACT.Copy).then_inc(hi_done, 1)

                def split_mid(b, m, r):
                    act.wait_ge(rest_done, m + 1)
                    nc.scalar.activation(slot(r, 1), heads(qk_rest, r), ACT.Copy).then_inc(mid_done, 1)

                def keep_k(b, m, r):
                    act.wait_ge(k_turned, m + 1)
                    need(act, exp_scores[1], m - 1)
                    nc.scalar.activation(kT[:, r, :, :], ps_k_b, ACT.Copy).then_inc(kT_done, 1)

                def keep_q(b, m, r):
                    act.wait_ge(q_turned, m + 1)
                    need(act, exp_scores[1], m - 1)
                    nc.scalar.activation(qT[:, r, :, :], ps_q_b, ACT.Copy).then_inc(qT_done, 1)

                def keep_v(b, m, r):
                    act.wait_ge(v_made, m + 1)
                    need(act, pv_made[1], m - 1)
                    nc.scalar.activation(v_one[:, r, :, 0:HD], ps_in[:, 256:384].rearrange("p (h d) -> p h d", h=HEADS),
                                         ACT.Copy).then_inc(v_done, 1)

                def keep_max(b, m, r):
                    act.wait_ge(m_turned, m + 1)
                    need(act, exp_scores[1], m - 1)
                    nc.scalar.activation(mT[:, r, :], ps_k_b[:, 0, :], ACT.Copy).then_inc(mT_done, 1)

                def exponentials(b, m, r, u):
                    act.wait_ge(masked_done[u] if layer else exp_scores[u], (b if layer else m) + 1)
                    need(act, pv_made[u], m)
                    scored = masked[:, u, :, :, :] if layer else ps_exp[:, :, :, :]
                    nc.scalar.activation(probs[:, u, :, :, :], scored, ACT.Exp).then_inc(exp_done[u], 1)

                def keep_o(b, m, r):
                    act.wait_ge(pv_made[0], m + 1)
                    act.wait_ge(pv_made[1], m + 1)
                    need(act, o_turned, m)
                    nc.scalar.activation(o_raw[:, :], ps_out[:, :], ACT.Copy).then_inc(o_done, 1)

                def keep_normed(b, m, r):
                    act.wait_ge(norm_turned, m + 1)
                    need(act, attn_made, m)
                    nc.scalar.activation(o_normT[:, :], ps_out[:, 0:128], ACT.Copy).then_inc(normT_done, 1)

                def keep_xn(b, m, r):
                    act.wait_ge(xn_turned, b + 1)
                    need(act, all_done, b - 1)
                    need(act, gate_made, b - 1)
                    nc.scalar.activation(xnT_ring[:, r, :], ps_in[:, 0:128], ACT.Copy).then_inc(ring_done, 1)

                def keep_scores(b, m, r):
                    act.wait_ge(gate_made, b + 1)
                    nc.scalar.activation(scores[:, b, :], ps_in[:, 0:EXPERTS], ACT.Copy).then_inc(score_done, 1)

                def keep_x_quantised(b, m, r):
                    act.wait_ge(xq_turned, b + 1)
                    need(act, gu_made, b - 1)
                    nc.scalar.activation(xqT[:, r, :], ps_in_b[:, 0, :], ACT.Copy).then_inc(xqT_done, 1)

                def gate_tanh(b, m, r):
                    act.wait_ge(back_x_done, b + 1)
                    act.wait_ge(gu_made, b + 1)
                    need(act, gated_done, b - 1)
                    nc.scalar.activation(gate[:, r, :], ps_gate[:, :], ACT.Tanh, scale=back_x[:, r, 0:1]).then_inc(gate_done, 1)

                def keep_h(b, m, r):
                    act.wait_ge(hq_turned, b + 1)
                    need(act, down_made, b)
                    nc.scalar.activation(hqT[:, :, :], ps_in_b[:, 0:I_TILES, :], ACT.Copy).then_inc(hqT_done, 1)

                def first_layer(i, live, at):
                    if live(4):
                        keep_o(*at(4))
                    if live(3):
                        keep_max(*at(3))
                    if live(2):
                        keep_q(*at(2))
                        keep_v(*at(2))
                    if live(3):
                        exponentials(*at(3), 0)
                    if live(5):
                        keep_xn(*at(5))
                    if live(4):
                        keep_normed(*at(4))
                    if live(5):
                        keep_scores(*at(5))
                    if live(3):
                        exponentials(*at(3), 1)
                    if live(0):
                        keep_inputs(*at(0))
                    if live(1):
                        keep_k(*at(1))

                def second_layer(i, live, at):
                    if live(2):
                        keep_q(*at(2))
                    if live(5):
                        keep_x_quantised(*at(5))
                    if live(4):
                        keep_normed(*at(4))
                    if live(0):
                        normalise(*at(0))
                    if live(2):
                        keep_v(*at(2))
                    if live(5):
                        gate_tanh(*at(5))
                    if live(6):
                        keep_h(*at(6))
                    if live(0):
                        keep_inputs(*at(0))
                    if live(3):
                        exponentials(*at(3), 0)
                    if live(0):
                        keep_qk(*at(0))
                    if live(3):
                        exponentials(*at(3), 1)
                    if live(4):
                        normalise2(*at(4))
                    if live(0):
                        split_hi(*at(0))
                    if live(1):
                        keep_k(*at(1))
                    if live(3):
                        keep_o(*at(3))
                    if live(2):
                        keep_max(*at(2))
                    if live(0):
                        split_mid(*at(0))
                pipeline(act, layer, DEPTHS[layer], second_layer if layer else first_layer)

            def weight_sums():
                act.wait_ge(ffn_loaded, FFN_CONSTS)
                nc.scalar.activation(w_abs[:, 0:INNER], w_gu[:, 0, :], ACT.Abs, accum_out=w_sums[:, 0:1]).then_inc(w_summed, 1)
                nc.scalar.activation(w_abs[:, INNER:2 * INNER], w_gu[:, 1, :], ACT.Abs, accum_out=w_sums[:, 1:2]).then_inc(w_summed, 1)
                act.wait_ge(w_summed, 2)
                nc.scalar.activation(w_abs[:, 0:INNER].rearrange("p (k d) -> p k d", k=I_TILES), w_dn[:, :, :], ACT.Abs,
                                     accum_out=w_sums[:, 2:3]).then_inc(w_summed, 1)

            def route_tanh(lo, hi, done):
                act.wait_ge(route_dve, done)
                nc.scalar.activation(weight[:, lo:hi, :], weight[:, lo:hi, :], ACT.Tanh).then_inc(route_tanh_done, 1)

            def experts():
                def group(g):
                    for m in range(EXPERTS * H_TILES):
                        n = EXPERTS * H_TILES * g + m
                        if isinstance(g, int) and m == (ROUTE_PARTS - 1) * H_TILES:
                            route_tanh(GROUP, BATCHES, 2 * ROUTE_STEPS - 1)
                        act.wait_ge(h1_made, n + 1)
                        need(act, hidden_done, n - 1)
                        nc.scalar.activation(silu[:, m % 2, :], ps_h1[m % 2], ACT.Silu).then_inc(silu_done, 1)

                group(0)
                with act.Fori(1, GROUPS, 1) as g:
                    group(g)

            weight_sums()
            layer_steps(0)
            route_tanh(0, GROUP, ROUTE_STEPS - 1)
            experts()
            act.wait_ge(expert_added, EXPERTS * GROUPS)
            layer_steps(1)

        @block.tensor
        def _(pe):
            pe.wait_ge(dve_setup, 6)
            nc.tensor.matmul(ps_in[:, 0:128], bv_rep[:, :], wo[0][:, :], start=True, stop=True).then_inc(pe_setup, 1)

            def layer_steps(layer):
                four = lambda a: a.unsqueeze(1).broadcast_to([128, UH // 2, 128])

                def turn_inputs(b, m, r):
                    pe.wait_ge(xn_done, m + 1)
                    pe.wait_ge(ctx_loaded[r], 8 * (m - r) + 16)
                    nc.tensor.transpose(ps_in[:, 0:128], xn[:, r, :], eye[:, :])
                    nc.tensor.transpose(ps_in[:, 128:256], ctx_in[:, r, :], eye[:, :]).then_inc(xc_turned, 1)

                def project_qk(b, m, r):
                    pe.wait_ge(xcT_done, m + 1)
                    nc.tensor.matmul(ps_in[:, 0:128], xcT[:, r, 0:128], wq[layer][:, :], start=True, stop=True)
                    nc.tensor.matmul(ps_in[:, 128:256], xcT[:, r, 128:256], wkv[layer][:, 0:128],
                                     start=True, stop=True).then_inc(qk_made, 1)

                def project_v(b, m, r):
                    pe.wait_ge(xcT_done, m + 1)
                    nc.tensor.matmul(ps_in[:, 256:384], xcT[:, r, 128:256], wkv[layer][:, 128:256],
                                     start=True, stop=True).then_inc(v_made, 1)

                def turn_k(b, m, r):
                    pe.wait_ge(stack_done, 4 * (m + 1))
                    for p in range(HEADS // 2):
                        last = nc.tensor.transpose(ps_k_b[:, p, :], stack[:, r, 1, 2 * p:2 * p + 2, :], eye_b[:, :])
                    last.then_inc(k_turned, 1)

                def turn_q(b, m, r):
                    pe.wait_ge(stack_done, 4 * (m + 1))
                    for p in range(HEADS // 2):
                        last = nc.tensor.transpose(ps_q_b[:, p, :], stack[:, r, 0, 2 * p:2 * p + 2, :], eye_b[:, :])
                    last.then_inc(q_turned, 1)

                def mask_scores(b, m, r, u):
                    for j in range(2):
                        for c in range(3):
                            nc.tensor.matmul(ps_max[:, j, :, :], eye_b[:, :], four(mask_parts[:, c, :]),
                                             start=(c == 0), stop=False, skip_group_check=True)

                def scores_for_max(b, m, r, u):
                    pe.wait_ge(kT_done, m + 1)
                    pe.wait_ge(qT_done, m + 1)
                    for g in range(UH // 2):
                        for j in range(2):
                            rows = slice(SLOT_ROWS * j, SLOT_ROWS * (j + 1))
                            p = UH // 2 * u + g
                            last = nc.tensor.matmul(ps_max[:, j, g, :], qT[rows, r, p, :], kT[rows, r, p, :],
                                                    start=(layer == 0), stop=True, skip_group_check=True)
                    last.then_inc(max_scores[u], 1)

                def turn_max(b, m, r):
                    pe.wait_ge(neg_done, m + 1)
                    nc.tensor.transpose(ps_k_b[:, 0, :], neg_parts[:, r, :, :, :], eye_b[:, :]).then_inc(m_turned, 1)

                def scores_for_exp(b, m, r, u):
                    pe.wait_ge(mT_done, m + 1)
                    for g in range(UH // 2):
                        for j in range(2):
                            rows = slice(SLOT_ROWS * j, SLOT_ROWS * (j + 1))
                            p = UH // 2 * u + g
                            nc.tensor.matmul(ps_exp[:, j, g, :], kT[rows, r, p, :], qT[rows, r, p, :],
                                             start=True, stop=False, skip_group_check=True)
                            last = nc.tensor.matmul(ps_exp[:, j, g, :], sel[rows, 2 * p + j, :], mT[rows, r, :],
                                                    start=False, stop=True, skip_group_check=True)
                    last.then_inc(exp_scores[u], 1)

                def probs_times_v(b, m, r, u):
                    pe.wait_ge(exp_done[u], m + 1)
                    pe.wait_ge(v_done, m + 1)
                    if u == 0:
                        need(pe, attn_done, m)
                    for g in range(UH // 2):
                        for j in range(2):
                            h = UH * u + 2 * g + j
                            strip = V_COLS * (h % 4)
                            last = nc.tensor.matmul(ps_out[strip:strip + V_COLS, 128 * (h // 4):128 * (h // 4 + 1)],
                                                    v_one[:, r, h, :], probs[:, u, j, g, :], start=True, stop=True,
                                                    skip_group_check=True)
                    last.then_inc(pv_made[u], 1)

                def turn_o(b, m, r):
                    pe.wait_ge(o_done, m + 1)
                    for c in range(4):
                        last = nc.tensor.transpose(ps_out[:, 128 * c:128 * c + 128], o_raw[:, 128 * c:128 * c + 128],
                                                   eye[:, :])
                    last.then_inc(o_turned, 1)

                def turn_normed(b, m, r):
                    pe.wait_ge(norm_done, m + 1)
                    nc.tensor.transpose(ps_out[:, 0:128], o_norm[:, :], eye[:, :]).then_inc(norm_turned, 1)

                def project_out(b, m, r):
                    pe.wait_ge(normT_done, m + 1)
                    nc.tensor.matmul(ps_out[:, 128:256], o_normT[:, :], wo[layer][:, :],
                                     start=True, stop=True).then_inc(attn_made, 1)

                def turn_xn(b, m, r):
                    pe.wait_ge(xn2_done, m + 1)
                    nc.tensor.transpose(ps_in[:, 0:128], xn2[:, r, :], eye[:, :]).then_inc(xn_turned, 1)

                def gate_scores(b, m, r):
                    pe.wait_ge(ring_done, b + 1)
                    nc.tensor.matmul(ps_in[:, 0:EXPERTS], xnT_ring[:, r, :], gate_w[:, :],
                                     start=True, stop=True).then_inc(gate_made, 1)

                def turn_x_quantised(b, m, r):
                    pe.wait_ge(xq_done, b + 1)
                    nc.tensor.transpose(ps_in_b[:, 0, :], xq[:, r, :], eye_b[:, :]).then_inc(xq_turned, 1)

                def project_gate_up(b, m, r):
                    pe.wait_ge(xqT_done, b + 1)
                    nc.tensor.matmul(ps_gate[:, :], xqT[:, r, :], wq_gu[:, 0, :], start=True, stop=True)
                    nc.tensor.matmul(ps_up[:, :], xqT[:, r, :], wq_gu[:, 1, :], start=True, stop=True).then_inc(gu_made, 1)

                def turn_h(b, m, r):
                    pe.wait_ge(hq_done, b + 1)
                    for k in range(I_TILES):
                        last = nc.tensor.transpose(ps_in_b[:, k, :], hq[:, 128 * k:128 * k + 128], eye_b[:, :])
                    last.then_inc(hq_turned, 1)

                def project_down(b, m, r):
                    pe.wait_ge(hqT_done, b + 1)
                    for k in range(I_TILES):
                        last = nc.tensor.matmul(ps_in[:, 0:128], hqT[:, k, :], wq_dn[:, k, :],
                                                start=(k == 0), stop=(k == I_TILES - 1))
                    last.then_inc(down_made, 1)

                def first_layer(i, live, at):
                    if live(2):
                        latest(pe, (live(3), qT_done, i - 2))
                        turn_q(*at(2))
                    if live(3):
                        latest(pe, (live(2), kT_done, i - 1), (live(4), mT_done, i - 3))
                        turn_max(*at(3))
                    if live(2):
                        latest(pe, (live(1), qk_done, i), (live(1), xcT_done, i), (live(6), score_done, i - 5),
                               (live(6), ring_done, i - 5), (live(3), v_done, i - 2))
                        project_v(*at(2))
                    if live(3):
                        latest(pe, (live(4), exp_done[1], i - 3), (live(4), exp_done[0], i - 3))
                        scores_for_exp(*at(3), 0)
                    if live(4):
                        turn_o(*at(4))
                    if live(5):
                        latest(pe, (live(2), v_done, i - 1), (live(1), qk_done, i), (live(1), xcT_done, i),
                               (live(6), score_done, i - 5), (live(6), ring_done, i - 5))
                        turn_xn(*at(5))
                    if live(2):
                        latest(pe, (live(3), max_done[1], i - 2), (live(3), max_done[0], i - 2))
                        scores_for_max(*at(2), 0)
                    if live(4):
                        turn_normed(*at(4))
                    if live(3):
                        latest(pe, (live(3), exp_done[0], i - 2), (live(4), exp_done[1], i - 3))
                        scores_for_exp(*at(3), 1)
                    if live(5):
                        latest(pe, (live(5), ring_done, i - 4), (live(2), v_done, i - 1), (live(1), qk_done, i),
                               (live(1), xcT_done, i), (live(6), score_done, i - 5))
                        gate_scores(*at(5))
                    if live(4):
                        project_out(*at(4))
                    if live(2):
                        latest(pe, (live(2), max_done[0], i - 1), (live(3), max_done[1], i - 2))
                        scores_for_max(*at(2), 1)
                    if live(0):
                        latest(pe, (live(5), score_done, i - 4), (live(5), ring_done, i - 4),
                               (live(2), v_done, i - 1), (live(1), qk_done, i), (live(1), xcT_done, i))
                        turn_inputs(*at(0))
                    if live(1):
                        latest(pe, (live(3), mT_done, i - 2), (live(2), kT_done, i - 1))
                        turn_k(*at(1))
                    if live(3):
                        probs_times_v(*at(3), 0)
                    if live(0):
                        latest(pe, (live(0), xcT_done, i + 1), (live(5), score_done, i - 4),
                               (live(5), ring_done, i - 4), (live(2), v_done, i - 1), (live(1), qk_done, i))
                        project_qk(*at(0))
                    if live(3):
                        probs_times_v(*at(3), 1)

                def second_layer(i, live, at):
                    if live(4):
                        turn_o(*at(4))
                    if live(3):
                        latest(pe, (live(4), masked_done[1], i - 3), (live(4), masked_done[0], i - 3))
                        scores_for_exp(*at(3), 0)
                    if live(5):
                        latest(pe, (live(7), ffn_done, i - 6), (live(1), qk_done, i + BATCHES),
                               (live(1), xcT_done, i + BATCHES), (live(7), hqT_done, i - 6),
                               (live(3), v_done, i + BATCHES - 2), (live(6), xqT_done, i - 5))
                        turn_x_quantised(*at(5))
                    if live(4):
                        turn_normed(*at(4))
                    if live(2):
                        scores_for_max(*at(2), 0)
                        latest(pe, (live(5), xqT_done, i - 4), (live(7), ffn_done, i - 6),
                               (live(1), qk_done, i + BATCHES), (live(1), xcT_done, i + BATCHES),
                               (live(7), hqT_done, i - 6), (live(3), v_done, i + BATCHES - 2))
                        project_v(*at(2))
                    if live(5):
                        latest(pe, (live(2), qT_done, i + BATCHES - 1), (live(6), gated_done, i - 5))
                        latest(pe, (live(3), mT_done, i + BATCHES - 2), (live(2), kT_done, i + BATCHES - 1),
                               (live(6), h_done, i - 5))
                        project_gate_up(*at(5))
                    if live(4):
                        project_out(*at(4))
                    if live(6):
                        latest(pe, (live(2), v_done, i + BATCHES - 1), (live(5), xqT_done, i - 4),
                               (live(7), ffn_done, i - 6), (live(1), qk_done, i + BATCHES),
                               (live(1), xcT_done, i + BATCHES), (live(7), hqT_done, i - 6))
                        turn_h(*at(6))
                    if live(3):
                        latest(pe, (live(3), masked_done[0], i - 2), (live(4), masked_done[1], i - 3))
                        scores_for_exp(*at(3), 1)
                    if live(0):
                        latest(pe, (live(6), hqT_done, i - 5), (live(2), v_done, i + BATCHES - 1),
                               (live(5), xqT_done, i - 4), (live(7), ffn_done, i - 6),
                               (live(1), qk_done, i + BATCHES), (live(1), xcT_done, i + BATCHES))
                        turn_inputs(*at(0))
                    if live(2):
                        latest(pe, (live(2), max_done[0], i + BATCHES - 1), (live(3), max_done[1], i + BATCHES - 2))
                        mask_scores(*at(2), 1)
                    if live(0):
                        latest(pe, (live(0), xcT_done, i + BATCHES + 1), (live(6), hqT_done, i - 5),
                               (live(2), v_done, i + BATCHES - 1), (live(5), xqT_done, i - 4),
                               (live(7), ffn_done, i - 6), (live(1), qk_done, i + BATCHES))
                        project_qk(*at(0))
                    if live(2):
                        scores_for_max(*at(2), 1)
                    if live(3):
                        probs_times_v(*at(3), 0)
                    if live(6):
                        latest(pe, (live(0), qk_done, i + BATCHES + 1), (live(0), xcT_done, i + BATCHES + 1),
                               (live(6), hqT_done, i - 5), (live(2), v_done, i + BATCHES - 1),
                               (live(5), xqT_done, i - 4), (live(7), ffn_done, i - 6))
                        project_down(*at(6))
                    if live(1):
                        latest(pe, (live(5), h_done, i - 4), (live(3), mT_done, i + BATCHES - 2),
                               (live(2), kT_done, i + BATCHES - 1))
                        turn_k(*at(1))
                        latest(pe, (live(5), gated_done, i - 4), (live(2), qT_done, i + BATCHES - 1))
                        turn_q(*at(1))
                    if live(3):
                        probs_times_v(*at(3), 1)
                    if live(1):
                        latest(pe, (live(2), max_done[1], i + BATCHES - 1), (live(2), max_done[0], i + BATCHES - 1))
                        mask_scores(*at(1), 0)
                    if live(2):
                        latest(pe, (live(1), kT_done, i + BATCHES), (live(5), h_done, i - 4),
                               (live(3), mT_done, i + BATCHES - 2))
                        turn_max(*at(2))
                pipeline(pe, layer, DEPTHS[layer], second_layer if layer else first_layer)

            def weight_totals():
                pe.wait_ge(w_summed, 3)
                pe.wait_ge(score_done, BATCHES)
                nc.tensor.matmul(ps_in[:, 0:3], ones[:, :], w_sums[:, :], start=True, stop=True).then_inc(w_totalled, 1)

            def experts():
                def up(g, e):
                    x_group = xnT_all[:, bass.ds(GROUP * g, GROUP), :]
                    for k in range(H_TILES):
                        m = (EXPERTS * g + e) * H_TILES + k
                        need(pe, hidden_done, m - 1)
                        nc.tensor.matmul(ps_h1[k % 2], w12[:, e, 128 * k:128 * k + 128], x_group,
                                         start=True, stop=True).then_inc(h1_made, 1)
                        k2 = TWO_H // 2 + 128 * k
                        nc.tensor.matmul(ps_h2[k % 2], w12[:, e, k2:k2 + 128], x_group,
                                         start=True, stop=True).then_inc(h2_made, 1)

                def down(g, e):
                    pe.wait_ge(hidden_done, (EXPERTS * g + e + 1) * H_TILES)
                    need(pe, expert_added, EXPERTS * g + e - 1)
                    for b in range(GROUP):
                        for k in range(H_TILES):
                            last = nc.tensor.matmul(ps_expert[e % 2][:, 128 * b:128 * b + 128],
                                                    hidden[:, e % 2, k, 128 * b:128 * b + 128], w3[:, e, k, :],
                                                    start=(k == 0), stop=(k == H_TILES - 1))
                    last.then_inc(expert_made, 1)

                def group(g, first):
                    for e in range(EXPERTS):
                        up(g, e)
                        if e:
                            down(g, e - 1)
                        elif not first:
                            down(g - 1, EXPERTS - 1)

                pe.wait_ge(all_done, BATCHES)
                group(0, True)
                with pe.Fori(1, GROUPS, 1) as g:
                    group(g, False)
                down(GROUPS - 1, EXPERTS - 1)

            pe.wait_ge(ffn_loaded, FFN_CONSTS)
            pe.wait_ge(dve_setup, SETUP_ALL)
            layer_steps(0)
            weight_totals()
            experts()
            pe.wait_ge(mask_split, MASK_STEPS)
            pe.wait_ge(w_quantised, 9)
            pe.wait_ge(expert_added, EXPERTS * GROUPS)
            layer_steps(1)


def layouts(inputs):
    import numpy as np

    a = {k: np.asarray(v) for k, v in inputs.items()}
    turn = lambda w, *axes: np.ascontiguousarray(np.transpose(w, axes))
    d = a["x"].shape[-1]
    out = {
        "x": a["x"], "ctx": a["ctx_1024"], "mask": a["fside_SxS2_0"], "maskT": turn(a["fside_SxS2_0"], 1, 0), "g_xattn": a["g_xattn"], "g_ffn": a["g_ffn"],
        "Wq0": a["L0_xattn_Wq"], "Wk0": a["L0_xattn_Wk"], "Wv0": a["L0_xattn_Wv"], "Wo0": a["L0_xattn_Wo"],
        "bq": a["L0_xattn_bq"], "bk": a["L0_xattn_bk"], "bv": a["L0_xattn_bv"], "bo": a["L0_xattn_bo"],
        "Wq1": turn(a["L1_xattn_WQ"], 1, 0, 2).reshape(d, d), "Wk1": turn(a["L1_xattn_WK"], 1, 0, 2).reshape(d, d),
        "Wv1": turn(a["L1_xattn_WV"], 1, 0, 2).reshape(d, d), "Wo1": a["L1_xattn_WO"],
        "w12T": turn(a["L0_ffn_w12"], 2, 0, 1), "w3T": turn(a["L0_ffn_w3"], 2, 0, 1),
        "gateT": turn(a["L0_ffn_gate_w"], 1, 0),
        "w_gateT": turn(a["L1_ffn_w_gate"], 1, 0), "w_upT": turn(a["L1_ffn_w_up"], 1, 0),
        "w_downT": turn(a["L1_ffn_w_down"], 1, 0),
        "eye": np.eye(128, dtype=np.float32), "before": np.tril(np.ones((8, 8), np.float32), -1),
    }
    return {k: np.ascontiguousarray(v) for k, v in out.items()}


def kernel(**inputs):
    import concourse.bacc as bacc
    from concourse.bass_utils import run_bass_kernel_spmd

    arrays = layouts(inputs)
    nc = bacc.Bacc("TRN2", target_bir_lowering=False, num_devices=1)
    t = {k: nc.dram_tensor(f"in_{k}", a.shape, mybir.dt.from_np(a.dtype), kind="ExternalInput").ap()
         for k, a in arrays.items()}
    t["out"] = nc.dram_tensor("out_x", arrays["x"].shape, mybir.dt.float32, kind="ExternalOutput").ap()
    gated_cross_attention_stack(nc, t)
    r = run_bass_kernel_spmd(nc, [{f"in_{k}": a for k, a in arrays.items()}], core_ids=[0])
    return r.results[0]["out_x"]
```

```python
import concourse.bass as bass
from concourse import mybir
from contextlib import ExitStack


def gated_cross_attention_stack(nc, t):
    F32, BF16 = mybir.dt.float32, mybir.dt.bfloat16
    ALU = mybir.AluOpType
    ACT = mybir.ActivationFunctionType
    AX = mybir.AxisListType

    BATCHES, _, D = t["x"].shape
    HEADS, HD = 16, D // 16
    UNITS, UH = 2, HEADS // 2
    EXPERTS, TWO_H = t["w12T"].shape[1:]
    H_TILES = TWO_H // 2 // 128
    INNER = t["gate_upT"].shape[1] // 2
    I_TILES = INNER // 128
    GROUP = 4
    GROUPS = BATCHES // GROUP
    SLOTS, SLOT_ROWS = 8, 64
    V_COLS = 32
    EPS = 1e-5
    MAGIC = 1.5 * 2.0 ** 23

    ctx = ExitStack()
    with ctx:
        def sb(name, shape, dt=F32):
            return ctx.enter_context(nc.sbuf_tensor(f"{name}_sb", shape, dt))

        def sem(name):
            return ctx.enter_context(nc.semaphore(name))

        def need(eng, semaphore, count):
            if not isinstance(count, int) or count > 0:
                eng.wait_ge(semaphore, count)

        x_all = sb("x_all", [128, BATCHES, D])
        early = sb("early", [128, t["early"].shape[1]])
        late = sb("late", [128, t["late"].shape[1]])
        rows = sb("rows", [128, t["rows"].shape[0]])
        eye, wo0, wq0, wkv0 = early[:, 0:128], early[:, 128:256], early[:, 256:384], early[:, 384:640]
        gate_w, bv_col = early[:, 640:640 + EXPERTS], early[:, 640 + EXPERTS:641 + EXPERTS]
        wo1, wq1, wkv1 = late[:, 0:128], late[:, 128:256], late[:, 256:512]
        mask, maskT = late[:, 512:640], late[:, 640:768]
        wq, wkv, wo = (wq0, wq1), (wkv0, wkv1), (wo0, wo1)
        bqk, bo_row, gains = rows[:, 0:256], rows[:, 256:384], rows[:, 384:388]
        eye_b = sb("eye_bf16", [128, 128], BF16)
        ones = sb("ones_f32", [128, 128])
        half = sb("minus_half", [128, 1])
        eps = sb("eps", [128, 1])
        zero = sb("zero", [128, 1])
        tanh_g = sb("tanh_g", [128, 4])
        bv_rep = sb("bv_rep", [128, 128])
        bias_out = sb("bias_out", [128, 128])
        mask_rest = sb("mask_rest", [128, 128])
        mask_parts = sb("mask_parts", [128, 3, 128], BF16)
        sel_ind = sb("sel_ind", [128, HEADS])
        sel = sb("sel", [128, HEADS, 128], BF16)
        ctx_in = sb("ctx_in", [128, 2, D])
        stats = sb("stats", [128, 2, 6])
        mean_var = sb("mean_var", [128, 2, 2])
        var_eps = sb("var_eps", [128, 2, 1])
        rstd = sb("rstd", [128, 2, 1])
        neg_mean = sb("neg_mean", [128, 2, 1])
        shift = sb("shift", [128, 2, 1])
        xn = sb("xn", [128, 2, D])
        xcT = sb("xcT", [128, 2, 256])
        qk = sb("qk", [128, 2, 256])
        qk_rest = sb("qk_rest", [128, 2, 256])
        stack = sb("stack", [128, 2, 2, HEADS, SLOTS * HD], BF16)
        qT = sb("qT", [128, 2, HEADS // 2, 128], BF16)
        kT = sb("kT", [128, 2, HEADS // 2, 128], BF16)
        v_one = sb("v_one", [128, 2, HEADS, V_COLS])
        neg_max = sb("neg_max", [128, 2, HEADS])
        neg_rest = sb("neg_rest", [128, 2, HEADS])
        neg_parts = sb("neg_parts", [128, 2, 2, 4, HEADS], BF16)
        mT = sb("mT", [128, 2, 128], BF16)
        masked = sb("masked", [128, UNITS, 2, UH // 2, 128])
        probs = sb("probs", [128, UNITS, 2, UH // 2, 128])
        o_raw = sb("o_raw", [128, 512])
        o_rden = sb("o_rden", [128, HEADS])
        o_norm = sb("o_norm", [128, 128])
        o_normT = sb("o_normT", [128, 128])

        w12 = sb("w12", [128, EXPERTS, TWO_H])
        w3 = sb("w3", [128, EXPERTS, H_TILES, D])
        before = sb("before", [128, EXPERTS, EXPERTS])
        stats2 = sb("stats2", [128, 2, 6])
        mean_var2 = sb("mean_var2", [128, 2, 2])
        var_eps2 = sb("var_eps2", [128, 2, 1])
        rstd2 = sb("rstd2", [128, 2, 1])
        neg_mean2 = sb("neg_mean2", [128, 2, 1])
        shift2 = sb("shift2", [128, 2, 1])
        xn2 = sb("xn2", [128, 2, D])
        xnT_ring = sb("xnT_ring", [128, 2, 128])
        xnT_all = sb("xnT_all", [128, BATCHES, 128])
        scores = sb("scores", [128, BATCHES, EXPERTS])
        greater = sb("greater", [128, BATCHES, EXPERTS, EXPERTS])
        at_least = sb("at_least", [128, BATCHES, EXPERTS, EXPERTS])
        rank = sb("rank", [128, BATCHES, EXPERTS])
        chosen = sb("chosen", [128, BATCHES, EXPERTS])
        midway = sb("midway", [128, BATCHES])
        weight = sb("weight", [128, BATCHES, EXPERTS])
        silu = sb("silu", [128, 2, GROUP * 128])
        hidden = sb("hidden", [128, 2, H_TILES, GROUP * 128])
        w_gu = sb("w_gu", [128, 2, INNER])
        w_dn = sb("w_dn", [128, I_TILES, D])
        w_abs = sb("w_abs", [128, 2 * INNER])
        w_sums = sb("w_sums", [128, 3])
        w_mean = sb("w_mean", [128, 3])
        w_scale = sb("w_scale", [128, 3])
        w_inv = sb("w_inv", [128, 3])
        w_factor = sb("w_factor", [128, 3])
        half_gain = sb("half_gain", [128, 1])
        w_back = sb("w_back", [128, 3])
        wq_gu = sb("wq_gu", [128, 2, INNER], BF16)
        wq_dn = sb("wq_dn", [128, I_TILES, D], BF16)
        top_x = sb("top_x", [128, 2, 1])
        clip_x = sb("clip_x", [128, 2, 1])
        scale_x = sb("scale_x", [128, 2, 1])
        back_x = sb("back_x", [128, 2, 2])
        back_gu = sb("back_gu", [128, 2, 1])
        top_h = sb("top_h", [128, 2, 1])
        clip_h = sb("clip_h", [128, 2, 1])
        scale_h = sb("scale_h", [128, 2, 1])
        back_h = sb("back_h", [128, 2, 1])
        x_round = sb("x_round", [128, D])
        xq = sb("xq", [128, 2, D], BF16)
        xqT = sb("xqT", [128, 2, 128], BF16)
        gate = sb("gate", [128, 2, INNER])
        gated = sb("gated", [128, INNER])
        h = sb("h", [128, 2, INNER])
        h_round = sb("h_round", [128, INNER])
        hq = sb("hq", [128, INNER], BF16)
        hqT = sb("hqT", [128, I_TILES, 128], BF16)

        ps_max = ctx.enter_context(nc.psum_tensor("ps_max", [128, 2, UH // 2, 128], F32))
        ps_exp = ctx.enter_context(nc.psum_tensor("ps_exp", [128, 2, UH // 2, 128], F32))
        ps_q = ctx.enter_context(nc.psum_tensor("ps_q", [128, 512], F32))
        ps_k = ctx.enter_context(nc.psum_tensor("ps_k", [128, 512], F32))
        ps_in = ctx.enter_context(nc.psum_tensor("ps_in", [128, 512], F32))
        ps_out = ctx.enter_context(nc.psum_tensor("ps_out", [128, 512], F32))
        ps_h1 = [ps_max[:, u, :, :].rearrange("p g k -> p (g k)") for u in range(2)]
        ps_h2 = [ps_exp[:, u, :, :].rearrange("p g k -> p (g k)") for u in range(2)]
        ps_expert = [ps_q, ps_k]
        ps_gate, ps_up = ps_q, ps_k
        ps_in_b = ps_in[:, :].bitcast(BF16).rearrange("p (h t) -> p h t", h=HEADS // 2)
        ps_q_b = ps_q[:, :].bitcast(BF16).rearrange("p (h t) -> p h t", h=HEADS // 2)
        ps_k_b = ps_k[:, :].bitcast(BF16).rearrange("p (h t) -> p h t", h=HEADS // 2)

        x_loaded, consts_loaded, ffn_loaded, out_stored = (
            sem("x_loaded"), sem("consts_loaded"), sem("ffn_loaded"), sem("out_stored"))
        rest_loaded = sem("rest_loaded")
        ctx_loaded = [sem(f"ctx_loaded{r}") for r in range(2)]
        dve_setup, act_setup, pool_setup, pe_setup = sem("dve_setup"), sem("act_setup"), sem("pool_setup"), sem("pe_setup")
        layer1_ready = sem("layer1_ready")
        stats_done, aggr_done, eps_done, rstd_done, shift_done, xn_done = (
            sem("stats_done"), sem("aggr_done"), sem("eps_done"), sem("rstd_done"), sem("shift_done"), sem("xn_done"))
        xc_turned, xcT_done, qk_made, qk_done, v_made, v_done = (
            sem("xc_turned"), sem("xcT_done"), sem("qk_made"), sem("qk_done"), sem("v_made"), sem("v_done"))
        hi_done, rest_done, mid_done, lo_done, stack_done = (
            sem("hi_done"), sem("rest_done"), sem("mid_done"), sem("lo_done"), sem("stack_done"))
        k_turned, q_turned, kT_done, qT_done = sem("k_turned"), sem("q_turned"), sem("kT_done"), sem("qT_done")
        unit = lambda name: [sem(f"{name}{u}") for u in range(UNITS)]
        max_scores, max_done, exp_scores, masked_done, exp_done, pv_made = (
            unit("max_scores"), unit("max_done"), unit("exp_scores"), unit("masked_done"), unit("exp_done"),
            unit("pv_made"))
        n0_done, n0_rest, n1_done, neg_done, m_turned, mT_done = (
            sem("n0_done"), sem("n0_rest"), sem("n1_done"), sem("neg_done"), sem("m_turned"), sem("mT_done"))
        o_done, o_turned, rden_done, norm_done, norm_turned, normT_done = (
            sem("o_done"), sem("o_turned"), sem("rden_done"), sem("norm_done"), sem("norm_turned"), sem("normT_done"))
        attn_made, bias_added, attn_done = sem("attn_made"), sem("bias_added"), sem("attn_done")
        stats2_done, aggr2_done, eps2_done, rstd2_done, shift2_done, xn2_done = (
            sem("stats2_done"), sem("aggr2_done"), sem("eps2_done"), sem("rstd2_done"), sem("shift2_done"), sem("xn2_done"))
        xn_turned, ring_done, all_done, gate_made, score_done = (
            sem("xn_turned"), sem("ring_done"), sem("all_done"), sem("gate_made"), sem("score_done"))
        route_dve, route_tanh_done, gains_done = sem("route_dve"), sem("route_tanh_done"), sem("gains_done")
        h1_made, h2_made, silu_done, hidden_done, expert_made, expert_added = (
            sem("h1_made"), sem("h2_made"), sem("silu_done"), sem("hidden_done"), sem("expert_made"), sem("expert_added"))
        w_summed, w_totalled, w_scaled, w_quantised = (
            sem("w_summed"), sem("w_totalled"), sem("w_scaled"), sem("w_quantised"))
        top_x_done, clip_x_done, recip_x_done, scale_x_done, back_x_done, back_gu_done = (
            sem("top_x_done"), sem("clip_x_done"), sem("recip_x_done"), sem("scale_x_done"), sem("back_x_done"),
            sem("back_gu_done"))
        x_rounded, xq_done, xq_turned, xqT_done, gu_made, gate_done, gated_done, h_done = (
            sem("x_rounded"), sem("xq_done"), sem("xq_turned"), sem("xqT_done"), sem("gu_made"), sem("gate_done"),
            sem("gated_done"), sem("h_done"))
        top_h_done, clip_h_done, recip_h_done, scale_h_done, back_h_done = (
            sem("top_h_done"), sem("clip_h_done"), sem("recip_h_done"), sem("scale_h_done"), sem("back_h_done"))
        h_rounded, hq_done, hq_turned, hqT_done, down_made, ffn_done = (
            sem("h_rounded"), sem("hq_done"), sem("hq_turned"), sem("hqT_done"), sem("down_made"), sem("ffn_done"))

        LAST = BATCHES - 1

        def pipeline(eng, layer, depth, step, after_step=None):
            def one(i, odd, live):
                step(i, live, lambda l: (i - l, i - l + BATCHES * layer, (odd + l) % 2))

            first = (depth + 3) // 2 * 2
            after = first + (BATCHES - first) // 2 * 2
            for i in range(first):
                one(i, i % 2, lambda l: 0 <= i - l <= LAST)
            with eng.Fori(first, after - 1, 2) as j:
                for u in range(2):
                    one(j + u, u, lambda l: True)
            for i in range(after, LAST + depth + 1):
                one(i, i % 2, lambda l: 0 <= i - l <= LAST)
                if after_step:
                    after_step(i)

        def latest(eng, *reads):
            for exists, semaphore, count in reads:
                if exists:
                    need(eng, semaphore, count)
                    return


        block = ctx.enter_context(nc.Block())

        const_loads = [(early[:, :], t["early"]), (rows[:, :], t["rows"].partition_broadcast(128))]
        ffn_loads = [
            (before[:, :, :].rearrange("p a b -> p (a b)"), t["before"].rearrange("a b -> (a b)").partition_broadcast(128)),
            (w12[:, :, :], t["w12T"]), (w3[:, :, :, :], t["w3T"].rearrange("(k p) e d -> p e k d", k=H_TILES)),
            (w_gu[:, :, :].rearrange("p w n -> p (w n)"), t["gate_upT"]),
            (w_dn[:, :, :], t["w_downT"].rearrange("(k p) d -> p k d", k=I_TILES)),
            (late[:, :], t["late"]),
        ]
        CONSTS = 16 * len(const_loads)
        FFN_CONSTS = 16 * len(ffn_loads)
        ROUTE_PARTS, ROUTE_STEPS = 7, 11
        DEPTHS = (5, 6)
        SETUP_BIAS, SETUP_ALL = 7, 9
        POOL_SETUP, LAYER1_STEPS = 9, 6
        HEAD_START = LAST + DEPTHS[0] - 2

        @block.sync
        def _(sp):
            sp.dma_start(x_all[:, 0, :], t["x"][0, :, :]).then_inc(x_loaded, 16)
            sp.dma_start(ctx_in[:, 0, :], t["ctx"][0, :, :]).then_inc(ctx_loaded[0], 16)
            sp.dma_start(ctx_in[:, 1, :], t["ctx"][1, :, :]).then_inc(ctx_loaded[1], 16)
            sp.wait_ge(consts_loaded, CONSTS)
            sp.dma_start(x_all[:, 1:BATCHES, :], t["x"][1:BATCHES, :, :].rearrange("b s d -> s b d")).then_inc(rest_loaded, 16)

            def load_context(i, r, layer):
                sp.wait_ge(xc_turned, i + BATCHES * layer - 1)
                sp.dma_start(ctx_in[:, r, :], t["ctx"][i, :, :]).then_inc(ctx_loaded[r], 16)

            for i in range(2, 2 + len(ffn_loads)):
                load_context(i, i % 2, 0)
                dst, src = ffn_loads[i - 2]
                sp.dma_start(dst, src).then_inc(ffn_loaded, 16)
            for layer, first in ((0, 2 + len(ffn_loads)), (1, 0)):
                with sp.Fori(first, LAST, 2) as j:
                    for u in range(2):
                        load_context(j + u, u, layer)
            with sp.Fori(0, BATCHES, 1) as b:
                sp.wait_ge(ffn_done, b + 1)
                sp.dma_start(t["out"][b, :, :], x_all[:, b, :]).then_inc(out_stored, 16)
            sp.wait_ge(out_stored, 16 * BATCHES)

        @block.gpsimd
        def _(pool):
            nc.gpsimd.memset(half[:, :], -0.5).then_inc(pool_setup, 1)
            nc.gpsimd.memset(eps[:, :], EPS).then_inc(pool_setup, 1)
            nc.gpsimd.memset(zero[:, :], 0.0).then_inc(pool_setup, 1)
            nc.gpsimd.memset(ones[:, :], 1.0).then_inc(pool_setup, 1)
            nc.gpsimd.memset(stack[:, :, :, :, :], 0.0).then_inc(pool_setup, 1)
            nc.gpsimd.memset(neg_parts[:, :, :, :, :], 0.0).then_inc(pool_setup, 1)
            nc.gpsimd.memset(v_one[:, :, :, :], 0.0).then_inc(pool_setup, 1)
            pool.wait_ge(pool_setup, 7)
            for r in range(2):
                nc.gpsimd.memset(v_one[:, r, :, HD:HD + 1], 1.0).then_inc(pool_setup, 1)

            def layer_steps(layer):
                def add_eps(b, m, r):
                    pool.wait_ge(aggr_done, m + 1)
                    nc.gpsimd.tensor_tensor(var_eps[:, r, :], mean_var[:, r, 1:2], eps[:, :], ALU.add).then_inc(eps_done, 1)
                    if layer == 1:
                        nc.gpsimd.tensor_tensor(neg_mean[:, r, :], zero[:, :], mean_var[:, r, 0:1],
                                                ALU.subtract).then_inc(shift_done, 1)

                def inverse_deviation(b, m, r):
                    pool.wait_ge(eps_done, m + 1)
                    nc.gpsimd.tensor_tensor(rstd[:, r, :], var_eps[:, r, :], half[:, :], ALU.pow).then_inc(rstd_done, 1)
                    if layer == 1:
                        pool.wait_ge(rstd_done, m + 1)
                        pool.wait_ge(shift_done, 2 * b + 1)
                        nc.gpsimd.tensor_tensor(shift[:, r, :], neg_mean[:, r, :], rstd[:, r, :],
                                                ALU.mult).then_inc(shift_done, 1)

                def add_eps2(b, m, r):
                    pool.wait_ge(aggr2_done, m + 1)
                    nc.gpsimd.tensor_tensor(var_eps2[:, r, :], mean_var2[:, r, 1:2], eps[:, :], ALU.add).then_inc(eps2_done, 1)
                    if layer == 1:
                        nc.gpsimd.tensor_tensor(neg_mean2[:, r, :], zero[:, :], mean_var2[:, r, 0:1],
                                                ALU.subtract).then_inc(shift2_done, 1)

                def inverse_deviation2(b, m, r):
                    pool.wait_ge(eps2_done, m + 1)
                    nc.gpsimd.tensor_tensor(rstd2[:, r, :], var_eps2[:, r, :], half[:, :], ALU.pow).then_inc(rstd2_done, 1)
                    if layer == 1:
                        pool.wait_ge(rstd2_done, m + 1)
                        pool.wait_ge(shift2_done, 2 * b + 1)
                        nc.gpsimd.tensor_tensor(shift2[:, r, :], neg_mean2[:, r, :], rstd2[:, r, :],
                                                ALU.mult).then_inc(shift2_done, 1)

                def add_bias(b, m, r):
                    pool.wait_ge(xn_done, m + 1)
                    if isinstance(b, int) and b == 0:
                        pool.wait_ge(dve_setup, SETUP_BIAS)
                    nc.gpsimd.tensor_tensor(x_all[:, b, :], x_all[:, b, :], bias_out[:, :], ALU.add).then_inc(bias_added, 1)

                def repeat_parts(b, m, r):
                    pool.wait_ge(lo_done, m + 1)
                    q, k = stack[:, r, 0, :, :], stack[:, r, 1, :, :]
                    pair = lambda a, c: a[:, :, c * HD:(c + 2) * HD]
                    nc.gpsimd.tensor_tensor(pair(q, 5), pair(q, 1),
                                            zero[:, :].unsqueeze(2).broadcast_to([128, HEADS, 2 * HD]),
                                            ALU.add).then_inc(stack_done, 1)
                    nc.gpsimd.tensor_scalar(pair(k, 3), pair(k, 1), 1.0, 0.0, ALU.mult, ALU.add).then_inc(stack_done, 1)
                    for a, c in ((q, 3), (k, 5)):
                        dst = pair(a, c).rearrange("p h (c d) -> p h c d", c=2)
                        src = a[:, :, 0:HD].unsqueeze(2).broadcast_to([128, HEADS, 2, HD])
                        nc.gpsimd.tensor_scalar(dst, src, 1.0, 0.0, ALU.mult, ALU.add).then_inc(stack_done, 1)

                def gather_xn(b, m, r):
                    pool.wait_ge(ring_done, b + 1)
                    nc.gpsimd.tensor_copy(xnT_all[:, b, :], xnT_ring[:, r, :]).then_inc(all_done, 1)

                def round_x(b, m, r):
                    pool.wait_ge(scale_x_done, b + 1)
                    nc.gpsimd.tensor_tensor(back_x[:, r, :], clip_x[:, r, :].broadcast_to([128, 2]), w_back[:, 0:2],
                                            ALU.mult).then_inc(back_x_done, 1)
                    nc.gpsimd.tensor_scalar(x_round[:, :], xn2[:, r, :], scale_x[:, r, :], MAGIC, ALU.mult, ALU.add).then_inc(x_rounded, 1)
                    pool.wait_ge(back_x_done, b + 1)
                    nc.gpsimd.tensor_tensor(back_gu[:, r, :], back_x[:, r, 0:1], back_x[:, r, 1:2],
                                            ALU.mult).then_inc(back_gu_done, 1)

                def round_h(b, m, r):
                    pool.wait_ge(scale_h_done, b + 1)
                    nc.gpsimd.tensor_tensor(back_h[:, r, :], clip_h[:, r, :], w_back[:, 2:3], ALU.mult).then_inc(back_h_done, 1)
                    nc.gpsimd.tensor_scalar(h_round[:, :], h[:, r, :], scale_h[:, r, :], MAGIC, ALU.mult, ALU.add).then_inc(h_rounded, 1)

                def first_layer(i, live, at):
                    if live(5):
                        inverse_deviation2(*at(5))
                    if live(1):
                        add_bias(*at(1))
                    if live(0):
                        add_eps(*at(0))
                        inverse_deviation(*at(0))
                    if live(1):
                        repeat_parts(*at(1))
                    if live(5):
                        gather_xn(*at(5))
                    if live(4):
                        add_eps2(*at(4))

                def second_layer(i, live, at):
                    if live(0):
                        add_eps(*at(0))
                    if live(5):
                        round_x(*at(5))
                    if live(0):
                        inverse_deviation(*at(0))
                    if live(6):
                        round_h(*at(6))
                    if live(4):
                        add_eps2(*at(4))
                    if live(1):
                        repeat_parts(*at(1))
                    if live(4):
                        inverse_deviation2(*at(4))
                pipeline(pool, layer, DEPTHS[layer], second_layer if layer else first_layer)

            def quantise_weights():
                pool.wait_ge(w_scaled, 5)
                for m, (w, out) in enumerate(((w_gu[:, 0, :], wq_gu[:, 0, :]), (w_gu[:, 1, :], wq_gu[:, 1, :]),
                                              (w_dn[:, :, :], wq_dn[:, :, :]))):
                    nc.gpsimd.tensor_scalar(w, w, w_scale[:, m:m + 1], MAGIC, ALU.mult, ALU.add).then_inc(w_quantised, 1)
                    pool.wait_ge(w_quantised, 3 * m + 1)
                    nc.gpsimd.tensor_scalar(w, w, -MAGIC, 1.0, ALU.add, ALU.min).then_inc(w_quantised, 1)
                    pool.wait_ge(w_quantised, 3 * m + 2)
                    nc.gpsimd.tensor_scalar(out, w, -1.0, 1.0, ALU.max, ALU.mult).then_inc(w_quantised, 1)

            layer_steps(0)
            quantise_weights()
            layer_steps(1)

        @block.vector
        def _(dve):
            scale = float(HD) ** -0.5
            dve.wait_ge(consts_loaded, CONSTS)
            nc.vector.tensor_copy(eye_b[:, :], eye[:, :]).then_inc(dve_setup, 1)
            nc.vector.tensor_scalar(wq[0][:, :], wq[0][:, :], scale, None, ALU.mult).then_inc(dve_setup, 1)
            nc.vector.tensor_scalar(bqk[:, 0:128], bqk[:, 0:128], scale, None, ALU.mult).then_inc(dve_setup, 1)
            nc.vector.tensor_reduce(sel_ind[:, :], eye[:, :].rearrange("p (a c h) -> p h a c", a=2, c=4)[:, :, :, 0:3],
                                    AX.XY, ALU.add).then_inc(dve_setup, 1)
            dve.wait_ge(pool_setup, POOL_SETUP)
            nc.vector.tensor_scalar(bv_rep[:, :], ones[:, :], bv_col[:, 0:1], None, ALU.mult).then_inc(dve_setup, 1)

            def output_bias():
                dve.wait_ge(pe_setup, 1)
                nc.vector.tensor_tensor(bias_out[:, :], ps_in[:, 0:128], bo_row[:, :], ALU.add).then_inc(dve_setup, 1)
                dve.wait_ge(dve_setup, SETUP_BIAS - 1)
                dve.wait_ge(act_setup, 1)
                nc.vector.tensor_scalar(bias_out[:, :], bias_out[:, :], tanh_g[:, 0:1], None, ALU.mult).then_inc(dve_setup, 1)
                nc.vector.tensor_scalar(wo[0][:, :], wo[0][:, :], tanh_g[:, 0:1], None, ALU.mult).then_inc(dve_setup, 1)
                nc.vector.tensor_scalar(half_gain[:, :], tanh_g[:, 2:3], 0.5, None, ALU.mult).then_inc(dve_setup, 1)

            output_bias()
            dve.wait_ge(x_loaded, 16)

            def layer_steps(layer):
                def statistics(b, m, r):
                    if layer == 0 and isinstance(b, int) and b == 1:
                        dve.wait_ge(rest_loaded, 16)
                    nc.vector.bn_stats(stats[:, r, :], x_all[:, b, :]).then_inc(stats_done, 1)

                def statistics_ready(b, m, r):
                    dve.wait_ge(stats_done, m + 1)

                def mean_and_variance(b, m, r):
                    nc.vector.bn_aggr(mean_var[:, r, :], stats[:, r, :]).then_inc(aggr_done, 1)

                def normalise(b, m, r):
                    dve.wait_ge(rstd_done, m + 1)
                    nc.vector.tensor_scalar(xn[:, r, :], x_all[:, b, :], mean_var[:, r, 0:1], rstd[:, r, :],
                                            ALU.subtract, ALU.mult).then_inc(xn_done, 1)

                heads = lambda a, r: a[:, r, :].rearrange("p (w h d) -> p w h d", w=2, h=HEADS)
                slot = lambda r, c: stack[:, r, :, :, c * HD:(c + 1) * HD]

                def keep_qk(b, m, r):
                    dve.wait_ge(qk_made, m + 1)
                    nc.vector.tensor_tensor(qk[:, r, :], ps_in[:, 0:256], bqk[:, :], ALU.add).then_inc(qk_done, 1)

                def split_hi(b, m, r):
                    dve.wait_ge(qk_done, m + 1)
                    nc.vector.tensor_copy(slot(r, 0), heads(qk, r)).then_inc(hi_done, 1)

                def split_rest(b, m, r):
                    dve.wait_ge(hi_done, m + 1)
                    nc.vector.tensor_tensor(heads(qk_rest, r), heads(qk, r), slot(r, 0), ALU.subtract).then_inc(rest_done, 1)

                def split_mid(b, m, r):
                    dve.wait_ge(rest_done, m + 1)
                    nc.vector.tensor_copy(slot(r, 1), heads(qk_rest, r)).then_inc(mid_done, 1)

                def split_lo(b, m, r):
                    dve.wait_ge(mid_done, m + 1)
                    nc.vector.tensor_tensor(slot(r, 2), heads(qk_rest, r), slot(r, 1), ALU.subtract).then_inc(lo_done, 1)

                def row_max(b, m, r, u):
                    dve.wait_ge(max_scores[u], m + 1)
                    out = neg_max[:, r, UH * u:UH * u + UH].rearrange("p (g j) -> p j g", j=2)
                    nc.vector.tensor_reduce(out, ps_max[:, :, :, :], AX.X, ALU.max, negate=True).then_inc(max_done[u], 1)

                part = lambda r, c: neg_parts[:, r, :, c, :]
                twice = lambda a: a.unsqueeze(1).broadcast_to([128, 2, HEADS])

                def max_hi(b, m, r):
                    dve.wait_ge(max_done[0], m + 1)
                    dve.wait_ge(max_done[1], m + 1)
                    nc.vector.tensor_copy(part(r, 0), twice(neg_max[:, r, :])).then_inc(n0_done, 1)

                def max_rest(b, m, r):
                    dve.wait_ge(n0_done, m + 1)
                    nc.vector.tensor_tensor(neg_rest[:, r, :], neg_max[:, r, :], neg_parts[:, r, 0, 0, :],
                                            ALU.subtract).then_inc(n0_rest, 1)

                def max_mid(b, m, r):
                    dve.wait_ge(n0_rest, m + 1)
                    nc.vector.tensor_copy(part(r, 1), twice(neg_rest[:, r, :])).then_inc(n1_done, 1)

                def max_lo(b, m, r):
                    dve.wait_ge(n1_done, m + 1)
                    nc.vector.tensor_tensor(part(r, 2), twice(neg_rest[:, r, :]), part(r, 1), ALU.subtract).then_inc(neg_done, 1)

                def add_mask(b, m, r, u):
                    dve.wait_ge(exp_scores[u], m + 1)
                    for j in range(2):
                        last = nc.vector.tensor_tensor(masked[:, u, j, :, :], ps_exp[:, j, :, :],
                                                       maskT[:, :].unsqueeze(1).broadcast_to([128, UH // 2, 128]), ALU.add)
                    last.then_inc(masked_done[u], 1)

                o_heads = ps_out[:, :].rearrange("p (h c) -> p h c", h=HEADS)

                def invert_sums(b, m, r):
                    dve.wait_ge(o_turned, m + 1)
                    nc.vector.reciprocal(o_rden[:, :], o_heads[:, :, HD]).then_inc(rden_done, 1)

                def divide(b, m, r):
                    dve.wait_ge(rden_done, m + 1)
                    nc.vector.tensor_tensor(o_norm[:, :].rearrange("p (h d) -> p h d", h=HEADS), o_heads[:, :, 0:HD],
                                            o_rden[:, :].unsqueeze(2).broadcast_to([128, HEADS, HD]),
                                            ALU.mult).then_inc(norm_done, 1)

                def add_attention(b, m, r):
                    dve.wait_ge(attn_made, m + 1)
                    if layer == 0:
                        dve.wait_ge(bias_added, m + 1)
                    nc.vector.tensor_tensor(x_all[:, b, :], ps_out[:, 128:256], x_all[:, b, :], ALU.add).then_inc(attn_done, 1)

                def attention_added(b, m, r):
                    dve.wait_ge(attn_done, m + 1)

                def statistics2(b, m, r):
                    nc.vector.bn_stats(stats2[:, r, :], x_all[:, b, :]).then_inc(stats2_done, 1)

                def statistics2_ready(b, m, r):
                    dve.wait_ge(stats2_done, m + 1)

                def mean_and_variance2(b, m, r):
                    nc.vector.bn_aggr(mean_var2[:, r, :], stats2[:, r, :]).then_inc(aggr2_done, 1)

                def normalise2(b, m, r):
                    dve.wait_ge(rstd2_done, m + 1)
                    nc.vector.tensor_scalar(xn2[:, r, :], x_all[:, b, :], mean_var2[:, r, 0:1], rstd2[:, r, :],
                                            ALU.subtract, ALU.mult).then_inc(xn2_done, 1)

                def top_of_x(b, m, r):
                    dve.wait_ge(xn2_done, m + 1)
                    nc.vector.tensor_reduce(top_x[:, r, :], xn2[:, r, :], AX.X, ALU.max, apply_absolute_value=True).then_inc(top_x_done, 1)

                def clip_x_top(b, m, r):
                    dve.wait_ge(top_x_done, b + 1)
                    nc.vector.tensor_scalar(clip_x[:, r, :], top_x[:, r, :], 1e-5, None, ALU.max).then_inc(clip_x_done, 1)

                def invert_x_top(b, m, r):
                    dve.wait_ge(clip_x_done, b + 1)
                    nc.vector.reciprocal(scale_x[:, r, :], clip_x[:, r, :]).then_inc(recip_x_done, 1)

                def x_scale(b, m, r):
                    dve.wait_ge(recip_x_done, b + 1)
                    nc.vector.tensor_scalar(scale_x[:, r, :], scale_x[:, r, :], 127.0, None, ALU.mult).then_inc(scale_x_done, 1)

                def clip_x_quantised(b, m, r):
                    dve.wait_ge(x_rounded, b + 1)
                    nc.vector.tensor_scalar(xq[:, r, :], x_round[:, :], MAGIC, 127.0, ALU.subtract, ALU.min).then_inc(xq_done, 1)

                def times_gate(b, m, r):
                    dve.wait_ge(gate_done, b + 1)
                    nc.vector.scalar_tensor_tensor(gated[:, :], gate[:, r, :], 1.0, ps_gate[:, :], ALU.add, ALU.mult).then_inc(gated_done, 1)

                def times_up(b, m, r):
                    dve.wait_ge(back_gu_done, b + 1)
                    dve.wait_ge(gated_done, b + 1)
                    nc.vector.scalar_tensor_tensor(h[:, r, :], ps_up[:, :], back_gu[:, r, :], gated[:, :],
                                                   ALU.mult, ALU.mult).then_inc(h_done, 1)

                def top_of_h(b, m, r):
                    dve.wait_ge(h_done, b + 1)
                    nc.vector.tensor_reduce(top_h[:, r, :], h[:, r, :], AX.X, ALU.max, apply_absolute_value=True).then_inc(top_h_done, 1)

                def clip_h_top(b, m, r):
                    dve.wait_ge(top_h_done, b + 1)
                    nc.vector.tensor_scalar(clip_h[:, r, :], top_h[:, r, :], 1e-5, None, ALU.max).then_inc(clip_h_done, 1)

                def invert_h_top(b, m, r):
                    dve.wait_ge(clip_h_done, b + 1)
                    nc.vector.reciprocal(scale_h[:, r, :], clip_h[:, r, :]).then_inc(recip_h_done, 1)

                def h_scale(b, m, r):
                    dve.wait_ge(recip_h_done, b + 1)
                    nc.vector.tensor_scalar(scale_h[:, r, :], scale_h[:, r, :], 127.0, None, ALU.mult).then_inc(scale_h_done, 1)

                def clip_h_quantised(b, m, r):
                    dve.wait_ge(h_rounded, b + 1)
                    nc.vector.tensor_scalar(hq[:, :], h_round[:, :], MAGIC, 127.0, ALU.subtract, ALU.min).then_inc(hq_done, 1)

                def add_feed_forward(b, m, r):
                    dve.wait_ge(down_made, b + 1)
                    dve.wait_ge(back_h_done, b + 1)
                    nc.vector.scalar_tensor_tensor(x_all[:, b, :], ps_in[:, 0:128], back_h[:, r, :], x_all[:, b, :],
                                                   ALU.mult, ALU.add).then_inc(ffn_done, 1)

                def first_layer(i, live, at):
                    if live(0):
                        statistics(*at(0))
                    if live(0):
                        statistics_ready(*at(0))
                    if live(1):
                        split_rest(*at(1))
                    if live(0):
                        mean_and_variance(*at(0))
                    if live(1):
                        split_mid(*at(1))
                    if live(5):
                        normalise2(*at(5))
                    if live(1):
                        split_lo(*at(1))
                    if live(2):
                        row_max(*at(2), 0)
                    if live(0):
                        normalise(*at(0))
                    if live(4):
                        invert_sums(*at(4))
                        divide(*at(4))
                    if live(2):
                        row_max(*at(2), 1)
                        max_hi(*at(2))
                    if live(4):
                        add_attention(*at(4))
                    if live(4):
                        attention_added(*at(4))
                    if live(2):
                        max_rest(*at(2))
                    if live(4):
                        statistics2(*at(4))
                    if live(0):
                        keep_qk(*at(0))
                    if live(2):
                        max_mid(*at(2))
                    if live(0):
                        split_hi(*at(0))
                    if live(4):
                        statistics2_ready(*at(4))
                    if live(2):
                        max_lo(*at(2))
                    if live(4):
                        mean_and_variance2(*at(4))

                def second_layer(i, live, at):
                    if live(0):
                        statistics(*at(0))
                    if live(5):
                        clip_x_top(*at(5))
                    if live(0):
                        statistics_ready(*at(0))
                    if live(3):
                        max_rest(*at(3))
                    if live(0):
                        mean_and_variance(*at(0))
                    if live(5):
                        invert_x_top(*at(5))
                    if live(3):
                        max_mid(*at(3))
                    if live(5):
                        x_scale(*at(5))
                    if live(3):
                        max_lo(*at(3))
                    if live(1):
                        split_rest(*at(1))
                    if live(6):
                        top_of_h(*at(6))
                    if live(4):
                        invert_sums(*at(4))
                    if live(6):
                        clip_h_top(*at(6))
                    if live(5):
                        clip_x_quantised(*at(5))
                    if live(6):
                        invert_h_top(*at(6))
                    if live(4):
                        divide(*at(4))
                    if live(6):
                        h_scale(*at(6))
                    if live(2):
                        row_max(*at(2), 0)
                    if live(3):
                        add_mask(*at(3), 0)
                    if live(4):
                        add_attention(*at(4))
                    if live(4):
                        attention_added(*at(4))
                    if live(1):
                        split_lo(*at(1))
                    if live(4):
                        statistics2(*at(4))
                    if live(4):
                        statistics2_ready(*at(4))
                    if live(6):
                        clip_h_quantised(*at(6))
                    if live(4):
                        mean_and_variance2(*at(4))
                    if live(5):
                        times_gate(*at(5))
                    if live(3):
                        add_mask(*at(3), 1)
                    if live(5):
                        times_up(*at(5))
                    if live(2):
                        row_max(*at(2), 1)
                    if live(4):
                        top_of_x(*at(4))
                    if live(2):
                        max_hi(*at(2))
                    if live(6):
                        add_feed_forward(*at(6))
                pipeline(dve, layer, DEPTHS[layer], second_layer if layer else first_layer,
                         after_step if layer == 0 else None)

            def route(part, lo, hi, done):
                size = hi - lo
                pairs = [128, size, EXPERTS, EXPERTS]
                sc, ch, w = scores[:, lo:hi, :], chosen[:, lo:hi, :], weight[:, lo:hi, :]
                gr, al = greater[:, lo:hi, :, :], at_least[:, lo:hi, :, :]
                other, this = sc.unsqueeze(2).broadcast_to(pairs), sc.unsqueeze(3).broadcast_to(pairs)
                lower = before[:, :, :].unsqueeze(1).broadcast_to(pairs)
                mid = midway[:, lo:hi].unsqueeze(2).broadcast_to([128, size, EXPERTS])
                if part == 0:
                    dve.wait_ge(ffn_loaded, FFN_CONSTS)
                    dve.wait_ge(score_done, hi)
                    nc.vector.tensor_tensor(gr, other, this, ALU.is_gt).then_inc(route_dve, 1)
                    nc.vector.tensor_tensor(al, other, this, ALU.is_ge).then_inc(route_dve, 1)
                if part == 1:
                    dve.wait_ge(route_dve, done + 2)
                    nc.vector.tensor_tensor(al, al, gr, ALU.subtract).then_inc(route_dve, 1)
                if part == 2:
                    dve.wait_ge(route_dve, done + 3)
                    nc.vector.tensor_tensor(al, al, lower, ALU.mult).then_inc(route_dve, 1)
                if part == 3:
                    dve.wait_ge(route_dve, done + 4)
                    nc.vector.tensor_tensor(gr, al, gr, ALU.add).then_inc(route_dve, 1)
                if part == 4:
                    dve.wait_ge(route_dve, done + 5)
                    nc.vector.tensor_reduce(rank[:, lo:hi, :], gr, AX.X, ALU.add).then_inc(route_dve, 1)
                if part == 5:
                    dve.wait_ge(route_dve, done + 6)
                    nc.vector.tensor_scalar(ch, rank[:, lo:hi, :], 2.0, None, ALU.is_lt).then_inc(route_dve, 1)
                    dve.wait_ge(route_dve, done + 7)
                    nc.vector.tensor_tensor(w, ch, sc, ALU.mult).then_inc(route_dve, 1)
                    dve.wait_ge(route_dve, done + 8)
                    nc.vector.tensor_reduce(midway[:, lo:hi], w, AX.X, ALU.add).then_inc(route_dve, 1)
                    dve.wait_ge(route_dve, done + 9)
                    nc.vector.scalar_tensor_tensor(w, mid, -0.5, sc, ALU.mult, ALU.add).then_inc(route_dve, 1)
                    nc.vector.tensor_scalar(ch, ch, half_gain[:, :], None, ALU.mult).then_inc(gains_done, 1)
                if part == 6:
                    dve.wait_ge(route_tanh_done, 1 if lo == 0 else 2)
                    dve.wait_ge(gains_done, 1 if lo == 0 else 2)
                    nc.vector.scalar_tensor_tensor(w, w, 1.0, ch, ALU.add, ALU.mult).then_inc(route_dve, 1)

            def add_expert(g, e):
                dve.wait_ge(expert_made, EXPERTS * g + e + 1)
                need(dve, expert_added, EXPERTS * g + e)
                for b in range(GROUP):
                    nc_b = GROUP * g + b
                    last = nc.vector.scalar_tensor_tensor(x_all[:, nc_b, :], ps_expert[e % 2][:, 128 * b:128 * (b + 1)],
                                                          weight[:, nc_b, e:e + 1], x_all[:, nc_b, :],
                                                          ALU.mult, ALU.add)
                last.then_inc(expert_added, 1)

            def experts():
                def group(g, first):
                    for e in range(EXPERTS):
                        if first and e < ROUTE_PARTS:
                            route(e, GROUP, BATCHES, ROUTE_STEPS)
                        for k in range(H_TILES):
                            m = (EXPERTS * g + e) * H_TILES + k
                            u = k % 2
                            dve.wait_ge(silu_done, m + 1)
                            dve.wait_ge(h2_made, m + 1)
                            nc.vector.tensor_tensor(hidden[:, e % 2, k, :], silu[:, u, :], ps_h2[u], ALU.mult).then_inc(hidden_done, 1)
                        if e:
                            add_expert(g, e - 1)
                        elif not first:
                            add_expert(g - 1, EXPERTS - 1)

                dve.wait_ge(route_dve, ROUTE_STEPS)
                group(0, True)
                dve.wait_ge(route_dve, 2 * ROUTE_STEPS)
                with dve.Fori(1, GROUPS, 1) as g:
                    group(g, False)
                add_expert(GROUPS - 1, EXPERTS - 1)
                dve.wait_ge(expert_added, EXPERTS * GROUPS)

            def add_expert(g, e):
                dve.wait_ge(expert_made, EXPERTS * g + e + 1)
                need(dve, expert_added, EXPERTS * g + e)
                for b in range(GROUP):
                    nc_b = GROUP * g + b
                    last = nc.vector.scalar_tensor_tensor(x_all[:, nc_b, :], ps_expert[e % 2][:, 128 * b:128 * (b + 1)],
                                                          weight[:, nc_b, e:e + 1], x_all[:, nc_b, :],
                                                          ALU.mult, ALU.add)
                last.then_inc(expert_added, 1)

            def second_layer_weights():
                nc.vector.tensor_copy(mask_parts[:, 0, :], mask[:, :]).then_inc(layer1_ready, 1)
                dve.wait_ge(layer1_ready, 1)
                nc.vector.tensor_tensor(mask_rest[:, :], mask[:, :], mask_parts[:, 0, :], ALU.subtract).then_inc(layer1_ready, 1)
                dve.wait_ge(layer1_ready, 2)
                nc.vector.tensor_copy(mask_parts[:, 1, :], mask_rest[:, :]).then_inc(layer1_ready, 1)
                dve.wait_ge(layer1_ready, 3)
                nc.vector.tensor_tensor(mask_parts[:, 2, :], mask_rest[:, :], mask_parts[:, 1, :],
                                        ALU.subtract).then_inc(layer1_ready, 1)
                nc.vector.tensor_scalar(wq[1][:, :], wq[1][:, :], scale, None, ALU.mult).then_inc(layer1_ready, 1)
                nc.vector.tensor_scalar(wo[1][:, :], wo[1][:, :], tanh_g[:, 1:2], None, ALU.mult).then_inc(layer1_ready, 1)

            def expert(g, e, first):
                for k in range(H_TILES):
                    m = (EXPERTS * g + e) * H_TILES + k
                    u = k % 2
                    dve.wait_ge(silu_done, m + 1)
                    dve.wait_ge(h2_made, m + 1)
                    nc.vector.tensor_tensor(hidden[:, e % 2, k, :], silu[:, u, :], ps_h2[u], ALU.mult).then_inc(hidden_done, 1)
                if e:
                    add_expert(g, e - 1)
                elif not first:
                    add_expert(g - 1, EXPERTS - 1)

            def after_step(i):
                if i == HEAD_START - 2:
                    for part in range(0, 3):
                        route(part, 0, GROUP, 0)
                if i == HEAD_START - 1:
                    for part in range(3, 6):
                        route(part, 0, GROUP, 0)
                if i == HEAD_START:
                    route(6, 0, GROUP, 0)
                    expert(0, 0, True)
                if i == HEAD_START + 1:
                    dve.wait_ge(route_dve, ROUTE_STEPS)
                    expert(0, 1, True)

            def experts():
                for e in range(2, EXPERTS):
                    for part in range(ROUTE_PARTS):
                        if e == max(2, part + 1):
                            route(part, GROUP, BATCHES, ROUTE_STEPS)
                    if e == EXPERTS - 2:
                        weight_scales()
                    if e == EXPERTS - 1:
                        second_layer_weights()
                    expert(0, e, True)
                dve.wait_ge(route_dve, 2 * ROUTE_STEPS)
                with dve.Fori(1, GROUPS, 1) as g:
                    for e in range(EXPERTS):
                        expert(g, e, False)
                add_expert(GROUPS - 1, EXPERTS - 1)

            def weight_scales():
                nc.vector.memset(w_factor[:, 0:1], 0.5)
                nc.vector.memset(w_factor[:, 1:2], 1.0)
                nc.vector.tensor_copy(w_factor[:, 2:3], tanh_g[:, 3:4])
                dve.wait_ge(w_totalled, 1)
                nc.vector.tensor_scalar(w_mean[:, :], ps_in[:, 0:3], 1.0 / (INNER * D), 1e-5, ALU.mult, ALU.max).then_inc(w_scaled, 1)
                dve.wait_ge(w_scaled, 1)
                nc.vector.reciprocal(w_scale[:, :], w_mean[:, :]).then_inc(w_scaled, 1)
                dve.wait_ge(w_scaled, 2)
                nc.vector.reciprocal(w_inv[:, :], w_scale[:, :]).then_inc(w_scaled, 1)
                dve.wait_ge(w_scaled, 3)
                nc.vector.tensor_tensor(w_back[:, :], w_inv[:, :], w_factor[:, :], ALU.mult).then_inc(w_scaled, 1)
                dve.wait_ge(w_scaled, 4)
                nc.vector.tensor_scalar(w_back[:, :], w_back[:, :], 1.0 / 127.0, None, ALU.mult).then_inc(w_scaled, 1)

            layer_steps(0)
            experts()
            dve.wait_ge(expert_added, EXPERTS * GROUPS)
            layer_steps(1)

        @block.scalar
        def _(act):
            for dst, src in const_loads:
                act.dma_start(dst, src).then_inc(consts_loaded, 16)
            act.wait_ge(consts_loaded, CONSTS)
            nc.scalar.activation(tanh_g[:, :], gains[:, :], ACT.Tanh).then_inc(act_setup, 1)
            act.wait_ge(dve_setup, 4)
            nc.scalar.activation(sel[:, :, :], sel_ind[:, :].unsqueeze(2).broadcast_to([128, HEADS, 128]), ACT.Copy).then_inc(act_setup, 1)
            act.wait_ge(pool_setup, POOL_SETUP)

            def layer_steps(layer):
                def normalise(b, m, r):
                    act.wait_ge(shift_done, 2 * b + 2)
                    nc.scalar.activation(xn[:, r, :], x_all[:, b, :], ACT.Identity, bias=shift[:, r, :],
                                         scale=rstd[:, r, :]).then_inc(xn_done, 1)

                def normalise2(b, m, r):
                    act.wait_ge(shift2_done, 2 * b + 2)
                    nc.scalar.activation(xn2[:, r, :], x_all[:, b, :], ACT.Identity, bias=shift2[:, r, :],
                                         scale=rstd2[:, r, :]).then_inc(xn2_done, 1)

                def keep_inputs(b, m, r):
                    act.wait_ge(xc_turned, m + 1)
                    nc.scalar.activation(xcT[:, r, :], ps_in[:, 0:256], ACT.Copy).then_inc(xcT_done, 1)

                def keep_qk(b, m, r):
                    act.wait_ge(qk_made, m + 1)
                    nc.scalar.activation(qk[:, r, :], ps_in[:, 0:256], ACT.Copy).then_inc(qk_done, 1)

                heads = lambda a, r: a[:, r, :].rearrange("p (w h d) -> p w h d", w=2, h=HEADS)
                slot = lambda r, c: stack[:, r, :, :, c * HD:(c + 1) * HD]

                def split_hi(b, m, r):
                    act.wait_ge(qk_done, m + 1)
                    nc.scalar.activation(slot(r, 0), heads(qk, r), ACT.Copy).then_inc(hi_done, 1)

                def split_mid(b, m, r):
                    act.wait_ge(rest_done, m + 1)
                    nc.scalar.activation(slot(r, 1), heads(qk_rest, r), ACT.Copy).then_inc(mid_done, 1)

                def keep_k(b, m, r):
                    act.wait_ge(k_turned, m + 1)
                    nc.scalar.activation(kT[:, r, :, :], ps_k_b, ACT.Copy).then_inc(kT_done, 1)

                def keep_q(b, m, r):
                    act.wait_ge(q_turned, m + 1)
                    nc.scalar.activation(qT[:, r, :, :], ps_q_b, ACT.Copy).then_inc(qT_done, 1)

                def keep_v(b, m, r):
                    act.wait_ge(v_made, m + 1)
                    need(act, pv_made[1], m - 1)
                    nc.scalar.activation(v_one[:, r, :, 0:HD], ps_in[:, 256:384].rearrange("p (h d) -> p h d", h=HEADS),
                                         ACT.Copy).then_inc(v_done, 1)

                def keep_max(b, m, r):
                    act.wait_ge(m_turned, m + 1)
                    nc.scalar.activation(mT[:, r, :], ps_k_b[:, 0, :], ACT.Copy).then_inc(mT_done, 1)

                def exponentials(b, m, r, u):
                    act.wait_ge(masked_done[u] if layer else exp_scores[u], (b if layer else m) + 1)
                    scored = masked[:, u, :, :, :] if layer else ps_exp[:, :, :, :]
                    nc.scalar.activation(probs[:, u, :, :, :], scored, ACT.Exp).then_inc(exp_done[u], 1)

                def keep_o(b, m, r):
                    act.wait_ge(pv_made[0], m + 1)
                    act.wait_ge(pv_made[1], m + 1)
                    nc.scalar.activation(o_raw[:, :], ps_out[:, :], ACT.Copy).then_inc(o_done, 1)

                def keep_normed(b, m, r):
                    act.wait_ge(norm_turned, m + 1)
                    nc.scalar.activation(o_normT[:, :], ps_out[:, 0:128], ACT.Copy).then_inc(normT_done, 1)

                def keep_xn(b, m, r):
                    act.wait_ge(xn_turned, b + 1)
                    nc.scalar.activation(xnT_ring[:, r, :], ps_in[:, 0:128], ACT.Copy).then_inc(ring_done, 1)

                def keep_scores(b, m, r):
                    act.wait_ge(gate_made, b + 1)
                    nc.scalar.activation(scores[:, b, :], ps_in[:, 0:EXPERTS], ACT.Copy).then_inc(score_done, 1)

                def keep_x_quantised(b, m, r):
                    act.wait_ge(xq_turned, b + 1)
                    nc.scalar.activation(xqT[:, r, :], ps_in_b[:, 0, :], ACT.Copy).then_inc(xqT_done, 1)

                def gate_tanh(b, m, r):
                    act.wait_ge(back_x_done, b + 1)
                    act.wait_ge(gu_made, b + 1)
                    nc.scalar.activation(gate[:, r, :], ps_gate[:, :], ACT.Tanh, scale=back_x[:, r, 0:1]).then_inc(gate_done, 1)

                def keep_h(b, m, r):
                    act.wait_ge(hq_turned, b + 1)
                    nc.scalar.activation(hqT[:, :, :], ps_in_b[:, 0:I_TILES, :], ACT.Copy).then_inc(hqT_done, 1)

                def first_layer(i, live, at):
                    if live(5):
                        keep_xn(*at(5))
                    if live(3):
                        exponentials(*at(3), 0)
                    if live(0):
                        keep_inputs(*at(0))
                    if live(4):
                        keep_normed(*at(4))
                    if live(3):
                        exponentials(*at(3), 1)
                    if live(1):
                        keep_k(*at(1))
                        keep_q(*at(1))
                    if live(2):
                        keep_max(*at(2))
                    if live(1):
                        keep_v(*at(1))
                    if live(3):
                        keep_o(*at(3))
                    if live(5):
                        keep_scores(*at(5))

                def second_layer(i, live, at):
                    if live(4):
                        keep_o(*at(4))
                    if live(2):
                        keep_k(*at(2))
                        keep_v(*at(2))
                    if live(3):
                        keep_max(*at(3))
                    if live(0):
                        normalise(*at(0))
                    if live(5):
                        keep_x_quantised(*at(5))
                    if live(1):
                        split_mid(*at(1))
                    if live(4):
                        keep_normed(*at(4))
                    if live(0):
                        keep_inputs(*at(0))
                    if live(5):
                        gate_tanh(*at(5))
                    if live(3):
                        exponentials(*at(3), 0)
                    if live(0):
                        keep_qk(*at(0))
                        split_hi(*at(0))
                    if live(6):
                        keep_h(*at(6))
                    if live(3):
                        exponentials(*at(3), 1)
                    if live(4):
                        normalise2(*at(4))
                    if live(1):
                        keep_q(*at(1))
                pipeline(act, layer, DEPTHS[layer], second_layer if layer else first_layer,
                         after_step if layer == 0 else None)

            def weight_sums():
                act.wait_ge(ffn_loaded, FFN_CONSTS)
                nc.scalar.activation(w_abs[:, 0:INNER], w_gu[:, 0, :], ACT.Abs, accum_out=w_sums[:, 0:1]).then_inc(w_summed, 1)
                nc.scalar.activation(w_abs[:, INNER:2 * INNER], w_gu[:, 1, :], ACT.Abs, accum_out=w_sums[:, 1:2]).then_inc(w_summed, 1)
                act.wait_ge(w_summed, 2)
                nc.scalar.activation(w_abs[:, 0:INNER].rearrange("p (k d) -> p k d", k=I_TILES), w_dn[:, :, :], ACT.Abs,
                                     accum_out=w_sums[:, 2:3]).then_inc(w_summed, 1)

            def route_tanh(lo, hi, done):
                act.wait_ge(route_dve, done)
                nc.scalar.activation(weight[:, lo:hi, :], weight[:, lo:hi, :], ACT.Tanh).then_inc(route_tanh_done, 1)

            def expert(g, e):
                for k in range(H_TILES):
                    m = (EXPERTS * g + e) * H_TILES + k
                    act.wait_ge(h1_made, m + 1)
                    need(act, hidden_done, m - 1)
                    nc.scalar.activation(silu[:, k % 2, :], ps_h1[k % 2], ACT.Silu).then_inc(silu_done, 1)

            def after_step(i):
                if i == HEAD_START - 1:
                    route_tanh(0, GROUP, ROUTE_STEPS - 1)
                if HEAD_START <= i < HEAD_START + 2:
                    expert(0, i - HEAD_START)

            def experts():
                for e in range(2, EXPERTS):
                    if e == EXPERTS - 1:
                        route_tanh(GROUP, BATCHES, 2 * ROUTE_STEPS - 1)
                    if e == 3:
                        weight_sums()
                    expert(0, e)
                with act.Fori(1, GROUPS, 1) as g:
                    for e in range(EXPERTS):
                        expert(g, e)

            layer_steps(0)
            experts()
            act.wait_ge(expert_added, EXPERTS * GROUPS)
            layer_steps(1)

        @block.tensor
        def _(pe):
            pe.wait_ge(dve_setup, 5)
            nc.tensor.matmul(ps_in[:, 0:128], bv_rep[:, :], wo[0][:, :], start=True, stop=True).then_inc(pe_setup, 1)

            def layer_steps(layer):
                four = lambda a: a.unsqueeze(1).broadcast_to([128, UH // 2, 128])

                def turn_inputs(b, m, r):
                    pe.wait_ge(ctx_loaded[r], 8 * (m - r) + 16)
                    nc.tensor.transpose(ps_in[:, 128:256], ctx_in[:, r, :], eye[:, :])
                    pe.wait_ge(xn_done, m + 1)
                    nc.tensor.transpose(ps_in[:, 0:128], xn[:, r, :], eye[:, :]).then_inc(xc_turned, 1)

                def project_qk(b, m, r):
                    pe.wait_ge(xcT_done, m + 1)
                    nc.tensor.matmul(ps_in[:, 0:128], xcT[:, r, 0:128], wq[layer][:, :], start=True, stop=True)
                    nc.tensor.matmul(ps_in[:, 128:256], xcT[:, r, 128:256], wkv[layer][:, 0:128],
                                     start=True, stop=True).then_inc(qk_made, 1)

                def project_v(b, m, r):
                    pe.wait_ge(xcT_done, m + 1)
                    nc.tensor.matmul(ps_in[:, 256:384], xcT[:, r, 128:256], wkv[layer][:, 128:256],
                                     start=True, stop=True).then_inc(v_made, 1)

                def turn_k(b, m, r):
                    pe.wait_ge(stack_done, 4 * (m + 1))
                    for p in range(HEADS // 2):
                        last = nc.tensor.transpose(ps_k_b[:, p, :], stack[:, r, 1, 2 * p:2 * p + 2, :], eye_b[:, :])
                    last.then_inc(k_turned, 1)

                def turn_q(b, m, r):
                    pe.wait_ge(stack_done, 4 * (m + 1))
                    for p in range(HEADS // 2):
                        last = nc.tensor.transpose(ps_q_b[:, p, :], stack[:, r, 0, 2 * p:2 * p + 2, :], eye_b[:, :])
                    last.then_inc(q_turned, 1)

                def mask_scores(b, m, r, u):
                    for j in range(2):
                        for c in range(3):
                            nc.tensor.matmul(ps_max[:, j, :, :], eye_b[:, :], four(mask_parts[:, c, :]),
                                             start=(c == 0), stop=False, skip_group_check=True)

                def scores_for_max(b, m, r, u):
                    pe.wait_ge(kT_done, m + 1)
                    pe.wait_ge(qT_done, m + 1)
                    for g in range(UH // 2):
                        for j in range(2):
                            rows = slice(SLOT_ROWS * j, SLOT_ROWS * (j + 1))
                            p = UH // 2 * u + g
                            last = nc.tensor.matmul(ps_max[:, j, g, :], qT[rows, r, p, :], kT[rows, r, p, :],
                                                    start=(layer == 0), stop=True, skip_group_check=True)
                    last.then_inc(max_scores[u], 1)

                def turn_max(b, m, r):
                    pe.wait_ge(neg_done, m + 1)
                    nc.tensor.transpose(ps_k_b[:, 0, :], neg_parts[:, r, :, :, :], eye_b[:, :]).then_inc(m_turned, 1)

                def scores_for_exp(b, m, r, u):
                    pe.wait_ge(mT_done, m + 1)
                    for g in range(UH // 2):
                        for j in range(2):
                            rows = slice(SLOT_ROWS * j, SLOT_ROWS * (j + 1))
                            p = UH // 2 * u + g
                            nc.tensor.matmul(ps_exp[:, j, g, :], kT[rows, r, p, :], qT[rows, r, p, :],
                                             start=True, stop=False, skip_group_check=True)
                            last = nc.tensor.matmul(ps_exp[:, j, g, :], sel[rows, 2 * p + j, :], mT[rows, r, :],
                                                    start=False, stop=True, skip_group_check=True)
                    last.then_inc(exp_scores[u], 1)

                def probs_times_v(b, m, r, u):
                    pe.wait_ge(exp_done[u], m + 1)
                    pe.wait_ge(v_done, m + 1)
                    if u == 0:
                        need(pe, attn_done, m)
                    for g in range(UH // 2):
                        for j in range(2):
                            h = UH * u + 2 * g + j
                            strip = V_COLS * (h % 4)
                            last = nc.tensor.matmul(ps_out[strip:strip + V_COLS, 128 * (h // 4):128 * (h // 4 + 1)],
                                                    v_one[:, r, h, :], probs[:, u, j, g, :], start=True, stop=True,
                                                    skip_group_check=True)
                    last.then_inc(pv_made[u], 1)

                def turn_o(b, m, r):
                    pe.wait_ge(o_done, m + 1)
                    for c in range(4):
                        last = nc.tensor.transpose(ps_out[:, 128 * c:128 * c + 128], o_raw[:, 128 * c:128 * c + 128],
                                                   eye[:, :])
                    last.then_inc(o_turned, 1)

                def turn_normed(b, m, r):
                    pe.wait_ge(norm_done, m + 1)
                    nc.tensor.transpose(ps_out[:, 0:128], o_norm[:, :], eye[:, :]).then_inc(norm_turned, 1)

                def project_out(b, m, r):
                    pe.wait_ge(normT_done, m + 1)
                    nc.tensor.matmul(ps_out[:, 128:256], o_normT[:, :], wo[layer][:, :],
                                     start=True, stop=True).then_inc(attn_made, 1)

                def turn_xn(b, m, r):
                    pe.wait_ge(xn2_done, m + 1)
                    nc.tensor.transpose(ps_in[:, 0:128], xn2[:, r, :], eye[:, :]).then_inc(xn_turned, 1)

                def gate_scores(b, m, r):
                    pe.wait_ge(ring_done, b + 1)
                    nc.tensor.matmul(ps_in[:, 0:EXPERTS], xnT_ring[:, r, :], gate_w[:, :],
                                     start=True, stop=True).then_inc(gate_made, 1)

                def turn_x_quantised(b, m, r):
                    pe.wait_ge(xq_done, b + 1)
                    nc.tensor.transpose(ps_in_b[:, 0, :], xq[:, r, :], eye_b[:, :]).then_inc(xq_turned, 1)

                def project_gate_up(b, m, r):
                    pe.wait_ge(xqT_done, b + 1)
                    nc.tensor.matmul(ps_gate[:, :], xqT[:, r, :], wq_gu[:, 0, :], start=True, stop=True)
                    nc.tensor.matmul(ps_up[:, :], xqT[:, r, :], wq_gu[:, 1, :], start=True, stop=True).then_inc(gu_made, 1)

                def turn_h(b, m, r):
                    pe.wait_ge(hq_done, b + 1)
                    for k in range(I_TILES):
                        last = nc.tensor.transpose(ps_in_b[:, k, :], hq[:, 128 * k:128 * k + 128], eye_b[:, :])
                    last.then_inc(hq_turned, 1)

                def project_down(b, m, r):
                    pe.wait_ge(hqT_done, b + 1)
                    for k in range(I_TILES):
                        last = nc.tensor.matmul(ps_in[:, 0:128], hqT[:, k, :], wq_dn[:, k, :],
                                                start=(k == 0), stop=(k == I_TILES - 1))
                    last.then_inc(down_made, 1)

                def first_layer(i, live, at):
                    if live(5):
                        latest(pe, (live(6), score_done, i - 5), (live(2), v_done, i - 1), (live(1), qk_done, i),
                               (live(1), xcT_done, i), (live(6), ring_done, i - 5))
                        turn_xn(*at(5))
                    if live(4):
                        turn_o(*at(4))
                    if live(2):
                        latest(pe, (live(2), max_done[0], i - 1), (live(3), max_done[1], i - 2))
                        scores_for_max(*at(2), 1)
                    if live(0):
                        latest(pe, (live(5), ring_done, i - 4), (live(6), score_done, i - 5),
                               (live(2), v_done, i - 1), (live(1), qk_done, i), (live(1), xcT_done, i))
                        turn_inputs(*at(0))
                    if live(4):
                        turn_normed(*at(4))
                    if live(3):
                        latest(pe, (live(3), exp_done[0], i - 2), (live(4), exp_done[1], i - 3))
                        scores_for_exp(*at(3), 1)
                    if live(4):
                        project_out(*at(4))
                    if live(1):
                        latest(pe, (live(3), mT_done, i - 2), (live(2), kT_done, i - 1))
                        turn_k(*at(1))
                    if live(0):
                        latest(pe, (live(0), xcT_done, i + 1), (live(5), ring_done, i - 4),
                               (live(6), score_done, i - 5), (live(2), v_done, i - 1), (live(1), qk_done, i))
                        project_qk(*at(0))
                    if live(1):
                        latest(pe, (live(2), qT_done, i - 1))
                        turn_q(*at(1))
                    if live(3):
                        probs_times_v(*at(3), 0)
                    if live(1):
                        latest(pe, (live(0), qk_done, i + 1), (live(0), xcT_done, i + 1), (live(5), ring_done, i - 4),
                               (live(6), score_done, i - 5), (live(2), v_done, i - 1))
                        project_v(*at(1))
                    if live(2):
                        latest(pe, (live(1), kT_done, i), (live(3), mT_done, i - 2))
                        turn_max(*at(2))
                    if live(3):
                        probs_times_v(*at(3), 1)
                    if live(1):
                        latest(pe, (live(2), max_done[1], i - 1), (live(2), max_done[0], i - 1))
                        scores_for_max(*at(1), 0)
                    if live(5):
                        latest(pe, (live(1), v_done, i), (live(0), qk_done, i + 1), (live(0), xcT_done, i + 1),
                               (live(5), ring_done, i - 4), (live(6), score_done, i - 5))
                        gate_scores(*at(5))
                    if live(2):
                        latest(pe, (live(3), exp_done[1], i - 2), (live(3), exp_done[0], i - 2))
                        scores_for_exp(*at(2), 0)

                def second_layer(i, live, at):
                    if live(4):
                        turn_o(*at(4))
                    if live(2):
                        latest(pe, (live(7), ffn_done, i - 6), (live(7), hqT_done, i - 6),
                               (live(1), qk_done, i + BATCHES), (live(1), xcT_done, i + BATCHES),
                               (live(6), xqT_done, i - 5), (live(3), v_done, i + BATCHES - 2))
                        project_v(*at(2))
                    if live(3):
                        latest(pe, (live(2), kT_done, i + BATCHES - 1), (live(6), h_done, i - 5),
                               (live(4), mT_done, i + BATCHES - 3))
                        turn_max(*at(3))
                    if live(2):
                        scores_for_max(*at(2), 0)
                    if live(5):
                        latest(pe, (live(2), v_done, i + BATCHES - 1), (live(7), ffn_done, i - 6),
                               (live(7), hqT_done, i - 6), (live(1), qk_done, i + BATCHES),
                               (live(1), xcT_done, i + BATCHES), (live(6), xqT_done, i - 5))
                        turn_x_quantised(*at(5))
                    if live(3):
                        latest(pe, (live(4), masked_done[1], i - 3), (live(4), masked_done[0], i - 3))
                        scores_for_exp(*at(3), 0)
                    if live(4):
                        turn_normed(*at(4))
                    if live(0):
                        latest(pe, (live(5), xqT_done, i - 4), (live(2), v_done, i + BATCHES - 1),
                               (live(7), ffn_done, i - 6), (live(7), hqT_done, i - 6),
                               (live(1), qk_done, i + BATCHES), (live(1), xcT_done, i + BATCHES))
                        turn_inputs(*at(0))
                    if live(5):
                        latest(pe, (live(2), qT_done, i + BATCHES - 1), (live(6), gated_done, i - 5))
                        latest(pe, (live(3), mT_done, i + BATCHES - 2), (live(2), kT_done, i + BATCHES - 1),
                               (live(6), h_done, i - 5))
                        project_gate_up(*at(5))
                    if live(4):
                        project_out(*at(4))
                    if live(0):
                        latest(pe, (live(0), xcT_done, i + BATCHES + 1), (live(5), xqT_done, i - 4),
                               (live(2), v_done, i + BATCHES - 1), (live(7), ffn_done, i - 6),
                               (live(7), hqT_done, i - 6), (live(1), qk_done, i + BATCHES))
                        project_qk(*at(0))
                    if live(3):
                        latest(pe, (live(3), masked_done[0], i - 2), (live(4), masked_done[1], i - 3))
                        scores_for_exp(*at(3), 1)
                    if live(2):
                        latest(pe, (live(2), max_done[0], i + BATCHES - 1), (live(3), max_done[1], i + BATCHES - 2))
                        mask_scores(*at(2), 1)
                    if live(6):
                        latest(pe, (live(0), qk_done, i + BATCHES + 1), (live(0), xcT_done, i + BATCHES + 1),
                               (live(5), xqT_done, i - 4), (live(2), v_done, i + BATCHES - 1),
                               (live(7), ffn_done, i - 6), (live(7), hqT_done, i - 6))
                        turn_h(*at(6))
                    if live(2):
                        scores_for_max(*at(2), 1)
                    if live(3):
                        probs_times_v(*at(3), 0)
                    if live(1):
                        latest(pe, (live(5), gated_done, i - 4), (live(2), qT_done, i + BATCHES - 1))
                        turn_q(*at(1))
                        latest(pe, (live(5), h_done, i - 4), (live(3), mT_done, i + BATCHES - 2),
                               (live(2), kT_done, i + BATCHES - 1))
                        turn_k(*at(1))
                    if live(6):
                        latest(pe, (live(6), hqT_done, i - 5), (live(0), qk_done, i + BATCHES + 1),
                               (live(0), xcT_done, i + BATCHES + 1), (live(5), xqT_done, i - 4),
                               (live(2), v_done, i + BATCHES - 1), (live(7), ffn_done, i - 6))
                        project_down(*at(6))
                    if live(3):
                        probs_times_v(*at(3), 1)
                    if live(1):
                        latest(pe, (live(2), max_done[1], i + BATCHES - 1), (live(2), max_done[0], i + BATCHES - 1))
                        mask_scores(*at(1), 0)
                pipeline(pe, layer, DEPTHS[layer], second_layer if layer else first_layer,
                         after_step if layer == 0 else None)

            def weight_totals():
                pe.wait_ge(w_summed, 3)
                pe.wait_ge(score_done, BATCHES)
                nc.tensor.matmul(ps_in[:, 0:3], ones[:, :], w_sums[:, :], start=True, stop=True).then_inc(w_totalled, 1)

            def up(g, e):
                if isinstance(g, int) and e == 0:
                    pe.wait_ge(all_done, GROUP)
                    pe.wait_ge(ffn_loaded, FFN_CONSTS)
                x_group = xnT_all[:, bass.ds(GROUP * g, GROUP), :]
                for k in range(H_TILES):
                    m = (EXPERTS * g + e) * H_TILES + k
                    need(pe, hidden_done, m - 1)
                    nc.tensor.matmul(ps_h1[k % 2], w12[:, e, 128 * k:128 * k + 128], x_group,
                                     start=True, stop=True).then_inc(h1_made, 1)
                    k2 = TWO_H // 2 + 128 * k
                    nc.tensor.matmul(ps_h2[k % 2], w12[:, e, k2:k2 + 128], x_group,
                                     start=True, stop=True).then_inc(h2_made, 1)

            def down(g, e):
                pe.wait_ge(hidden_done, (EXPERTS * g + e + 1) * H_TILES)
                need(pe, expert_added, EXPERTS * g + e - 1)
                for b in range(GROUP):
                    for k in range(H_TILES):
                        last = nc.tensor.matmul(ps_expert[e % 2][:, 128 * b:128 * b + 128],
                                                hidden[:, e % 2, k, 128 * b:128 * b + 128], w3[:, e, k, :],
                                                start=(k == 0), stop=(k == H_TILES - 1))
                last.then_inc(expert_made, 1)

            def expert(g, e, first):
                up(g, e)
                if e:
                    down(g, e - 1)
                elif not first:
                    down(g - 1, EXPERTS - 1)

            def after_step(i):
                if i == HEAD_START:
                    pe.wait_ge(exp_done[1], BATCHES)
                if HEAD_START <= i < HEAD_START + 2:
                    expert(0, i - HEAD_START, True)

            def experts():
                for e in range(2, EXPERTS):
                    expert(0, e, True)
                    if e == 4:
                        weight_totals()
                pe.wait_ge(all_done, BATCHES)
                with pe.Fori(1, GROUPS, 1) as g:
                    for e in range(EXPERTS):
                        expert(g, e, False)
                down(GROUPS - 1, EXPERTS - 1)

            pe.wait_ge(dve_setup, SETUP_ALL)
            pe.wait_ge(act_setup, 2)
            layer_steps(0)
            experts()
            pe.wait_ge(layer1_ready, LAYER1_STEPS)
            pe.wait_ge(w_quantised, 9)
            pe.wait_ge(expert_added, EXPERTS * GROUPS)
            layer_steps(1)


def layouts(inputs):
    import numpy as np

    a = {k: np.asarray(v) for k, v in inputs.items()}
    turn = lambda w, *axes: np.ascontiguousarray(np.transpose(w, axes))
    d = a["x"].shape[-1]
    side = lambda *parts: np.concatenate(parts, axis=1)
    heads = lambda w: turn(w, 1, 0, 2).reshape(d, d)
    out = {
        "x": a["x"], "ctx": a["ctx_1024"],
        "early": side(np.eye(128, dtype=np.float32), a["L0_xattn_Wo"], a["L0_xattn_Wq"], a["L0_xattn_Wk"],
                      a["L0_xattn_Wv"], turn(a["L0_ffn_gate_w"], 1, 0), a["L0_xattn_bv"].reshape(d, 1)),
        "rows": np.concatenate([a["L0_xattn_bq"], a["L0_xattn_bk"], a["L0_xattn_bo"], a["g_xattn"], a["g_ffn"]]),
        "late": side(a["L1_xattn_WO"], heads(a["L1_xattn_WQ"]), heads(a["L1_xattn_WK"]), heads(a["L1_xattn_WV"]),
                     a["fside_SxS2_0"], turn(a["fside_SxS2_0"], 1, 0)),
        "w12T": turn(a["L0_ffn_w12"], 2, 0, 1), "w3T": turn(a["L0_ffn_w3"], 2, 0, 1),
        "gate_upT": side(turn(a["L1_ffn_w_gate"], 1, 0), turn(a["L1_ffn_w_up"], 1, 0)),
        "w_downT": turn(a["L1_ffn_w_down"], 1, 0),
        "before": np.tril(np.ones((8, 8), np.float32), -1),
    }
    return {k: np.ascontiguousarray(v) for k, v in out.items()}


def kernel(**inputs):
    import concourse.bacc as bacc
    from concourse.bass_utils import run_bass_kernel_spmd

    arrays = layouts(inputs)
    nc = bacc.Bacc("TRN2", target_bir_lowering=False, num_devices=1)
    t = {k: nc.dram_tensor(f"in_{k}", a.shape, mybir.dt.from_np(a.dtype), kind="ExternalInput").ap()
         for k, a in arrays.items()}
    t["out"] = nc.dram_tensor("out_x", arrays["x"].shape, mybir.dt.float32, kind="ExternalOutput").ap()
    gated_cross_attention_stack(nc, t)
    r = run_bass_kernel_spmd(nc, [{f"in_{k}": a for k, a in arrays.items()}], core_ids=[0])
    return r.results[0]["out_x"]
```
